# Optimizing a Trainium2 kernel written in Bass

```python
import numpy as np
import jax
import jax.numpy as jnp

def _softmax(x, axis=-1):
    return jax.nn.softmax(x, axis=axis)

def _gelu(x):
    return jax.nn.gelu(x, approximate=True)

def _silu(x):
    return jax.nn.silu(x)

def _sigmoid(x):
    return jax.nn.sigmoid(x)

def _layernorm(x, axis=-1, eps=1e-05):
    m = jnp.mean(x, axis=axis, keepdims=True)
    v = jnp.var(x, axis=axis, keepdims=True)
    return (x - m) / jnp.sqrt(v + eps)

def _scatter_add(tgt, idx, src, axis=0):
    return tgt.at[idx].add(src)

def _segment_sum(src, seg, n):
    return jax.ops.segment_sum(src, seg, n)
kernel_name = 'mk_seq_postln_d2_jaxref_r8_95e276'

def setup_inputs(seed: int=0):
    np.random.seed(seed)
    _w = jnp.asarray

    def _L0_attn_setup():
        import math
        import jax, jax.numpy as jnp
        import numpy as np
        DIM = 128
        HID = 256
        QK = 128
        G = 32
        B, N = (4, 512)
        NUM_BUCKETS = 32
        MAX_DIST = 128

        def _rel_pos_bias(rel_emb, g, scale):
            pos = jnp.arange(g)
            rel = pos[None, :] - pos[:, None]
            n = -rel
            nb = NUM_BUCKETS // 2
            ret = (n < 0).astype(jnp.int32) * nb
            n = jnp.abs(n)
            max_exact = nb // 2
            is_small = n < max_exact
            val_large = max_exact + (jnp.log(jnp.maximum(n, 1).astype(jnp.float32) / max_exact) / math.log(MAX_DIST / max_exact) * (nb - max_exact)).astype(jnp.int32)
            val_large = jnp.minimum(val_large, nb - 1)
            bucket = ret + jnp.where(is_small, n, val_large)
            return rel_emb[bucket, 0] * scale

        def _layernorm(x, g, b, eps=1e-05):
            mu = jnp.mean(x, axis=-1, keepdims=True)
            var = jnp.mean((x - mu) ** 2, axis=-1, keepdims=True)
            return (x - mu) * jax.lax.rsqrt(var + eps) * g + b
        key = jax.random.key(seed)
        ks = jax.random.split(key, 8)
        return {'x': jax.random.normal(ks[0], (B, N, DIM), dtype=jnp.float32), 'ln_g': jnp.ones((DIM,), jnp.float32), 'ln_b': jnp.zeros((DIM,), jnp.float32), 'W_h': jax.random.normal(ks[1], (DIM, 2 * HID), jnp.float32) * 0.02, 'b_h': jnp.zeros((2 * HID,), jnp.float32), 'W_qk': jax.random.normal(ks[2], (DIM, QK), jnp.float32) * 0.02, 'b_qk': jnp.zeros((QK,), jnp.float32), 'os_gamma': jax.random.normal(ks[3], (4, QK), jnp.float32) * 0.02, 'os_beta': jnp.zeros((4, QK), jnp.float32), 'rel_emb': jax.random.normal(ks[4], (NUM_BUCKETS, 1), jnp.float32) * 0.02, 'W_out': jax.random.normal(ks[5], (HID, DIM), jnp.float32) * 0.02, 'b_out': jnp.zeros((DIM,), jnp.float32)}
    _L0_attn_in = _L0_attn_setup()

    def _L0_ffn_setup():
        import jax, jax.numpy as jnp
        import numpy as np
        B, T, D, E, K = (4, 256, 128, 8, 2)
        key = jax.random.key(seed)
        k1, k2, k3 = jax.random.split(key, 3)
        x = jax.random.normal(k1, (B, T, D), dtype=jnp.float32)
        Wg = jax.random.normal(k2, (D, E), dtype=jnp.float32) * (1.0 / np.sqrt(D))
        lim = float(np.sqrt(6.0 / (D + D)))
        We = jax.random.uniform(k3, (E, D, D), dtype=jnp.float32, minval=-lim, maxval=lim)
        return {'x': x, 'Wg': Wg, 'We': We}
    _L0_ffn_in = _L0_ffn_setup()

    def _L1_attn_setup():
        import jax, jax.numpy as jnp
        import numpy as np
        DIM = 128
        HEADS = 16
        HEAD_DIM = DIM // HEADS

        def _feature_map(z, W, b):
            p = jnp.einsum('bhtd,ed->bhte', z, W) + b
            return jnp.concatenate([jax.nn.softmax(p, axis=-1), jax.nn.softmax(-p, axis=-1)], axis=-1)
        key = jax.random.key(seed)
        ks = jax.random.split(key, 7)
        s = 0.02
        x = jax.random.normal(ks[0], (1, 128, DIM), dtype=jnp.float32)
        w_qkv = jax.random.normal(ks[1], (3 * DIM, DIM), dtype=jnp.float32) * s
        wq_map = jnp.eye(HEAD_DIM, dtype=jnp.float32) + jax.random.normal(ks[2], (HEAD_DIM, HEAD_DIM), dtype=jnp.float32) * s
        bq_map = jax.random.normal(ks[3], (HEAD_DIM,), dtype=jnp.float32) * s
        wk_map = jnp.eye(HEAD_DIM, dtype=jnp.float32) + jax.random.normal(ks[4], (HEAD_DIM, HEAD_DIM), dtype=jnp.float32) * s
        bk_map = jax.random.normal(ks[5], (HEAD_DIM,), dtype=jnp.float32) * s
        w_out = jax.random.normal(ks[6], (DIM, DIM), dtype=jnp.float32) * s
        return {'x': x, 'w_qkv': w_qkv, 'wq_map': wq_map, 'bq_map': bq_map, 'wk_map': wk_map, 'bk_map': bk_map, 'w_out': w_out}
    _L1_attn_in = _L1_attn_setup()

    def _L1_ffn_setup():
        import jax, jax.numpy as jnp
        import numpy as np
        B, S, H = (2, 128, 128)
        KD, NH, K = (128, 8, 8)
        NE = 8192
        NK = 32
        EPS = 1e-05
        key = jax.random.key(seed)
        ks = jax.random.split(key, 5)
        inputs = jax.random.normal(ks[0], (B, S, H), jnp.float32)
        bn_gamma = jnp.ones((H,), jnp.float32)
        bn_beta = jnp.zeros((H,), jnp.float32)
        w_q = jax.random.normal(ks[1], (2 * NH * KD, H), jnp.float32) * (1.0 / np.sqrt(H))
        keys_p = jax.random.normal(ks[2], (NH, NK, 2, KD), jnp.float32) * 0.02
        lim = float(np.sqrt(6.0 / (NE + H)))
        down = jax.random.uniform(ks[3], (NE, H), jnp.float32, -lim, lim)
        up = jax.random.uniform(ks[4], (NE, H), jnp.float32, -lim, lim)
        return {'inputs': inputs, 'bn_gamma': bn_gamma, 'bn_beta': bn_beta, 'w_q': w_q, 'keys_p': keys_p, 'down': down, 'up': up}
    _L1_ffn_in = _L1_ffn_setup()
    _d = {'L0_attn_x': _L0_attn_in['x'], 'L0_attn_ln_g': _L0_attn_in['ln_g'], 'L0_attn_ln_b': _L0_attn_in['ln_b'], 'L0_attn_W_h': _L0_attn_in['W_h'], 'L0_attn_b_h': _L0_attn_in['b_h'], 'L0_attn_W_qk': _L0_attn_in['W_qk'], 'L0_attn_b_qk': _L0_attn_in['b_qk'], 'L0_attn_os_gamma': _L0_attn_in['os_gamma'], 'L0_attn_os_beta': _L0_attn_in['os_beta'], 'L0_attn_rel_emb': _L0_attn_in['rel_emb'], 'L0_attn_W_out': _L0_attn_in['W_out'], 'L0_attn_b_out': _L0_attn_in['b_out'], 'L0_ffn_Wg': _L0_ffn_in['Wg'], 'L0_ffn_We': _L0_ffn_in['We'], 'L1_attn_w_qkv': _L1_attn_in['w_qkv'], 'L1_attn_wq_map': _L1_attn_in['wq_map'], 'L1_attn_bq_map': _L1_attn_in['bq_map'], 'L1_attn_wk_map': _L1_attn_in['wk_map'], 'L1_attn_bk_map': _L1_attn_in['bk_map'], 'L1_attn_w_out': _L1_attn_in['w_out'], 'L1_ffn_bn_gamma': _L1_ffn_in['bn_gamma'], 'L1_ffn_bn_beta': _L1_ffn_in['bn_beta'], 'L1_ffn_w_q': _L1_ffn_in['w_q'], 'L1_ffn_keys_p': _L1_ffn_in['keys_p'], 'L1_ffn_down': _L1_ffn_in['down'], 'L1_ffn_up': _L1_ffn_in['up']}
    _x0 = _d['L0_attn_x']
    _d['L0_attn_x'] = jax.random.normal(jax.random.fold_in(jax.random.key(seed), 1), (4, 512, 128), dtype=_x0.dtype)
    del _x0
    return _d

def reference(L0_attn_x, L0_attn_ln_g, L0_attn_ln_b, L0_attn_W_h, L0_attn_b_h, L0_attn_W_qk, L0_attn_b_qk, L0_attn_os_gamma, L0_attn_os_beta, L0_attn_rel_emb, L0_attn_W_out, L0_attn_b_out, L0_ffn_Wg, L0_ffn_We, L1_attn_w_qkv, L1_attn_wq_map, L1_attn_bq_map, L1_attn_wk_map, L1_attn_bk_map, L1_attn_w_out, L1_ffn_bn_gamma, L1_ffn_bn_beta, L1_ffn_w_q, L1_ffn_keys_p, L1_ffn_down, L1_ffn_up):

    def _L0_attn_ref(x, ln_g, ln_b, W_h, b_h, W_qk, b_qk, os_gamma, os_beta, rel_emb, W_out, b_out):
        import math
        import jax, jax.numpy as jnp
        import numpy as np
        DIM = 128
        HID = 256
        QK = 128
        G = 32
        B, N = (4, 512)
        NUM_BUCKETS = 32
        MAX_DIST = 128

        def _rel_pos_bias(rel_emb, g, scale):
            pos = jnp.arange(g)
            rel = pos[None, :] - pos[:, None]
            n = -rel
            nb = NUM_BUCKETS // 2
            ret = (n < 0).astype(jnp.int32) * nb
            n = jnp.abs(n)
            max_exact = nb // 2
            is_small = n < max_exact
            val_large = max_exact + (jnp.log(jnp.maximum(n, 1).astype(jnp.float32) / max_exact) / math.log(MAX_DIST / max_exact) * (nb - max_exact)).astype(jnp.int32)
            val_large = jnp.minimum(val_large, nb - 1)
            bucket = ret + jnp.where(is_small, n, val_large)
            return rel_emb[bucket, 0] * scale

        def _layernorm(x, g, b, eps=1e-05):
            mu = jnp.mean(x, axis=-1, keepdims=True)
            var = jnp.mean((x - mu) ** 2, axis=-1, keepdims=True)
            return (x - mu) * jax.lax.rsqrt(var + eps) * g + b
        b, n = (x.shape[0], x.shape[1])
        ng = n // G
        normed = _layernorm(x, ln_g, ln_b)
        hid = jax.nn.silu(normed @ W_h + b_h)
        v, gate = (hid[..., :HID], hid[..., HID:])
        qk = jax.nn.silu(normed @ W_qk + b_qk)
        heads = qk[..., None, :] * os_gamma + os_beta
        quad_q, lin_q, quad_k, lin_k = [heads[..., h, :] for h in range(4)]

        def grp(t):
            return t.reshape(b, ng, G, t.shape[-1])
        quad_q, quad_k, lin_q, lin_k, vg = map(grp, (quad_q, quad_k, lin_q, lin_k, v))
        sim = jnp.einsum('bgid,bgjd->bgij', quad_q, quad_k) / G
        sim = sim + _rel_pos_bias(rel_emb, G, QK ** 0.5)
        attn = jax.nn.relu(sim) ** 2
        quad_out = jnp.einsum('bgij,bgje->bgie', attn, vg)
        lin_kv = jnp.einsum('bgnd,bgne->bde', lin_k, vg) / n
        lin_out = jnp.einsum('bde,bgnd->bgne', lin_kv, lin_q)
        out = (quad_out + lin_out).reshape(b, n, HID)
        out = gate * out
        return out @ W_out + b_out + x

    def _L0_ffn_ref(x, Wg, We):
        import jax, jax.numpy as jnp
        import numpy as np
        B, T, D, E, K = (4, 256, 128, 8, 2)
        logits = jnp.einsum('btd,de->bte', x, Wg)
        gate = jax.nn.softmax(logits, axis=-1)
        top_val, top_idx = jax.lax.top_k(gate, K)
        top_w = top_val / (jnp.sum(top_val, axis=-1, keepdims=True) + 1e-09)
        x_experts = jnp.einsum('btd,edm->btem', x, We)
        x_sel = jnp.take_along_axis(x_experts, top_idx[..., None], axis=2)
        out = jnp.sum(x_sel * top_w[..., None], axis=2)
        return out

    def _L1_attn_ref(x, w_qkv, wq_map, bq_map, wk_map, bk_map, w_out):
        import jax, jax.numpy as jnp
        import numpy as np
        DIM = 128
        HEADS = 16
        HEAD_DIM = DIM // HEADS

        def _feature_map(z, W, b):
            p = jnp.einsum('bhtd,ed->bhte', z, W) + b
            return jnp.concatenate([jax.nn.softmax(p, axis=-1), jax.nn.softmax(-p, axis=-1)], axis=-1)
        b, t, dim = x.shape
        h, hd = (HEADS, HEAD_DIM)
        qkv = (x @ w_qkv.T).reshape(b, t, 3, h, hd)
        q, k, v = [jnp.transpose(qkv[:, :, i], (0, 2, 1, 3)) for i in range(3)]
        q = _feature_map(q, wq_map, bq_map)
        k = _feature_map(k, wk_map, bk_map)
        k_prefix = jnp.cumsum(k, axis=2)
        kv_prefix = jnp.cumsum(jnp.einsum('bhtf,bhtd->bhtfd', k, v), axis=2)
        numer = jnp.einsum('bhtf,bhtfd->bhtd', q, kv_prefix)
        denom = jnp.maximum(jnp.einsum('bhtf,bhtf->bht', q, k_prefix)[..., None], 1e-06)
        y = jnp.transpose(numer / denom, (0, 2, 1, 3)).reshape(b, t, dim)
        return y @ w_out.T

    def _L1_ffn_ref(inputs, bn_gamma, bn_beta, w_q, keys_p, down, up):
        import jax, jax.numpy as jnp
        import numpy as np
        B, S, H = (2, 128, 128)
        KD, NH, K = (128, 8, 8)
        NE = 8192
        NK = 32
        EPS = 1e-05
        b, s, d = inputs.shape
        x = inputs.reshape(b * s, d)
        mean = x.mean(axis=0)
        var = x.var(axis=0)
        xn = (x - mean) * jax.lax.rsqrt(var + EPS) * bn_gamma + bn_beta
        xn = xn.reshape(b, s, d)
        q = (xn @ w_q.T).reshape(b, s, 2, NH, KD).transpose(2, 0, 1, 3, 4)
        sim = jnp.einsum('pbnhd,hkpd->pbnhk', q, keys_p)
        scores, idx = jax.lax.top_k(sim, K)
        all_scores = (scores[0][..., :, None] + scores[1][..., None, :]).reshape(b, s, NH, K * K)
        all_idx = (idx[0][..., :, None] * NK + idx[1][..., None, :]).reshape(b, s, NH, K * K)
        sc, pk = jax.lax.top_k(all_scores, K)
        indices = jnp.take_along_axis(all_idx, pk, axis=-1)
        wd = down[indices]
        hmid = jnp.einsum('bnd,bnhkd->bnhk', inputs, wd)
        hmid = jax.nn.sigmoid(sc) * jax.nn.gelu(hmid, approximate=False)
        wu = up[indices]
        return jnp.einsum('bnhk,bnhkd->bnd', hmid, wu)
    x = L0_attn_x
    x = _layernorm(x + _L0_attn_ref(x, L0_attn_ln_g, L0_attn_ln_b, L0_attn_W_h, L0_attn_b_h, L0_attn_W_qk, L0_attn_b_qk, L0_attn_os_gamma, L0_attn_os_beta, L0_attn_rel_emb, L0_attn_W_out, L0_attn_b_out), axis=-1)
    x = _layernorm(x + _L0_ffn_ref(x, L0_ffn_Wg, L0_ffn_We), axis=-1)
    x = _layernorm(x + _L1_attn_ref(x, L1_attn_w_qkv, L1_attn_wq_map, L1_attn_bq_map, L1_attn_wk_map, L1_attn_bk_map, L1_attn_w_out), axis=-1)
    x = _layernorm(x + _L1_ffn_ref(x, L1_ffn_bn_gamma, L1_ffn_bn_beta, L1_ffn_w_q, L1_ffn_keys_p, L1_ffn_down, L1_ffn_up), axis=-1)
    return x

_drawn_inputs = setup_inputs


def setup_inputs(seed=0):
    import zlib

    import numpy as np

    out = dict(_drawn_inputs(seed))
    spreads = {'L0_attn_ln_g': (1.0, 0.6),
     'L0_attn_ln_b': (0.0, 0.8),
     'L0_attn_b_h': (0.0, 0.8),
     'L0_attn_b_qk': (0.0, 0.8),
     'L0_attn_os_beta': (0.0, 0.8),
     'L0_attn_b_out': (0.0, 0.1),
     'L1_ffn_bn_gamma': (1.0, 0.6),
     'L1_ffn_bn_beta': (0.0, 0.8)}
    factors = {'L0_attn_W_h': 8.0,
     'L0_attn_W_qk': 8.0,
     'L0_attn_os_gamma': 8.0,
     'L0_attn_rel_emb': 8.0,
     'L0_attn_W_out': 8.0,
     'L1_attn_w_qkv': 8.0,
     'L1_attn_wq_map': 8.0,
     'L1_attn_bq_map': 8.0,
     'L1_attn_wk_map': 8.0,
     'L1_attn_bk_map': 8.0,
     'L1_attn_w_out': 8.0,
     'L1_ffn_w_q': 7.222,
     'L1_ffn_keys_p': 7.197,
     'L1_ffn_down': 7.094,
     'L1_ffn_up': 7.006}
    for name, (base, spread) in spreads.items():
        noise = np.random.default_rng([zlib.crc32(name.encode()), seed]).standard_normal(out[name].shape)
        drawn = base * np.exp(spread * noise) if base else spread * noise
        out[name] = jnp.asarray(drawn.astype(out[name].dtype))
    for name, factor in factors.items():
        out[name] = (out[name] * factor).astype(out[name].dtype)
    return out
```

```python
from contextlib import ExitStack

import numpy as np
import concourse.bass as bass
from concourse import mybir

ALU = mybir.AluOpType
ACT = mybir.ActivationFunctionType
X = mybir.AxisListType.X
F32 = mybir.dt.float32
F16 = mybir.dt.float16
U32 = mybir.dt.uint32

P = 128
EPS = 1e-5
MASKED = -1e30
WEIGHT_SCALE = 4096.0


class Sem:

    def __init__(self, handle, per=1, start=0):
        self.h, self.per, self.start, self.seen = handle, per, start, 0

    def at(self, b, k):
        return b * self.per + (k + self.start)


def wait(eng, s, b, k=None):
    eng.wait_ge(s.h, s.at(b, s.per if k is None else k))


def wait_last(eng, s, b):
    assert s.start
    eng.wait_ge(s.h, s.at(b, 0))


class Shared:
    pass


def bucket_of(rel, buckets=32, max_dist=128):
    nb = buckets // 2
    n, exact = abs(rel), nb // 2
    if n < exact:
        return n + (nb if rel < 0 else 0)
    large = np.log(np.float32(n) / np.float32(exact)) / np.float32(np.log(max_dist / exact)) * np.float32(nb - exact)
    return min(exact + int(large), nb - 1) + (nb if rel < 0 else 0)


def bucket_runs(group):
    row = [bucket_of(m - (group - 1)) for m in range(2 * group - 1)]
    runs, i = [], 0
    while i < len(row):
        j = i + 1
        step = row[j] - row[i] if j < len(row) and row[j] - row[i] in (0, 1) else 0
        while j < len(row) and row[j] - row[j - 1] == step:
            j += 1
        runs.append((i, j - i, row[i], step))
        i = j
    return runs


def build(nc, x, ln_g, ln_b, W_h, b_h, W_qk, b_qk, os_gamma, os_beta, rel_emb, W_out, b_out, Wg, We,
          w_qkv, wq_map, bq_map, wk_map, bk_map, w_out, bn_gamma, bn_beta, w_q, keys_p, down, up, out):
    B, N, D = x.shape
    HID = W_h.shape[1] // 2
    EC = HID // P
    GROUP = 32
    T = N // P
    E = Wg.shape[1]
    HEADS, HD = D // wq_map.shape[0], wq_map.shape[0]
    QUADS = HEADS // 4
    NH, NK, _, KD = keys_p.shape
    K = 8
    SETS = 2 * NH
    EH = NK * NK // P
    PAIRS = T // 2

    ctx = ExitStack()
    with ctx:
        def sb(name, shape, dt=F32):
            return ctx.enter_context(nc.sbuf_tensor(name, shape, dt))

        def sem(name, per=1):
            s = Sem(ctx.enter_context(nc.semaphore(name)), per)
            return s

        bank = [ctx.enter_context(nc.psum_tensor(f"bank{i}", [P, 512], F32)) for i in range(8)]

        ident = sb("ident", [P, P])
        flip = sb("flip", [GROUP, P])
        spread = sb("spread", [HD, P])
        causal = sb("causal", [P, P])
        same8 = sb("same8", [P, HEADS, HD])
        minus_half = sb("minus_half", [P, 1])
        same_quad = sb("same_quad", [P, 4])
        iota_e = sb("iota_e", [P, E])
        iota_k = sb("iota_k", [P, K])
        iota_lo = sb("iota_lo", [P, P, P], F16)
        iota_hi = sb("iota_hi", [P, EH, P], F16)
        g_col, b_col = sb("g_col", [P, 1]), sb("b_col", [P, 1])
        wh, bh_gate, bh_v = sb("wh", [P, 2 * HID]), sb("bh_gate", [P, EC]), sb("bh_v", [P, HID])
        wqk, bqk_col = sb("wqk", [P, P]), sb("bqk_col", [P, 1])
        gam, bet = sb("gam", [P, 4]), sb("bet", [P, 4])
        hankel, bias_t, bias_raw = sb("hankel", [GROUP, GROUP]), sb("bias_t", [P, P]), sb("bias_raw", [P, GROUP])
        wout0, bout = sb("wout0", [P, EC, P]), sb("bout", [P, P])
        wg, we = sb("wg", [P, E]), sb("we", [P, E, P])
        wqkv = sb("wqkv", [P, 3, P])
        maps_t, maps_bd = sb("maps_t", [HD, 2, HD]), sb("maps_bd", [P, 2, HEADS, HD])
        map_bias = sb("map_bias", [P, 2, HD])
        wcomb = sb("wcomb", [P, 3 * P])
        wout1, wout1_t = sb("wout1", [P, P]), sb("wout1_t", [P, P])
        bn_g, bn_b = sb("bn_g", [P, 1]), sb("bn_b", [P, 1])
        upw, down_t = sb("upw", [P, EH, P]), sb("down_t", [P, EH, P])
        keysim = sb("keysim", [P, SETS, NK])
        x3t = sb("x3t", [P, B * N])
        x3 = sb("x3", [P, B * T, P])
        bn_raw = sb("bn_raw", [P, B, 6])
        bn_mv, bn_scale = sb("bn_mv", [P, 2]), sb("bn_scale", [P, 1])
        xall = sb("xall", [P, B * T, P])
        rel_row = nc.dram_tensor("rel_row", [2 * GROUP], F32, kind="Internal").ap()

        loaded = {n: sem("ld_" + n) for n in ("l0", "moe", "l1", "bn", "rel", "hankel", "peer", "keys")}
        x_in = sem("x_in", 16)
        consts = sem("consts")
        dset = sem("dve_setup")
        setup_mm, setup_cp = sem("setup_mm"), sem("setup_cp")

        load_count = {}

        def load(eng, group, dst, src):
            load_count[group] = load_count.get(group, 0) + 1
            eng.dma_start(dst, src, allow_slow_non_contiguous=True).then_inc(loaded[group].h, 16)

        def arrived(eng, group):
            eng.wait_ge(loaded[group].h, 16 * load_count[group])

        def col(v):
            return v.rearrange("(p a) -> p a", a=1)

        def rows(v, n=P):
            return bass.AP(v.tensor, v.offset, [[0, n]] + [list(s) for s in v.ap])

        def bc(ap, shape):
            return ap.broadcast_to(shape)

        setup_sb = ExitStack()
        wqn = setup_sb.enter_context(nc.sbuf_tensor("wqn", [P, SETS, P], F32))
        keysn = setup_sb.enter_context(nc.sbuf_tensor("keysn", [P, 2, 2, KD], F32))
        keys_t = setup_sb.enter_context(nc.sbuf_tensor("keys_t", [P, 2, 2, P], F32))
        downn = setup_sb.enter_context(nc.sbuf_tensor("downn", [P, EH, P], F32))
        iota_u = setup_sb.enter_context(nc.sbuf_tensor("iota_u", [P, P], F32))

        with nc.Block() as block:
            @block.sync
            def _(sp):
                for pos, n, first, step in bucket_runs(GROUP):
                    dst = rel_row[pos:pos + n]
                    src = bass.AP(rel_emb.tensor, rel_emb.offset + first, [[step, n], [1, 1]])
                    load(sp, "rel", dst.rearrange("(n a) -> n a", a=1), src)
                for b in range(B):
                    sp.dma_start(xall[:, T * b:T * b + T, :], x[b].rearrange("(t p) d -> p t d", p=P))\
                        .then_inc(x_in.h, 16)
                load(sp, "l0", g_col[:], col(ln_g))
                load(sp, "l0", b_col[:], col(ln_b))
                load(sp, "l0", wqk[:], W_qk)
                load(sp, "l0", wh[:], W_h)
                load(sp, "l0", bqk_col[:], col(b_qk))
                load(sp, "l0", bh_gate[:], b_h[HID:2 * HID].rearrange("(c p) -> p c", p=P))
                load(sp, "l0", bh_v[:], rows(b_h[0:HID]))
                load(sp, "l0", gam[:], os_gamma.rearrange("h p -> p h"))
                load(sp, "l0", bet[:], os_beta.rearrange("h p -> p h"))
                load(sp, "l0", wout0[:], W_out.rearrange("(c p) n -> p c n", p=P))
                load(sp, "l0", bout[:], rows(b_out))
                arrived(sp, "rel")
                load(sp, "hankel", hankel[:], bass.AP(rel_row.tensor, rel_row.offset, [[1, GROUP], [1, GROUP]]))
                load(sp, "moe", wg[:], Wg)
                load(sp, "moe", we[:], We.rearrange("e d m -> d e m"))

            @block.scalar
            def _(act):
                load(act, "l1", wqkv[:], w_qkv.rearrange("(i p) d -> p i d", p=P))
                for i, (w, bias) in enumerate(((wq_map, bq_map), (wk_map, bk_map))):
                    load(act, "l1", maps_t[:, i, :], w.rearrange("e d -> d e"))
                    load(act, "l1", map_bias[:, i, :], rows(bias))
                load(act, "l1", wout1[:], w_out)
                load(act, "keys", wqn[:], w_q.rearrange("(s p) d -> p s d", p=P))
                load(act, "keys", keysn[:].rearrange("p a s k -> p a (s k)"),
                     keys_p.rearrange("(a h) k s d -> (h k) a (s d)", a=2))
                load(act, "keys", downn[:], down[0:NK * NK, :].rearrange("(c p) d -> p c d", p=P))
                load(act, "peer", upw[:], up[0:NK * NK, :].rearrange("(c p) d -> p c d", p=P))
                load(act, "bn", bn_g[:], col(bn_gamma))
                load(act, "bn", bn_b[:], col(bn_beta))

            @block.gpsimd
            def _(pool):
                nc.gpsimd.memset(ident[:], 0.0)
                nc.gpsimd.memset(minus_half[:], -0.5)
                nc.gpsimd.memset(flip[:], 0.0)
                nc.gpsimd.memset(spread[:], 0.0)
                nc.gpsimd.memset(causal[:], 1.0)
                nc.gpsimd.memset(same8[:], 1.0)
                nc.gpsimd.memset(same_quad[:], 1.0)
                nc.gpsimd.iota(iota_u[:], pattern=[[1, P]], base=0, channel_multiplier=0,
                               allow_small_or_imprecise_dtypes=True).then_inc(consts.h, 1)
                pool.wait_ge(consts.h, 1)
                nc.gpsimd.affine_select(ident[:], ident[:], pattern=[[-1, P]], compare_op=ALU.not_equal, fill=1.0,
                                        base=0, channel_multiplier=1)
                nc.gpsimd.affine_select(flip[:].rearrange("p (g j) -> p g j", j=GROUP),
                                        flip[:].rearrange("p (g j) -> p g j", j=GROUP),
                                        pattern=[[0, P // GROUP], [1, GROUP]], compare_op=ALU.not_equal, fill=1.0,
                                        base=1 - GROUP, channel_multiplier=1)
                nc.gpsimd.affine_select(spread[:].rearrange("p (h d) -> p h d", d=HD),
                                        spread[:].rearrange("p (h d) -> p h d", d=HD),
                                        pattern=[[0, HEADS], [-1, HD]], compare_op=ALU.not_equal, fill=1.0,
                                        base=0, channel_multiplier=1)
                nc.gpsimd.affine_select(causal[:], causal[:], pattern=[[1, P]], compare_op=ALU.is_ge, fill=0.0,
                                        base=0, channel_multiplier=-1)
                nc.gpsimd.affine_select(same8[:], same8[:], pattern=[[-HD, HEADS], [0, HD]], compare_op=ALU.is_ge,
                                        fill=0.0, base=0, channel_multiplier=1)
                nc.gpsimd.affine_select(same_quad[:], same_quad[:], pattern=[[-32, 4]], compare_op=ALU.is_ge,
                                        fill=0.0, base=0, channel_multiplier=1).then_inc(consts.h, 1)
                pool.wait_ge(consts.h, 2)
                nc.gpsimd.affine_select(same8[:], same8[:], pattern=[[HD, HEADS], [0, HD]], compare_op=ALU.is_ge,
                                        fill=0.0, base=HD - 1, channel_multiplier=-1)
                nc.gpsimd.affine_select(same_quad[:], same_quad[:], pattern=[[32, 4]], compare_op=ALU.is_ge,
                                        fill=0.0, base=31, channel_multiplier=-1).then_inc(consts.h, 1)

            @block.vector
            def _(dve):
                nc.vector.memset(bias_t[:], MASKED).then_inc(dset.h, 1)
                dve.wait_ge(dset.h, 1)
                dve.wait_ge(consts.h, 1)
                nc.vector.tensor_copy(iota_e[:], iota_u[:, 0:E])
                nc.vector.tensor_copy(iota_k[:], iota_u[:, 0:K])
                nc.vector.tensor_copy(iota_hi[:], bc(iota_u[:, 0:EH].unsqueeze(2), [P, EH, P]))
                nc.vector.tensor_copy(iota_lo[:], bc(iota_u[:, :].unsqueeze(2), [P, P, P])).then_inc(dset.h, 1)
                dve.wait_ge(consts.h, 3)
                dve.wait_ge(setup_mm.h, 1)
                for i in range(2):
                    nc.vector.tensor_tensor(maps_bd[:, i], same8[:],
                                            bc(bank[0][:, HD * i:HD * i + HD].unsqueeze(1), [P, HEADS, HD]),
                                            ALU.mult).then_inc(dset.h, 1)
                dve.wait_ge(setup_mm.h, 2)
                for g in range(P // GROUP):
                    q = slice(GROUP * g, GROUP * g + GROUP)
                    nc.vector.tensor_scalar(bias_t[q, q], bank[1][q, 0:GROUP], float(P ** 0.5), None,
                                            ALU.mult)
                dve.wait_ge(setup_mm.h, 3)
                nc.vector.tensor_copy(wcomb[:], bank[2][:, 0:3 * P])
                nc.vector.tensor_copy(wout1_t[:], bank[2][:, 3 * P:4 * P])
                dve.wait_ge(setup_mm.h, 4)
                nc.vector.tensor_copy(keys_t[:].rearrange("p a s k -> p (a s k)"), bank[3][:]).then_inc(dset.h, 1)
                dve.wait_ge(setup_mm.h, 5)
                for c in range(2):
                    nc.vector.tensor_copy(down_t[:, 4 * c:4 * c + 4, :].rearrange("p c k -> p (c k)"), bank[4 + c][:])
                dve.wait_ge(setup_mm.h, 6)
                nc.vector.tensor_copy(keysim[:].rearrange("p s k -> p (s k)"), bank[6][:]).then_inc(dset.h, 1)

            @block.tensor
            def _(pe):
                pe.wait_ge(consts.h, 3)
                arrived(pe, "l1")
                for i in range(2):
                    mm = nc.tensor.matmul(bank[0][:, HD * i:HD * i + HD], spread[:], maps_t[:, i, :],
                                          start=True, stop=True)
                mm.then_inc(setup_mm.h, 1)
                arrived(pe, "hankel")
                nc.tensor.matmul(bank[1][:, 0:GROUP], flip[:], hankel[:], start=True, stop=True).then_inc(setup_mm.h, 1)
                pe.wait_ge(dset.h, 4)
                for i in range(2):
                    nc.tensor.matmul(bank[2][:, P * i:P * i + P], wqkv[:, i, :],
                                     maps_bd[:, i].rearrange("p h e -> p (h e)"), start=True, stop=True)
                nc.tensor.transpose(bank[2][:, 2 * P:3 * P], wqkv[:, 2, :], ident[:])
                nc.tensor.transpose(bank[2][:, 3 * P:4 * P], wout1[:], ident[:]).then_inc(setup_mm.h, 1)
                arrived(pe, "keys")
                for a in range(2):
                    for s in range(2):
                        mm = nc.tensor.transpose(bank[3][:, P * (2 * a + s):P * (2 * a + s) + P], keysn[:, a, s, :],
                                                 ident[:])
                mm.then_inc(setup_mm.h, 1)
                for c in range(EH):
                    mm = nc.tensor.transpose(bank[4 + c // 4][:, P * (c % 4):P * (c % 4) + P], downn[:, c, :], ident[:])
                mm.then_inc(setup_mm.h, 1)
                pe.wait_ge(dset.h, 5)
                for s in range(2):
                    for h in range(NH):
                        r = s * NH + h
                        mm = nc.tensor.matmul(bank[6][:, NK * r:NK * r + NK], wqn[:, r, :],
                                              keys_t[:, h // 4, s, NK * (h % 4):NK * (h % 4) + NK],
                                              start=True, stop=True)
                mm.then_inc(setup_mm.h, 1)
        setup_sb.close()

        shared = Shared()
        shared.B, shared.D, shared.E, shared.EC, shared.EH, shared.GROUP = B, D, E, EC, EH, GROUP
        shared.HD, shared.HEADS, shared.HID, shared.K, shared.N, shared.NH = HD, HEADS, HID, K, N, NH
        shared.NK, shared.PAIRS, shared.QUADS, shared.SETS, shared.T, shared.arrived = NK, PAIRS, QUADS, SETS, T, arrived
        shared.b_col, shared.bank, shared.bc, shared.bet, shared.bh_gate, shared.bh_v = b_col, bank, bc, bet, bh_gate, bh_v
        shared.bias_t, shared.bn_b, shared.bn_g, shared.bn_mv, shared.bn_raw, shared.bn_scale = bias_t, bn_b, bn_g, bn_mv, bn_raw, bn_scale
        shared.bout, shared.bqk_col, shared.causal, shared.down_t, shared.dset, shared.g_col = bout, bqk_col, causal, down_t, dset, g_col
        shared.gam, shared.ident, shared.iota_e, shared.iota_hi, shared.iota_k, shared.iota_lo = gam, ident, iota_e, iota_hi, iota_k, iota_lo
        shared.keysim, shared.map_bias, shared.minus_half, shared.out, shared.same_quad, shared.upw = keysim, map_bias, minus_half, out, same_quad, upw
        shared.wcomb, shared.we, shared.wg, shared.wh, shared.wout0, shared.wout1_t = wcomb, we, wg, wh, wout0, wout1_t
        shared.wqk, shared.x3, shared.x3t, shared.x_in, shared.xall = wqk, x3, x3t, x_in, xall
        layers_loop(nc, shared)
        peer_loop(nc, shared)


def wait_apart(eng, spare, s, value):
    eng.wait_ge(s.h, value)
    eng.sem_inc(spare, 1)


def layer_norm(nc, dve, spare, b, own, stats, mv, rstd, src, dst, tiles, var_ok, rstd_ok, done):
    for u in range(tiles):
        nc.vector.bn_stats(stats[:, u, :], src(u)).then_inc(own.h, 1)
        own.seen += 1
    for u in range(tiles):
        wait_apart(dve, spare, own, own.at(b, own.seen - tiles + u + 1))
        ins = nc.vector.bn_aggr(mv[:, u, :], stats[:, u, :])
    ins.then_inc(own.h, 1)
    own.seen += 1
    dve.wait_ge(own.h, own.at(b, own.seen))
    nc.vector.tensor_scalar(rstd[:], mv[:, :, 1:2], EPS, None, ALU.add).then_inc(var_ok.h, 1)
    var_ok.seen += 1
    dve.wait_ge(rstd_ok.h, rstd_ok.at(b, var_ok.seen))
    for u in range(tiles):
        nc.vector.tensor_scalar(dst(u), src(u), mv[:, u, 0:1], rstd[:, u, :], ALU.subtract, ALU.mult)\
            .then_inc(done.h, 1)


def layers_loop(nc, v):
    B, N, D, T, E, EC, HID = v.B, v.N, v.D, v.T, v.E, v.EC, v.HID
    HEADS, HD, QUADS, GROUP = v.HEADS, v.HD, v.QUADS, v.GROUP
    bank, ident, bc, arrived = v.bank, v.ident, v.bc, v.arrived
    VW = HD + 1
    ctx = ExitStack()
    with ctx:
        def sb(name, shape, dt=F32):
            return ctx.enter_context(nc.sbuf_tensor(name, shape, dt))

        primed = []

        def sem(name, per=1, start=0):
            s = Sem(ctx.enter_context(nc.semaphore(name)), per, start)
            if start:
                primed.append(s)
            return s

        xres = sb("xres", [P, T, P])
        xh = sb("xh", [P, T, P])
        normed_t = sb("normed_t", [P, N])
        qk_t = sb("qk_t", [P, N])
        heads_t = sb("heads_t", [P, 4, N])
        gate_t = sb("gate_t", [P, EC, N])
        val = sb("val", [P, T, HID])
        sim = sb("sim", [P, T, P])
        attn_t = sb("attn_t", [P, T, P])
        link = sb("link", [P, T, P])
        kv = sb("kv", [P, HID])
        gated_t = sb("gated_t", [P, EC, N])
        z = sb("z", [P, T, P])
        x1 = sb("x1", [P, T, P])
        x1t = sb("x1t", [P, N])
        lmax, lsum = sb("lmax", [P, T]), sb("lsum", [P, T])
        gate = sb("gate", [P, T, E])
        top, topi, topf = sb("top", [P, T, 8]), sb("topi", [P, T, 8], U32), sb("topf", [P, T, 8])
        hit0, hit1 = sb("hit0", [P, T, E]), sb("hit1", [P, T, E])
        wexp = sb("wexp", [P, T, E])
        z2 = sb("z2", [P, T, P])
        x2 = sb("x2", [P, T, P])
        x2t = sb("x2t", [P, N])
        pm = sb("pm", [P, 2 * HEADS, HD])
        pmax, pmin = sb("pmax", [P, 2 * HEADS]), sb("pmin", [P, 2 * HEADS])
        pe_in = sb("pe_in", [P, 2 * HEADS, 2, HD])
        psum_, prec = sb("psum_", [P, 2 * HEADS, 2]), sb("prec", [P, 2 * HEADS, 2])
        feat = sb("feat", [P, 2, HEADS, 32])
        vaug = sb("vaug", [P, HEADS, VW])
        qf_t, kf_t = sb("qf_t", [P, QUADS, P]), sb("kf_t", [P, QUADS, P])
        amask = sb("amask", [P, HEADS, P])
        state = sb("state", [P, 2, QUADS, 4, VW])
        state_new = sb("state_new", [P, QUADS, 4, VW])
        den = sb("den", [P, HEADS])
        y, yt = sb("y", [P, P]), sb("yt", [P, P])
        z3, x3b = sb("z3", [P, T, P]), sb("x3b", [P, T, P])
        stats, mv, rstd = sb("stats", [P, T, 6]), sb("mv", [P, T, 2]), sb("rstd", [P, T, 1])

        pads = sem("pads")
        xh_ok, xht_mm, normed_ok = sem("xh_ok", T), sem("xht_mm", 1), sem("normed_ok", 1)
        qk_mm, gate_mm, val_mm = sem("qk_mm", 1), sem("gate_mm", EC), sem("val_mm", 2)
        qk_ok, gate_ok, valb_ok, val_ok = sem("qk_ok", 1), sem("gate_ok", EC), sem("valb_ok", 2), sem("val_ok", 2)
        quad_ok, lin_ok = sem("quad_ok", 2, 1), sem("lin_ok", 2, 1)
        sim_mm, attn_ok = sem("sim_mm", 1), sem("attn_ok", 1)
        link_mm, link_ok, kv_mm, kv_ok = sem("link_mm", 1), sem("link_ok", 1), sem("kv_mm", 1), sem("kv_ok", 1)
        outt_mm, gated_ok, out_mm = sem("outt_mm", EC), sem("gated_ok", EC, 1), sem("out_mm", 1, 1)
        xres_ok, x1_ok = sem("xres_ok", 2), sem("x1_ok", T, 1)
        x1t_mm, x1t_ok, logit_mm = sem("x1t_mm", 1), sem("x1t_ok", 1), sem("logit_mm", 1)
        shift_ok, exp_ok = sem("shift_ok", 1), sem("exp_ok", 1)
        y_mm, y_used, x2_ok = sem("y_mm", T), sem("y_used", T), sem("x2_ok", T)
        x2t_mm, x2t_ok = sem("x2t_mm", 1), sem("x2t_ok", 1)
        qkv_mm, pm_ok, v_ok, spread_ok, fexp_ok, feat_ok = (sem("qkv_mm", T), sem("pm_ok", T), sem("v_ok", T),
                                                            sem("spread_ok", T), sem("fexp_ok", T), sem("feat_ok", T))
        ft_mm, qft_ok, kft_ok = sem("ft_mm", T), sem("qft_ok", T), sem("kft_ok", T)
        a_mm, amask_ok, num_mm, st_mm = sem("a_mm", T), sem("amask_ok", T), sem("num_mm", T), sem("st_mm", T - 1)
        st_ok, yv_ok, yt_mm, yt_ok = sem("st_ok", T - 1), sem("yv_ok", T), sem("yt_mm", T), sem("yt_ok", T)
        z3_mm, z3_ok, x3_ok, x3t_mm, x3t_ok = (sem("z3_mm", T), sem("z3_ok", T, 1), sem("x3_ok", T), sem("x3t_mm", 1),
                                               sem("x3t_ok", 1))
        bn_ok, x3_kept = sem("bn_ok", 1, 1), sem("x3_kept", 1, 1)
        var_ok, rstd_ok = sem("var_ok", 4), sem("rstd_ok", 4)
        spare = sem("spare").h
        own = sem("dve_own", 0)
        own.per = OWN_LAYERS
        pool_own = sem("pool_own", 2)

        with nc.Block() as block:
            @block.gpsimd
            def _(pool):
                for s in primed:
                    pool.sem_inc(s.h, 1)
                nc.gpsimd.memset(feat[:], 0.0)
                nc.gpsimd.memset(vaug[:], 1.0).then_inc(pads.h, 1)
                arrived(pool, "l0")

                def inverse_root(b, k):
                    wait(pool, var_ok, b, k)
                    nc.gpsimd.tensor_tensor(rstd[:], rstd[:], bc(v.minus_half[:].unsqueeze(1), [P, T, 1]), ALU.pow)\
                        .then_inc(rstd_ok.h, 1)

                with pool.Fori(0, B) as b:
                    inverse_root(b, 1)
                    wait_last(pool, x1_ok, b)
                    wait_apart(pool, spare, v.x_in, v.x_in.at(b, 16))
                    xs = v.xall[:, bass.ds(b * T, T), :]
                    nc.gpsimd.tensor_tensor(xres[:], xs, xs, ALU.add).then_inc(xres_ok.h, 1)
                    wait(pool, xres_ok, b, 1)
                    nc.gpsimd.tensor_tensor(xres[:], xres[:], bc(v.bout[:].unsqueeze(1), [P, T, P]), ALU.add)\
                        .then_inc(xres_ok.h, 1)
                    wait_last(pool, out_mm, b)
                    wait_apart(pool, spare, qk_ok, qk_ok.at(b, 1))
                    for h in (1, 3):
                        nc.gpsimd.tensor_scalar(heads_t[:, h, :], qk_t[:], v.gam[:, h:h + 1], v.bet[:, h:h + 1],
                                                ALU.mult, ALU.add).then_inc(lin_ok.h, 1)
                    for k in (2, 3, 4):
                        inverse_root(b, k)
                    wait_apart(pool, spare, x3_ok, x3_ok.at(b, T))
                    nc.gpsimd.tensor_copy(v.x3[:, bass.ds(b * T, T), :], x3b[:]).then_inc(x3_kept.h, 1)

            @block.scalar
            def _(act):
                act.wait_ge(pads.h, 1)
                arrived(act, "l0")
                with act.Fori(0, B) as b:
                    wait(act, xht_mm, b)
                    nc.scalar.activation(normed_t[:], bank[0][:], ACT.Identity, bias=v.b_col[:], scale=v.g_col[:])\
                        .then_inc(normed_ok.h, 1)
                    wait(act, qk_mm, b)
                    wait_last(act, lin_ok, b)
                    wait_last(act, quad_ok, b)
                    nc.scalar.activation(qk_t[:], bank[1][:], ACT.Silu, bias=v.bqk_col[:]).then_inc(qk_ok.h, 1)
                    wait_last(act, gated_ok, b)
                    for c in range(EC):
                        wait(act, gate_mm, b, c + 1)
                        nc.scalar.activation(gate_t[:, c, :], bank[2 + c][:], ACT.Silu, bias=v.bh_gate[:, c:c + 1])\
                            .then_inc(gate_ok.h, 1)
                    for i in range(2):
                        wait(act, valb_ok, b, i + 1)
                        nc.scalar.activation(val[:, 2 * i:2 * i + 2, :], val[:, 2 * i:2 * i + 2, :], ACT.Silu)\
                            .then_inc(val_ok.h, 1)
                    wait(act, link_mm, b)
                    nc.scalar.copy(link[:].rearrange("p t d -> p (t d)"), bank[7][:]).then_inc(link_ok.h, 1)
                    wait(act, kv_mm, b)
                    nc.scalar.mul(kv[:], bank[0][:, 0:HID], 1.0 / N).then_inc(kv_ok.h, 1)
                    wait(act, x1t_mm, b)
                    nc.scalar.copy(x1t[:], bank[4][:]).then_inc(x1t_ok.h, 1)
                    wait(act, shift_ok, b)
                    nc.scalar.activation(gate[:], gate[:], ACT.Exp).then_inc(exp_ok.h, 1)
                    wait(act, x2t_mm, b)
                    nc.scalar.copy(x2t[:], bank[4][:]).then_inc(x2t_ok.h, 1)
                    for u in range(T):
                        wait(act, pm_ok, b, u + 1)
                        if u:
                            wait(act, num_mm, b, u)
                        nc.scalar.copy(vaug[:, :, 0:HD],
                                       bank[0][:, 2 * P:3 * P].rearrange("p (h d) -> p h d", d=HD))\
                            .then_inc(v_ok.h, 1)
                        wait(act, spread_ok, b, u + 1)
                        nc.scalar.activation(pe_in[:], pe_in[:], ACT.Exp).then_inc(fexp_ok.h, 1)
                        wait(act, ft_mm, b, u + 1)
                        if u:
                            wait(act, num_mm, b, u)
                        nc.scalar.copy(qf_t[:].rearrange("p c t -> p (c t)"), bank[2][:]).then_inc(qft_ok.h, 1)
                        nc.scalar.copy(kf_t[:].rearrange("p c t -> p (c t)"), bank[3][:]).then_inc(kft_ok.h, 1)
                        wait(act, yt_mm, b, u + 1)
                        if u:
                            wait(act, z3_mm, b, u)
                        nc.scalar.copy(yt[:], bank[1][:, 288:288 + P]).then_inc(yt_ok.h, 1)
                    wait(act, x3t_mm, b)
                    nc.scalar.copy(v.x3t[:, bass.ds(b * N, N)], bank[4][:]).then_inc(x3t_ok.h, 1)

            @block.vector
            def _(dve):
                def step(ins, plain=False):
                    ins.then_inc(own.h, 1)
                    own.seen += 1
                    if plain:
                        wait_apart(dve, spare, own, own.at(bb, own.seen))
                    else:
                        dve.wait_ge(own.h, own.at(bb, own.seen))

                def norm(src, dst, done):
                    layer_norm(nc, dve, spare, bb, own, stats, mv, rstd, src, dst, T, var_ok, rstd_ok, done)

                arrived(dve, "l0")
                arrived(dve, "l1")
                dve.wait_ge(v.dset.h, 6)
                with dve.Fori(0, B) as b:
                    bb = b
                    own.seen = var_ok.seen = 0
                    wait_apart(dve, spare, v.x_in, v.x_in.at(b, 16))
                    norm(lambda u: v.xall[:, bass.ds(b * T + u, 1), :].rearrange("p a d -> p (a d)"),
                         lambda u: xh[:, u, :], xh_ok)
                    for i in range(2):
                        wait(dve, val_mm, b, i + 1)
                        nc.vector.tensor_tensor(val[:, 2 * i:2 * i + 2, :],
                                                bank[4 + i][:].rearrange("p (t e) -> p t e", t=2),
                                                bc(v.bh_v[:].unsqueeze(1), [P, 2, HID]), ALU.add)\
                            .then_inc(valb_ok.h, 1)
                    wait(dve, qk_ok, b)
                    for h in (0, 2):
                        nc.vector.tensor_scalar(heads_t[:, h, :], qk_t[:], v.gam[:, h:h + 1], v.bet[:, h:h + 1],
                                                ALU.mult, ALU.add).then_inc(quad_ok.h, 1)
                    wait(dve, sim_mm, b)
                    step(nc.vector.scalar_tensor_tensor(sim[:], bank[6][:].rearrange("p (t i) -> p t i", t=T),
                                                        1.0 / GROUP, bc(v.bias_t[:].unsqueeze(1), [P, T, P]),
                                                        ALU.mult, ALU.add))
                    nc.vector.scalar_tensor_tensor(attn_t[:], sim[:], 0.0, sim[:], ALU.max, ALU.mult)\
                        .then_inc(attn_ok.h, 1)
                    for c in range(EC):
                        wait(dve, outt_mm, b, c + 1)
                        wait(dve, gate_ok, b, c + 1)
                        nc.vector.tensor_tensor(gated_t[:, c, :], gate_t[:, c, :], bank[(1, 7)[c]][:], ALU.mult)\
                            .then_inc(gated_ok.h, 1)
                    wait(dve, out_mm, b)
                    wait(dve, xres_ok, b)
                    step(nc.vector.tensor_tensor(z[:], bank[0][:].rearrange("p (t d) -> p t d", t=T), xres[:],
                                                 ALU.add))
                    norm(lambda u: z[:, u, :], lambda u: x1[:, u, :], x1_ok)

                    wait(dve, logit_mm, b)
                    logits = bank[5][:, 0:T * E].rearrange("p (t e) -> p t e", t=T)
                    step(nc.vector.tensor_reduce(lmax[:], logits, X, ALU.max))
                    nc.vector.tensor_tensor(gate[:], logits, bc(lmax[:].unsqueeze(2), [P, T, E]), ALU.subtract)\
                        .then_inc(shift_ok.h, 1)
                    wait(dve, exp_ok, b)
                    step(nc.vector.tensor_reduce(lsum[:], gate[:], X, ALU.add))
                    step(nc.vector.reciprocal(lsum[:], lsum[:]))
                    step(nc.vector.tensor_tensor(gate[:], gate[:], bc(lsum[:].unsqueeze(2), [P, T, E]), ALU.mult), True)
                    for u in range(T):
                        ins = nc.vector.max(top[:, u, :], gate[:, u, :])
                    step(ins, True)
                    for u in range(T):
                        ins = nc.vector.max_index(topi[:, u, :], top[:, u, :], gate[:, u, :])
                    step(ins)
                    nc.vector.tensor_copy(topf[:], topi[:])
                    step(nc.vector.tensor_tensor(lsum[:], top[:, :, 0], top[:, :, 1], ALU.add))
                    step(nc.vector.tensor_scalar(lsum[:], lsum[:], 1e-9, None, ALU.add))
                    nc.vector.reciprocal(lsum[:], lsum[:])
                    iota = bc(v.iota_e[:].unsqueeze(1), [P, T, E])
                    for j, hit in ((0, hit0), (1, hit1)):
                        ins = nc.vector.tensor_tensor(hit[:], iota, bc(topf[:, :, j:j + 1], [P, T, E]), ALU.is_equal)
                    step(ins)
                    for j, hit in ((0, hit0), (1, hit1)):
                        ins = nc.vector.tensor_tensor(hit[:], hit[:], bc(top[:, :, j:j + 1], [P, T, E]), ALU.mult)
                    step(ins)
                    step(nc.vector.tensor_tensor(hit0[:], hit0[:], hit1[:], ALU.add))
                    step(nc.vector.tensor_tensor(wexp[:], hit0[:], bc(lsum[:].unsqueeze(2), [P, T, E]), ALU.mult), True)
                    for u in range(T):
                        wait(dve, y_mm, b, u + 1)
                        for e in range(E):
                            src = bank[(2, 6)[u % 2] + e // 4][:, P * (e % 4):P * (e % 4) + P]
                            ins = nc.vector.scalar_tensor_tensor(z2[:, u, :], src, wexp[:, u, e:e + 1],
                                                                 (z2 if e else x1)[:, u, :], ALU.mult, ALU.add)
                            if e < E - 1:
                                step(ins)
                        ins.then_inc(y_used.h, 1)
                    wait(dve, y_used, b)
                    norm(lambda u: z2[:, u, :], lambda u: x2[:, u, :], x2_ok)

                    for u in range(T):
                        wait(dve, qkv_mm, b, u + 1)
                        nc.vector.tensor_tensor(
                            pm[:].rearrange("p (i h) d -> p i h d", i=2),
                            bank[0][:, 0:2 * P].rearrange("p (i h d) -> p i h d", i=2, d=HD),
                            bc(v.map_bias[:].unsqueeze(2), [P, 2, HEADS, HD]), ALU.add).then_inc(pm_ok.h, 1)
                        wait(dve, pm_ok, b, u + 1)
                        nc.vector.tensor_reduce(pmax[:], pm[:], X, ALU.max)
                        step(nc.vector.tensor_reduce(pmin[:], pm[:], X, ALU.min))
                        nc.vector.tensor_tensor(pe_in[:, :, 0, :], pm[:], bc(pmax[:].unsqueeze(2), [P, 2 * HEADS, HD]),
                                                ALU.subtract)
                        nc.vector.tensor_tensor(pe_in[:, :, 1, :], bc(pmin[:].unsqueeze(2), [P, 2 * HEADS, HD]), pm[:],
                                                ALU.subtract).then_inc(spread_ok.h, 1)
                        wait(dve, fexp_ok, b, u + 1)
                        step(nc.vector.tensor_reduce(psum_[:], pe_in[:], X, ALU.add))
                        step(nc.vector.reciprocal(prec[:], psum_[:]))
                        if u:
                            if u < T:
                                wait(dve, st_mm, b, u)
                            wait(dve, ft_mm, b, u)
                        nc.vector.tensor_tensor(feat[:].rearrange("p i h (s f) -> p (i h) s f", s=4)[:, :, 0:2, :],
                                                pe_in[:], bc(prec[:].unsqueeze(3), [P, 2 * HEADS, 2, HD]), ALU.mult)\
                            .then_inc(feat_ok.h, 1)
                        if u < T - 1:
                            wait(dve, st_mm, b, u + 1)
                            fresh = bank[1][:, 144:288].rearrange("p (c g f) -> p c g f", c=QUADS, g=4)
                            keep = bc(v.same_quad[:].unsqueeze(1).unsqueeze(3), [P, QUADS, 4, VW])
                            if u == 0:
                                nc.vector.tensor_tensor(state[:, 1], fresh, keep, ALU.mult).then_inc(st_ok.h, 1)
                            else:
                                step(nc.vector.tensor_tensor(state_new[:], fresh, keep, ALU.mult))
                                nc.vector.tensor_tensor(state[:, (u + 1) % 2], state[:, u % 2], state_new[:], ALU.add)\
                                    .then_inc(st_ok.h, 1)
                        wait(dve, a_mm, b, u + 1)
                        for g in range(4):
                            ins = nc.vector.tensor_tensor(
                                amask[:].rearrange("p (c g) t -> p g c t", g=4)[:, g],
                                bank[4 + g][:].rearrange("p (c t) -> p c t", c=QUADS),
                                bc(v.causal[:].unsqueeze(1), [P, QUADS, P]), ALU.mult)
                        ins.then_inc(amask_ok.h, 1)
                        wait(dve, num_mm, b, u + 1)
                        nd = bank[1][:, 0:HEADS * VW].rearrange("p (h f) -> p h f", f=VW)
                        step(nc.vector.tensor_scalar(den[:], nd[:, :, HD], 1e-6, None, ALU.max))
                        step(nc.vector.reciprocal(den[:], den[:]))
                        nc.vector.tensor_tensor(y[:].rearrange("p (h d) -> p h d", d=HD), nd[:, :, 0:HD],
                                                bc(den[:].unsqueeze(2), [P, HEADS, HD]), ALU.mult)\
                            .then_inc(yv_ok.h, 1)
                        wait(dve, z3_mm, b, u + 1)
                        nc.vector.tensor_tensor(z3[:, u, :], x2[:, u, :], bank[0][:, 3 * P:4 * P], ALU.add)\
                            .then_inc(z3_ok.h, 1)
                    wait(dve, z3_ok, b)
                    wait_last(dve, x3_kept, b)
                    norm(lambda u: z3[:, u, :], lambda u: x3b[:, u, :], x3_ok)
                    wait_apart(dve, spare, x3t_ok, x3t_ok.at(b, 1))
                    nc.vector.bn_stats(v.bn_raw[:, bass.ds(b, 1), :].rearrange("p a s -> p (a s)"), bank[4][:])\
                        .then_inc(bn_ok.h, 1)
                assert own.seen == own.per, own.seen

            @block.tensor
            def _(pe):
                arrived(pe, "l0")
                arrived(pe, "moe")
                pe.wait_ge(v.dset.h, 6)
                with pe.Fori(0, B) as b:
                    wait_last(pe, z3_ok, b)
                    wait_last(pe, bn_ok, b)
                    for u in range(T):
                        wait(pe, xh_ok, b, u + 1)
                        ins = nc.tensor.transpose(bank[0][:, P * u:P * u + P], xh[:, u, :], ident[:])
                    ins.then_inc(xht_mm.h, 1)
                    wait(pe, normed_ok, b)
                    nc.tensor.matmul(bank[1][:], v.wqk[:], normed_t[:], start=True, stop=True).then_inc(qk_mm.h, 1)
                    for i in range(2):
                        for u in (2 * i, 2 * i + 1):
                            ins = nc.tensor.matmul(bank[4 + i][:, HID * (u % 2):HID * (u % 2) + HID],
                                                   normed_t[:, P * u:P * u + P], v.wh[:, 0:HID], start=True, stop=True)
                        ins.then_inc(val_mm.h, 1)
                    for c in range(EC):
                        nc.tensor.matmul(bank[2 + c][:], v.wh[:, HID + P * c:HID + P * c + P], normed_t[:],
                                         start=True, stop=True).then_inc(gate_mm.h, 1)
                    wait(pe, quad_ok, b)
                    for u in range(T):
                        q = slice(P * u, P * u + P)
                        ins = nc.tensor.matmul(bank[6][:, q], heads_t[:, 2, q], heads_t[:, 0, q], start=True, stop=True)
                    ins.then_inc(sim_mm.h, 1)
                    wait(pe, lin_ok, b)
                    for u in range(T):
                        q = slice(P * u, P * u + P)
                        ins = nc.tensor.transpose(bank[7][:, q], heads_t[:, 3, q], ident[:])
                    ins.then_inc(link_mm.h, 1)
                    wait(pe, link_ok, b)
                    wait(pe, val_ok, b)
                    for u in range(T):
                        ins = nc.tensor.matmul(bank[0][:, 0:HID], link[:, u, :], val[:, u, :],
                                               start=(u == 0), stop=(u == T - 1))
                    ins.then_inc(kv_mm.h, 1)
                    wait(pe, kv_ok, b)
                    wait(pe, attn_ok, b)
                    for c in range(EC):
                        o = bank[(1, 7)[c]]
                        for u in range(T):
                            nc.tensor.matmul(o[:, P * u:P * u + P], val[:, u, P * c:P * c + P], attn_t[:, u, :],
                                             start=(u == 0), stop=False, skip_group_check=True)
                        ins = nc.tensor.matmul(o[:], kv[:, P * c:P * c + P], heads_t[:, 1, :], start=False, stop=True,
                                               skip_group_check=True)
                        ins.then_inc(outt_mm.h, 1)
                    wait(pe, gated_ok, b)
                    for u in range(T):
                        for c in range(EC):
                            ins = nc.tensor.matmul(bank[0][:, P * u:P * u + P], gated_t[:, c, P * u:P * u + P],
                                                   v.wout0[:, c, :], start=(c == 0), stop=(c == EC - 1))
                    ins.then_inc(out_mm.h, 1)

                    for u in range(T):
                        wait(pe, x1_ok, b, u + 1)
                        ins = nc.tensor.transpose(bank[4][:, P * u:P * u + P], x1[:, u, :], ident[:])
                    ins.then_inc(x1t_mm.h, 1)
                    wait(pe, x1t_ok, b)
                    for u in range(T):
                        ins = nc.tensor.matmul(bank[5][:, E * u:E * u + E], x1t[:, P * u:P * u + P], v.wg[:],
                                               start=True, stop=True)
                    ins.then_inc(logit_mm.h, 1)
                    for u in range(T):
                        if u >= 2:
                            wait(pe, y_used, b, u - 1)
                        for k in range(2):
                            ins = nc.tensor.matmul(bank[(2, 6)[u % 2] + k][:], x1t[:, P * u:P * u + P],
                                                   v.we[:, 4 * k:4 * k + 4, :].rearrange("p e m -> p (e m)"),
                                                   start=True, stop=True)
                        ins.then_inc(y_mm.h, 1)

                    for u in range(T):
                        wait(pe, x2_ok, b, u + 1)
                        ins = nc.tensor.transpose(bank[4][:, P * u:P * u + P], x2[:, u, :], ident[:])
                    ins.then_inc(x2t_mm.h, 1)
                    wait(pe, x2t_ok, b)
                    for u in range(T):
                        if u:
                            wait(pe, z3_ok, b, u)
                        nc.tensor.matmul(bank[0][:, 0:3 * P], x2t[:, P * u:P * u + P], v.wcomb[:],
                                         start=True, stop=True).then_inc(qkv_mm.h, 1)
                        wait(pe, feat_ok, b, u + 1)
                        if u:
                            wait(pe, kft_ok, b, u)
                        for i in range(2):
                            for c in range(QUADS):
                                ins = nc.tensor.transpose(
                                    bank[2 + i][:, P * c:P * c + P],
                                    feat[:, i, 4 * c:4 * c + 4, :].rearrange("p h f -> p (h f)"), ident[:])
                        ins.then_inc(ft_mm.h, 1)
                        wait(pe, v_ok, b, u + 1)
                        if u < T - 1:
                            for c in range(QUADS):
                                ins = nc.tensor.matmul(bank[1][:, 144 + 36 * c:144 + 36 * c + 36],
                                                       feat[:, 1, 4 * c:4 * c + 4, :].rearrange("p h f -> p (h f)"),
                                                       vaug[:, 4 * c:4 * c + 4, :].rearrange("p h f -> p (h f)"),
                                                       start=True, stop=True)
                            ins.then_inc(st_mm.h, 1)
                        wait(pe, qft_ok, b, u + 1)
                        wait(pe, kft_ok, b, u + 1)
                        if u:
                            wait(pe, amask_ok, b, u)
                        for c in range(QUADS):
                            for g in range(4):
                                r = slice(32 * g, 32 * g + 32)
                                ins = nc.tensor.matmul(bank[4 + g][:, P * c:P * c + P], kf_t[r, c, :], qf_t[r, c, :],
                                                       start=True, stop=True)
                        ins.then_inc(a_mm.h, 1)
                        wait(pe, amask_ok, b, u + 1)
                        if u < T - 1:
                            wait(pe, st_ok, b, u + 1)
                        first = True
                        if u:
                            for c in range(QUADS):
                                nc.tensor.matmul(bank[1][:, 36 * c:36 * c + 36], qf_t[:, c, :],
                                                 state[:, u % 2, c].rearrange("p g f -> p (g f)"),
                                                 start=first, stop=False, skip_group_check=True)
                                first = False
                        for h in range(HEADS):
                            ins = nc.tensor.matmul(bank[1][:, VW * h:VW * h + VW], amask[:, h, :], vaug[:, h, :],
                                                   start=first, stop=True, skip_group_check=True)
                            first = False
                        ins.then_inc(num_mm.h, 1)
                        wait(pe, yv_ok, b, u + 1)
                        nc.tensor.transpose(bank[1][:, 288:288 + P], y[:], ident[:]).then_inc(yt_mm.h, 1)
                        wait(pe, yt_ok, b, u + 1)
                        nc.tensor.matmul(bank[0][:, 3 * P:4 * P], yt[:], v.wout1_t[:], start=True, stop=True)\
                            .then_inc(z3_mm.h, 1)
                    for u in range(T):
                        wait(pe, x3_ok, b, u + 1)
                        ins = nc.tensor.transpose(
                            bank[4][:, P * u:P * u + P], x3b[:, u, :], ident[:])
                    ins.then_inc(x3t_mm.h, 1)


OWN_LAYERS = 84
OWN_PEER = 37


def peer_loop(nc, v):
    B, N, T, NH, NK, K, SETS, EH, PAIRS = v.B, v.N, v.T, v.NH, v.NK, v.K, v.SETS, v.EH, v.PAIRS
    bank, ident, bc, arrived = v.bank, v.ident, v.bc, v.arrived
    HK = NH * K
    LB = 512 // (2 * EH)
    QB = P // LB
    ctx = ExitStack()
    with ctx:
        def sb(name, shape, dt=F32):
            return ctx.enter_context(nc.sbuf_tensor(name, shape, dt))

        primed = []

        def sem(name, per=1, start=0):
            s = Sem(ctx.enter_context(nc.semaphore(name)), per, start)
            if start:
                primed.append(s)
            return s

        xn = sb("xn", [P, N])
        keysims = sb("keysims", [P, T, SETS, NK])
        side, side_i = sb("side", [P, T, SETS, K]), sb("side_i", [P, T, SETS, K], U32)
        cand = sb("cand", [P, 2, NH, K, K])
        best, best_i = sb("best", [P, T, NH, K]), sb("best_i", [P, NH, K], U32)
        rc = sb("rc", [P, 2, HK], U32)
        eq = sb("eq", [P, SETS, K, K])
        dec = sb("dec", [P, SETS, K])
        e_num, lohi = sb("e_num", [P, HK], U32), sb("lohi", [P, T, 2, HK], U32)
        comp = sb("comp", [P, PAIRS, 3, 2, HK])
        lh_t = sb("lh_t", [P, 2, P], F16)
        w_t = sb("w_t", [P, P])
        w_hi, w_lo = sb("w_hi", [P, P], F16), sb("w_lo", [P, P], F16)
        hot_lo = sb("hot_lo", [P, P, P], F16)
        hot_hi = sb("hot_hi", [P, EH, P], F16)
        hot_w = sb("hot_w", [P, 2, 2, EH, P], F16)
        hid = sb("hid", [P, T, EH, P])
        mix = sb("mix", [P, 2 * EH, P])
        z4, o4 = sb("z4", [P, T, P]), sb("o4", [P, T, P])
        stats, mv, rstd = sb("stats4", [P, T, 6]), sb("mv4", [P, T, 2]), sb("rstd4", [P, T, 1])
        bn_inv = sb("bn_inv", [P, 1])

        bn_var, bn_pow, bn_done = sem("bn_var"), sem("bn_pow"), sem("bn_done")
        zeroed = sem("zeroed")
        xn_ok, xn_sub = sem("xn_ok", 1), sem("xn_sub", 1)
        ksim_mm, ksim_ok = sem("ksim_mm", T, 1), sem("ksim_ok", T)
        h_mm, h_ok = sem("h_mm", EH, 1), sem("h_ok", EH)
        side_ok, cand_ok, best_ok = sem("side_ok", T, 1), sem("cand_ok", T), sem("best_ok", T)
        lohi_ok, sig_ok, comp_ok = sem("lohi_ok", T), sem("sig_ok", T), sem("comp_ok", T)
        comp_mm, comp_t_ok = sem("comp_mm", PAIRS, 1), sem("comp_t_ok", PAIRS)
        hot_ok, g_mm, mix_ok = sem("hot_ok", PAIRS), sem("g_mm", PAIRS * QB, 1), sem("mix_ok", PAIRS * QB, 1)
        out_mm, z4_ok, o4_ok, stored = sem("out4_mm", T, 1), sem("z4_ok", T, 1), sem("o4_ok", T), sem("stored", 16, 1)
        var_ok, rstd_ok = sem("var4_ok", 1), sem("rstd4_ok", 1)
        spare = sem("spare4").h
        own = sem("dve_own4", OWN_PEER)

        with nc.Block() as block:
            @block.sync
            def _(sp):
                with sp.Fori(0, B) as b:
                    wait(sp, o4_ok, b)
                    sp.dma_start(v.out[bass.ds(b, 1), :, :].rearrange("a (t p) d -> p (a t) d", p=P), o4[:])\
                        .then_inc(stored.h, 16)
                sp.wait_ge(stored.h, stored.start + 16 * B)

            @block.gpsimd
            def _(pool):
                for s in primed:
                    pool.sem_inc(s.h, 1)
                nc.gpsimd.memset(hot_w[:], 0.0).then_inc(zeroed.h, 1)
                pool.wait_ge(bn_var.h, 1)
                nc.gpsimd.tensor_tensor(bn_inv[:], bn_inv[:], v.minus_half[:], ALU.pow).then_inc(bn_pow.h, 1)
                with pool.Fori(0, B) as b:
                    for u in range(T):
                        wait(pool, side_ok, b, u + 1)
                        if u >= 2:
                            wait(pool, best_ok, b, u - 1)
                        nc.gpsimd.tensor_tensor(
                            cand[:, u % 2], bc(side[:, u, 0:NH, :].unsqueeze(3), [P, NH, K, K]),
                            bc(side[:, u, NH:SETS, :].unsqueeze(2), [P, NH, K, K]), ALU.add).then_inc(cand_ok.h, 1)
                    wait(pool, var_ok, b)
                    nc.gpsimd.tensor_tensor(rstd[:], rstd[:], bc(v.minus_half[:].unsqueeze(1), [P, T, 1]), ALU.pow)\
                        .then_inc(rstd_ok.h, 1)

            @block.scalar
            def _(act):
                with act.Fori(0, B) as b:
                    for u in range(T):
                        wait(act, ksim_mm, b, u + 1)
                        wait_last(act, side_ok, b)
                        nc.scalar.copy(keysims[:, u].rearrange("p s k -> p (s k)"), bank[0][:]).then_inc(ksim_ok.h, 1)
                    wait_last(act, mix_ok, b)
                    for c in range(EH):
                        wait(act, h_mm, b, c + 1)
                        nc.scalar.activation(hid[:, :, c, :], bank[6 + c % 2][:].rearrange("p (t l) -> p t l", t=T),
                                             ACT.Gelu).then_inc(h_ok.h, 1)
                    wait_last(act, comp_mm, b)
                    for u in range(T):
                        wait(act, best_ok, b, u + 1)
                        nc.scalar.activation(comp[:, u // 2, 2, u % 2, :],
                                             best[:, u].rearrange("p h k -> p (h k)"), ACT.Sigmoid)\
                            .then_inc(sig_ok.h, 1)
                        wait(act, lohi_ok, b, u + 1)
                        nc.scalar.copy(comp[:, u // 2, 0:2, u % 2, :], lohi[:, u]).then_inc(comp_ok.h, 1)
                        if u % 2:
                            p = u // 2
                            wait(act, comp_mm, b, p + 1)
                            if p:
                                wait(act, hot_ok, b, p)
                            nc.scalar.copy(w_t[:], bank[1][:, 2 * P:3 * P])
                            nc.scalar.copy(lh_t[:].rearrange("p i l -> p (i l)"), bank[1][:, 0:2 * P])\
                                .then_inc(comp_t_ok.h, 1)

            @block.vector
            def _(dve):
                def step(ins, plain=False):
                    ins.then_inc(own.h, 1)
                    own.seen += 1
                    if plain:
                        wait_apart(dve, spare, own, own.at(bb, own.seen))
                    else:
                        dve.wait_ge(own.h, own.at(bb, own.seen))

                arrived(dve, "bn")
                nc.vector.bn_aggr(v.bn_mv[:], v.bn_raw[:].rearrange("p b s -> p (b s)")).then_inc(bn_done.h, 1)
                dve.wait_ge(bn_done.h, 1)
                nc.vector.tensor_scalar(bn_inv[:], v.bn_mv[:, 1:2], EPS, None, ALU.add).then_inc(bn_var.h, 1)
                dve.wait_ge(bn_pow.h, 1)
                nc.vector.tensor_tensor(v.bn_scale[:], bn_inv[:], v.bn_g[:], ALU.mult).then_inc(bn_done.h, 1)
                dve.wait_ge(bn_done.h, 2)
                dve.wait_ge(zeroed.h, 1)
                with dve.Fori(0, B) as b:
                    bb = b
                    own.seen = var_ok.seen = 0

                    def first_choice(u):
                        wait_apart(dve, spare, ksim_ok, ksim_ok.at(b, u + 1))
                        for s in range(SETS):
                            ins = nc.vector.max(side[:, u, s, :], keysims[:, u, s, :])
                        step(ins, True)
                        for s in range(SETS):
                            ins = nc.vector.max_index(side_i[:, u, s, :], side[:, u, s, :], keysims[:, u, s, :])
                        ins.then_inc(side_ok.h, 1)

                    def second_choice(u):
                        wait_apart(dve, spare, cand_ok, cand_ok.at(b, u + 1))
                        for h in range(NH):
                            ins = nc.vector.max(best[:, u, h, :], cand[:, u % 2, h].rearrange("p r c -> p (r c)"))
                        step(ins, True)
                        for h in range(NH):
                            ins = nc.vector.max_index(best_i[:, h, :], best[:, u, h, :],
                                                      cand[:, u % 2, h].rearrange("p r c -> p (r c)"))
                        ins.then_inc(best_ok.h, 1)
                        wait(dve, best_ok, b, u + 1)
                        flat = best_i[:].rearrange("p h k -> p (h k)")
                        nc.vector.tensor_scalar(rc[:, 0, :], flat, 3, None, ALU.logical_shift_right)
                        step(nc.vector.tensor_scalar(rc[:, 1, :], flat, K - 1, None, ALU.bitwise_and))
                        step(nc.vector.tensor_tensor(
                            eq[:], bc(rc[:].rearrange("p s (h k) -> p (s h) k", k=K).unsqueeze(3), [P, SETS, K, K]),
                            bc(v.iota_k[:].unsqueeze(1).unsqueeze(1), [P, SETS, K, K]), ALU.is_equal))
                        step(nc.vector.tensor_tensor(
                            eq[:], eq[:], bc(side_i[:, u].unsqueeze(2), [P, SETS, K, K]), ALU.mult))
                        step(nc.vector.tensor_reduce(dec[:], eq[:], X, ALU.add))
                        step(nc.vector.scalar_tensor_tensor(
                            e_num[:], dec[:, 0:NH, :].rearrange("p h k -> p (h k)"), float(NK),
                            dec[:, NH:SETS, :].rearrange("p h k -> p (h k)"), ALU.mult, ALU.add))
                        nc.vector.tensor_scalar(lohi[:, u, 0, :], e_num[:], P - 1, None, ALU.bitwise_and)
                        nc.vector.tensor_scalar(lohi[:, u, 1, :], e_num[:], 7, None, ALU.logical_shift_right)\
                            .then_inc(lohi_ok.h, 1)

                    def one_hots(p):
                        wait(dve, comp_t_ok, b, p + 1)
                        if p:
                            wait(dve, g_mm, b, QB * p)
                        else:
                            wait_last(dve, g_mm, b)
                        nc.vector.tensor_scalar(w_hi[:], w_t[:], WEIGHT_SCALE, None, ALU.mult)
                        nc.vector.tensor_tensor(hot_lo[:], bc(lh_t[:, 0:1, :], [P, P, P]), v.iota_lo[:], ALU.is_equal)
                        step(nc.vector.tensor_tensor(hot_hi[:], bc(lh_t[:, 1:2, :], [P, EH, P]), v.iota_hi[:],
                                                     ALU.is_equal))
                        step(nc.vector.scalar_tensor_tensor(w_lo[:], w_t[:], WEIGHT_SCALE, w_hi[:], ALU.mult,
                                                            ALU.subtract))
                        for t in range(2):
                            q = slice(HK * t, HK * t + HK)
                            for i, w in enumerate((w_hi, w_lo)):
                                ins = nc.vector.tensor_tensor(hot_w[q, i, t], hot_hi[q],
                                                              bc(w[q].unsqueeze(1), [HK, EH, P]), ALU.mult)
                        ins.then_inc(hot_ok.h, 1)

                    def weigh(p):
                        for q in range(QB):
                            wait(dve, g_mm, b, QB * p + q + 1)
                            if p == 0 and q == 0:
                                wait(dve, h_ok, b)
                                wait_last(dve, out_mm, b)
                            elif q == 0:
                                wait(dve, out_mm, b, 2 * p)
                            lanes = slice(LB * q, LB * q + LB)
                            nc.vector.scalar_tensor_tensor(
                                mix[:, :, lanes].rearrange("p e l -> p l e"),
                                bank[2 + q][:].rearrange("p (l e) -> p l e", e=2 * EH), 1.0 / WEIGHT_SCALE,
                                hid[:, 2 * p:2 * p + 2, :, lanes].rearrange("p t e l -> p l (t e)"),
                                ALU.mult, ALU.mult).then_inc(mix_ok.h, 1)

                    def residual(p):
                        wait(dve, out_mm, b, 2 * p + 2)
                        for u in (2 * p, 2 * p + 1):
                            nc.vector.tensor_tensor(z4[:, u, :], bank[p][:, P * (u % 2):P * (u % 2) + P],
                                                    v.x3[:, bass.ds(b * T + u, 1), :].rearrange("p a d -> p (a d)"),
                                                    ALU.add).then_inc(z4_ok.h, 1)

                    wait_last(dve, h_mm, b)
                    wait_last(dve, ksim_mm, b)
                    nc.vector.tensor_scalar(xn[:], v.x3t[:, bass.ds(b * N, N)], v.bn_mv[:, 0:1], v.bn_scale[:],
                                            ALU.subtract, ALU.mult).then_inc(xn_sub.h, 1)
                    wait(dve, xn_sub, b)
                    nc.vector.tensor_scalar(xn[:], xn[:], v.bn_b[:], None, ALU.add).then_inc(xn_ok.h, 1)
                    for u in (0, 1):
                        first_choice(u)
                    for u in (0, 1):
                        second_choice(u)
                    one_hots(0)
                    for u in (2, 3):
                        first_choice(u)
                    for u in (2, 3):
                        second_choice(u)
                    weigh(0)
                    one_hots(1)
                    weigh(1)
                    residual(0)
                    residual(1)
                    wait(dve, z4_ok, b)
                    dve.wait_ge(stored.h, b * 16 + stored.start)
                    layer_norm(nc, dve, spare, b, own, stats, mv, rstd, lambda u: z4[:, u, :], lambda u: o4[:, u, :],
                               T, var_ok, rstd_ok, o4_ok)
                assert own.seen == own.per, own.seen

            @block.tensor
            def _(pe):
                arrived(pe, "peer")
                with pe.Fori(0, B) as b:
                    wait(pe, xn_ok, b)
                    wait_last(pe, z4_ok, b)
                    for u in range(T):
                        if u:
                            wait(pe, ksim_ok, b, u)
                        nc.tensor.matmul(bank[0][:], xn[:, P * u:P * u + P],
                                         v.keysim[:].rearrange("p s k -> p (s k)"), start=True, stop=True)\
                            .then_inc(ksim_mm.h, 1)
                    for c in range(EH):
                        if c >= 2:
                            wait(pe, h_ok, b, c - 1)
                        nc.tensor.matmul(bank[6 + c % 2][:], v.down_t[:, c, :], v.x3t[:, bass.ds(b * N, N)],
                                         start=True, stop=True).then_inc(h_mm.h, 1)
                    for p in range(PAIRS):
                        wait(pe, comp_ok, b, 2 * p + 2)
                        for i in range(3):
                            ins = nc.tensor.transpose(bank[1][:, P * i:P * i + P],
                                                      comp[:, p, i].rearrange("p t k -> p (t k)"), ident[:])
                        ins.then_inc(comp_mm.h, 1)
                        wait(pe, hot_ok, b, p + 1)
                        for q in range(QB):
                            if p:
                                wait(pe, mix_ok, b, q + 1)
                            for lane in range(LB * q, LB * q + LB):
                                for i in range(2):
                                    c = 2 * EH * (lane % LB)
                                    ins = nc.tensor.matmul(
                                        bank[2 + q][:, c:c + 2 * EH], hot_lo[:, :, lane],
                                        hot_w[:, i, :, :, lane].rearrange("p t e -> p (t e)"),
                                        start=(i == 0), stop=(i == 1))
                            ins.then_inc(g_mm.h, 1)
                        wait(pe, mix_ok, b, QB * p + QB)
                        for t in range(2):
                            u = 2 * p + t
                            for e in range(EH):
                                ins = nc.tensor.matmul(bank[p][:, P * t:P * t + P], mix[:, EH * t + e, :],
                                                       v.upw[:, e, :], start=(e == 0), stop=(e == EH - 1))
                            ins.then_inc(out_mm.h, 1)


_INS = ["L0_attn_x", "L0_attn_ln_g", "L0_attn_ln_b", "L0_attn_W_h", "L0_attn_b_h", "L0_attn_W_qk", "L0_attn_b_qk",
        "L0_attn_os_gamma", "L0_attn_os_beta", "L0_attn_rel_emb", "L0_attn_W_out", "L0_attn_b_out", "L0_ffn_Wg",
        "L0_ffn_We", "L1_attn_w_qkv", "L1_attn_wq_map", "L1_attn_bq_map", "L1_attn_wk_map", "L1_attn_bk_map",
        "L1_attn_w_out", "L1_ffn_bn_gamma", "L1_ffn_bn_beta", "L1_ffn_w_q", "L1_ffn_keys_p", "L1_ffn_down",
        "L1_ffn_up"]


def kernel(**inputs):
    import numpy as _np
    import concourse.bacc as _bacc
    from concourse.bass_utils import run_bass_kernel_spmd as _run

    nc = _bacc.Bacc("TRN2", target_bir_lowering=False, num_devices=1)
    arrays, args = {}, []
    for name in _INS:
        a = _np.ascontiguousarray(inputs[name])
        arrays[f"in_{name}"] = a
        args.append(nc.dram_tensor(f"in_{name}", a.shape, mybir.dt.from_np(a.dtype), kind="ExternalInput").ap())
    shape = inputs["L0_attn_x"].shape
    args.append(nc.dram_tensor("out_0", shape, F32, kind="ExternalOutput").ap())
    build(nc, *args)
    r = _run(nc, [arrays], core_ids=[0])
    return r.results[0]["out_0"]
```

```python
from contextlib import ExitStack

import numpy as np
import concourse.bass as bass
from concourse import mybir

ALU = mybir.AluOpType
ACT = mybir.ActivationFunctionType
X = mybir.AxisListType.X
F32 = mybir.dt.float32
F16 = mybir.dt.float16
U32 = mybir.dt.uint32

P = 128
EPS = 1e-5
MASKED = -1e30
WEIGHT_SCALE = 4096.0


class Sem:

    def __init__(self, handle, per=1, start=0):
        self.h, self.per, self.start, self.seen = handle, per, start, 0

    def at(self, b, k):
        return b * self.per + (k + self.start)


def wait(eng, s, b, k=None):
    eng.wait_ge(s.h, s.at(b, s.per if k is None else k))


def wait_last(eng, s, b):
    assert s.start
    eng.wait_ge(s.h, s.at(b, 0))


class Shared:
    pass


def bucket_of(rel, buckets=32, max_dist=128):
    nb = buckets // 2
    n, exact = abs(rel), nb // 2
    if n < exact:
        return n + (nb if rel < 0 else 0)
    large = np.log(np.float32(n) / np.float32(exact)) / np.float32(np.log(max_dist / exact)) * np.float32(nb - exact)
    return min(exact + int(large), nb - 1) + (nb if rel < 0 else 0)


def bucket_runs(group):
    row = [bucket_of(m - (group - 1)) for m in range(2 * group - 1)]
    runs, i = [], 0
    while i < len(row):
        j = i + 1
        step = row[j] - row[i] if j < len(row) and row[j] - row[i] in (0, 1) else 0
        while j < len(row) and row[j] - row[j - 1] == step:
            j += 1
        runs.append((i, j - i, row[i], step))
        i = j
    return runs


def build(nc, x, ln_g, ln_b, W_h, b_h, W_qk, b_qk, os_gamma, os_beta, rel_emb, W_out, b_out, Wg, We,
          w_qkv, wq_map, bq_map, wk_map, bk_map, w_out, bn_gamma, bn_beta, w_q, keys_p, down, up, out):
    B, N, D = x.shape
    HID = W_h.shape[1] // 2
    EC = HID // P
    GROUP = 32
    T = N // P
    E = Wg.shape[1]
    HEADS, HD = D // wq_map.shape[0], wq_map.shape[0]
    QUADS = HEADS // 4
    NH, NK, _, KD = keys_p.shape
    K = 8
    SETS = 2 * NH
    EH = NK * NK // P
    PAIRS = T // 2

    ctx = ExitStack()
    with ctx:
        def sb(name, shape, dt=F32):
            return ctx.enter_context(nc.sbuf_tensor(name, shape, dt))

        def sem(name, per=1):
            s = Sem(ctx.enter_context(nc.semaphore(name)), per)
            return s

        psum = ctx.enter_context(nc.psum_tensor("psum", [P, 8, 512], F32))
        bank = [psum[:, i, :] for i in range(8)]

        ident = sb("ident", [P, P])
        flip = sb("flip", [GROUP, P])
        spread = sb("spread", [HD, P])
        causal = sb("causal", [P, P])
        same8 = sb("same8", [P, HEADS, HD])
        minus_half = sb("minus_half", [P, 1])
        same_quad = sb("same_quad", [P, 4])
        iota_e = sb("iota_e", [P, E])
        iota_k = sb("iota_k", [P, K])
        iota_lo = sb("iota_lo", [P, P, P], F16)
        iota_hi = sb("iota_hi", [P, EH, P], F16)
        g_col, b_col = sb("g_col", [P, 1]), sb("b_col", [P, 1])
        wh, bh_gate, bh_v = sb("wh", [P, 2 * HID]), sb("bh_gate", [P, EC]), sb("bh_v", [P, HID])
        wqk, bqk_col = sb("wqk", [P, P]), sb("bqk_col", [P, 1])
        gam, bet = sb("gam", [P, 4]), sb("bet", [P, 4])
        hankel, bias_t, bias_raw = sb("hankel", [GROUP, GROUP]), sb("bias_t", [P, P]), sb("bias_raw", [P, GROUP])
        wout0, bout = sb("wout0", [P, EC, P]), sb("bout", [P, P])
        wg, we = sb("wg", [P, E]), sb("we", [P, E, P])
        wqkv = sb("wqkv", [P, 3, P])
        maps_t, maps_bd = sb("maps_t", [HD, 2, HD]), sb("maps_bd", [P, 2, HEADS, HD])
        map_bias = sb("map_bias", [P, 2, HD])
        map_bias_all = sb("map_bias_all", [P, 2, HEADS, HD])
        wcomb = sb("wcomb", [P, 3 * P])
        wout1, wout1_t = sb("wout1", [P, P]), sb("wout1_t", [P, P])
        bn_g, bn_b = sb("bn_g", [P, 1]), sb("bn_b", [P, 1])
        upw, down_t = sb("upw", [P, EH, P]), sb("down_t", [P, EH, P])
        keysim = sb("keysim", [P, SETS, NK])
        x3t = sb("x3t", [P, B * N])
        x3 = sb("x3", [P, B * T, P])
        bn_raw = sb("bn_raw", [P, B, 6])
        bn_mv, bn_scale = sb("bn_mv", [P, 2]), sb("bn_scale", [P, 1])
        xall = sb("xall", [P, B * T, P])
        rel_row = nc.dram_tensor("rel_row", [2 * GROUP], F32, kind="Internal").ap()

        loaded = {n: sem("ld_" + n) for n in ("l0", "moe", "l1", "bn", "rel", "hankel", "peer", "keys")}
        x_in = sem("x_in", 16)
        consts, consts_lo = sem("consts"), sem("consts_lo")
        dset = sem("dve_setup")
        setup_mm, setup_cp = sem("setup_mm"), sem("setup_cp")

        load_count = {}

        def load(eng, group, dst, src):
            load_count[group] = load_count.get(group, 0) + 1
            eng.dma_start(dst, src, allow_slow_non_contiguous=True).then_inc(loaded[group].h, 16)

        def arrived(eng, group):
            eng.wait_ge(loaded[group].h, 16 * load_count[group])

        def col(v):
            return v.rearrange("(p a) -> p a", a=1)

        def rows(v, n=P):
            return bass.AP(v.tensor, v.offset, [[0, n]] + [list(s) for s in v.ap])

        def bc(ap, shape):
            return ap.broadcast_to(shape)

        setup_sb = ExitStack()
        wqn = setup_sb.enter_context(nc.sbuf_tensor("wqn", [P, SETS, P], F32))
        keysn = setup_sb.enter_context(nc.sbuf_tensor("keysn", [P, 2, 2, KD], F32))
        keys_t = setup_sb.enter_context(nc.sbuf_tensor("keys_t", [P, 2, 2, P], F32))
        downn = setup_sb.enter_context(nc.sbuf_tensor("downn", [P, EH, P], F32))
        iota_u = setup_sb.enter_context(nc.sbuf_tensor("iota_u", [P, P], F32))

        with nc.Block() as block:
            @block.sync
            def _(sp):
                for pos, n, first, step in bucket_runs(GROUP):
                    dst = rel_row[pos:pos + n]
                    src = bass.AP(rel_emb.tensor, rel_emb.offset + first, [[step, n], [1, 1]])
                    load(sp, "rel", dst.rearrange("(n a) -> n a", a=1), src)
                for b in range(B):
                    sp.dma_start(xall[:, T * b:T * b + T, :], x[b].rearrange("(t p) d -> p t d", p=P))\
                        .then_inc(x_in.h, 16)
                arrived(sp, "rel")
                load(sp, "hankel", hankel[:], bass.AP(rel_row.tensor, rel_row.offset, [[1, GROUP], [1, GROUP]]))
                load(sp, "l0", g_col[:], col(ln_g))
                load(sp, "l0", b_col[:], col(ln_b))
                load(sp, "l0", wqk[:], W_qk)
                load(sp, "l0", wh[:], W_h)
                load(sp, "l0", bqk_col[:], col(b_qk))
                load(sp, "l0", bh_gate[:], b_h[HID:2 * HID].rearrange("(c p) -> p c", p=P))
                load(sp, "l0", bh_v[:], rows(b_h[0:HID]))
                load(sp, "l0", gam[:], os_gamma.rearrange("h p -> p h"))
                load(sp, "l0", bet[:], os_beta.rearrange("h p -> p h"))
                load(sp, "l0", wout0[:], W_out.rearrange("(c p) n -> p c n", p=P))
                load(sp, "l0", bout[:], rows(b_out))
                load(sp, "moe", wg[:], Wg)
                load(sp, "moe", we[:], We.rearrange("e d m -> d e m"))

            @block.scalar
            def _(act):
                load(act, "l1", wqkv[:], w_qkv.rearrange("(i p) d -> p i d", p=P))
                for i, (w, bias) in enumerate(((wq_map, bq_map), (wk_map, bk_map))):
                    load(act, "l1", maps_t[:, i, :], w.rearrange("e d -> d e"))
                    load(act, "l1", map_bias[:, i, :], rows(bias))
                load(act, "l1", wout1[:], w_out)
                load(act, "keys", wqn[:], w_q.rearrange("(s p) d -> p s d", p=P))
                load(act, "keys", keysn[:].rearrange("p a s k -> p a (s k)"),
                     keys_p.rearrange("(a h) k s d -> (h k) a (s d)", a=2))
                load(act, "keys", downn[:], down[0:NK * NK, :].rearrange("(c p) d -> p c d", p=P))
                load(act, "peer", upw[:], up[0:NK * NK, :].rearrange("(c p) d -> p c d", p=P))
                load(act, "bn", bn_g[:], col(bn_gamma))
                load(act, "bn", bn_b[:], col(bn_beta))
                act.wait_ge(consts.h, 1)
                nc.scalar.copy(iota_lo[:], bc(iota_u[:, :].unsqueeze(2), [P, P, P])).then_inc(consts_lo.h, 1)
                act.wait_ge(consts_lo.h, 1)

            @block.gpsimd
            def _(pool):
                nc.gpsimd.memset(ident[:], 0.0)
                nc.gpsimd.memset(minus_half[:], -0.5)
                nc.gpsimd.memset(flip[:], 0.0)
                nc.gpsimd.memset(spread[:], 0.0)
                nc.gpsimd.memset(causal[:], 1.0)
                nc.gpsimd.memset(same8[:], 1.0)
                nc.gpsimd.memset(same_quad[:], 1.0)
                nc.gpsimd.iota(iota_u[:], pattern=[[1, P]], base=0, channel_multiplier=0,
                               allow_small_or_imprecise_dtypes=True).then_inc(consts.h, 1)
                pool.wait_ge(consts.h, 1)
                nc.gpsimd.affine_select(ident[:], ident[:], pattern=[[-1, P]], compare_op=ALU.not_equal, fill=1.0,
                                        base=0, channel_multiplier=1)
                nc.gpsimd.affine_select(flip[:].rearrange("p (g j) -> p g j", j=GROUP),
                                        flip[:].rearrange("p (g j) -> p g j", j=GROUP),
                                        pattern=[[0, P // GROUP], [1, GROUP]], compare_op=ALU.not_equal, fill=1.0,
                                        base=1 - GROUP, channel_multiplier=1)
                nc.gpsimd.affine_select(spread[:].rearrange("p (h d) -> p h d", d=HD),
                                        spread[:].rearrange("p (h d) -> p h d", d=HD),
                                        pattern=[[0, HEADS], [-1, HD]], compare_op=ALU.not_equal, fill=1.0,
                                        base=0, channel_multiplier=1)
                nc.gpsimd.affine_select(causal[:], causal[:], pattern=[[1, P]], compare_op=ALU.is_ge, fill=0.0,
                                        base=0, channel_multiplier=-1)
                nc.gpsimd.affine_select(same8[:], same8[:], pattern=[[-HD, HEADS], [0, HD]], compare_op=ALU.is_ge,
                                        fill=0.0, base=0, channel_multiplier=1)
                nc.gpsimd.affine_select(same_quad[:], same_quad[:], pattern=[[-32, 4]], compare_op=ALU.is_ge,
                                        fill=0.0, base=0, channel_multiplier=1).then_inc(consts.h, 1)
                pool.wait_ge(consts.h, 2)
                nc.gpsimd.affine_select(same8[:], same8[:], pattern=[[HD, HEADS], [0, HD]], compare_op=ALU.is_ge,
                                        fill=0.0, base=HD - 1, channel_multiplier=-1)
                nc.gpsimd.affine_select(same_quad[:], same_quad[:], pattern=[[32, 4]], compare_op=ALU.is_ge,
                                        fill=0.0, base=31, channel_multiplier=-1).then_inc(consts.h, 1)

            @block.vector
            def _(dve):
                nc.vector.memset(bias_t[:], MASKED).then_inc(dset.h, 1)
                dve.wait_ge(dset.h, 1)
                dve.wait_ge(consts.h, 1)
                nc.vector.tensor_copy(iota_e[:], iota_u[:, 0:E])
                nc.vector.tensor_copy(iota_k[:], iota_u[:, 0:K])
                nc.vector.tensor_copy(iota_hi[:], bc(iota_u[:, 0:EH].unsqueeze(2), [P, EH, P])).then_inc(dset.h, 1)
                dve.wait_ge(consts.h, 3)
                dve.wait_ge(setup_mm.h, 1)
                arrived(dve, "l1")
                nc.vector.tensor_copy(map_bias_all[:], bc(map_bias[:].unsqueeze(2), [P, 2, HEADS, HD]))
                for i in range(2):
                    nc.vector.tensor_tensor(maps_bd[:, i], same8[:],
                                            bc(bank[0][:, HD * i:HD * i + HD].unsqueeze(1), [P, HEADS, HD]),
                                            ALU.mult).then_inc(dset.h, 1)
                dve.wait_ge(setup_mm.h, 2)
                nc.vector.tensor_copy(wcomb[:], bank[2][:, 0:3 * P])
                nc.vector.tensor_copy(wout1_t[:], bank[2][:, 3 * P:4 * P])
                dve.wait_ge(setup_mm.h, 3)
                nc.vector.tensor_copy(keys_t[:].rearrange("p a s k -> p (a s k)"), bank[3][:]).then_inc(dset.h, 1)
                dve.wait_ge(setup_mm.h, 4)
                for c in range(2):
                    nc.vector.tensor_copy(down_t[:, 4 * c:4 * c + 4, :].rearrange("p c k -> p (c k)"), bank[4 + c][:])
                dve.wait_ge(setup_mm.h, 5)
                for g in range(P // GROUP):
                    q = slice(GROUP * g, GROUP * g + GROUP)
                    nc.vector.tensor_scalar(bias_t[q, q], bank[1][q, 0:GROUP], float(P ** 0.5), None,
                                            ALU.mult)
                dve.wait_ge(setup_mm.h, 6)
                nc.vector.tensor_copy(keysim[:].rearrange("p s k -> p (s k)"), bank[6][:]).then_inc(dset.h, 1)

            @block.tensor
            def _(pe):
                pe.wait_ge(consts.h, 3)
                arrived(pe, "l1")
                for i in range(2):
                    mm = nc.tensor.matmul(bank[0][:, HD * i:HD * i + HD], spread[:], maps_t[:, i, :],
                                          start=True, stop=True)
                mm.then_inc(setup_mm.h, 1)
                pe.wait_ge(dset.h, 4)
                for i in range(2):
                    nc.tensor.matmul(bank[2][:, P * i:P * i + P], wqkv[:, i, :],
                                     maps_bd[:, i].rearrange("p h e -> p (h e)"), start=True, stop=True)
                nc.tensor.transpose(bank[2][:, 2 * P:3 * P], wqkv[:, 2, :], ident[:])
                nc.tensor.transpose(bank[2][:, 3 * P:4 * P], wout1[:], ident[:]).then_inc(setup_mm.h, 1)
                arrived(pe, "keys")
                for a in range(2):
                    for s in range(2):
                        mm = nc.tensor.transpose(bank[3][:, P * (2 * a + s):P * (2 * a + s) + P], keysn[:, a, s, :],
                                                 ident[:])
                mm.then_inc(setup_mm.h, 1)
                for c in range(EH):
                    mm = nc.tensor.transpose(bank[4 + c // 4][:, P * (c % 4):P * (c % 4) + P], downn[:, c, :], ident[:])
                mm.then_inc(setup_mm.h, 1)
                arrived(pe, "hankel")
                nc.tensor.matmul(bank[1][:, 0:GROUP], flip[:], hankel[:], start=True, stop=True).then_inc(setup_mm.h, 1)
                pe.wait_ge(dset.h, 5)
                for s in range(2):
                    for h in range(NH):
                        r = s * NH + h
                        mm = nc.tensor.matmul(bank[6][:, NK * r:NK * r + NK], wqn[:, r, :],
                                              keys_t[:, h // 4, s, NK * (h % 4):NK * (h % 4) + NK],
                                              start=True, stop=True)
                mm.then_inc(setup_mm.h, 1)
        setup_sb.close()

        shared = Shared()
        shared.B, shared.D, shared.E, shared.EC, shared.EH, shared.GROUP = B, D, E, EC, EH, GROUP
        shared.HD, shared.HEADS, shared.HID, shared.K, shared.N, shared.NH = HD, HEADS, HID, K, N, NH
        shared.NK, shared.PAIRS, shared.QUADS, shared.SETS, shared.T, shared.arrived = NK, PAIRS, QUADS, SETS, T, arrived
        shared.b_col, shared.bank, shared.bc, shared.bet, shared.bh_gate, shared.bh_v = b_col, bank, bc, bet, bh_gate, bh_v
        shared.bias_t, shared.bn_b, shared.bn_g, shared.bn_mv, shared.bn_raw, shared.bn_scale = bias_t, bn_b, bn_g, bn_mv, bn_raw, bn_scale
        shared.bout, shared.bqk_col, shared.causal, shared.down_t, shared.dset, shared.g_col = bout, bqk_col, causal, down_t, dset, g_col
        shared.gam, shared.ident, shared.iota_e, shared.iota_hi, shared.iota_k, shared.iota_lo = gam, ident, iota_e, iota_hi, iota_k, iota_lo
        shared.keysim, shared.map_bias, shared.minus_half, shared.out, shared.same_quad, shared.upw = keysim, map_bias, minus_half, out, same_quad, upw
        shared.wcomb, shared.we, shared.wg, shared.wh, shared.wout0, shared.wout1_t = wcomb, we, wg, wh, wout0, wout1_t
        shared.wqk, shared.x3, shared.x3t, shared.x_in, shared.xall = wqk, x3, x3t, x_in, xall
        shared.psum, shared.map_bias_all = psum, map_bias_all
        layers_loop(nc, shared)
        peer_loop(nc, shared)


def wait_apart(eng, spare, s, value):
    eng.wait_ge(s.h, value)
    eng.sem_inc(spare, 1)


def layer_norm(nc, dve, spare, b, own, stats, mv, rstd, src, dst, tiles, var_ok, rstd_ok, done):
    for u in range(tiles):
        nc.vector.bn_stats(stats[:, u, :], src(u)).then_inc(own.h, 1)
        own.seen += 1
    for u in range(tiles):
        wait_apart(dve, spare, own, own.at(b, own.seen - tiles + u + 1))
        ins = nc.vector.bn_aggr(mv[:, u, :], stats[:, u, :])
    ins.then_inc(own.h, 1)
    own.seen += 1
    dve.wait_ge(own.h, own.at(b, own.seen))
    nc.vector.tensor_scalar(rstd[:], mv[:, :, 1:2], EPS, None, ALU.add).then_inc(var_ok.h, 1)
    var_ok.seen += 1
    dve.wait_ge(rstd_ok.h, rstd_ok.at(b, var_ok.seen))
    for u in range(tiles):
        nc.vector.tensor_scalar(dst(u), src(u), mv[:, u, 0:1], rstd[:, u, :], ALU.subtract, ALU.mult)\
            .then_inc(done.h, 1)


def layers_loop(nc, v):
    B, N, D, T, E, EC, HID = v.B, v.N, v.D, v.T, v.E, v.EC, v.HID
    HEADS, HD, QUADS, GROUP = v.HEADS, v.HD, v.QUADS, v.GROUP
    bank, psum, ident, bc, arrived = v.bank, v.psum, v.ident, v.bc, v.arrived
    VW = HD + 1
    ctx = ExitStack()
    with ctx:
        def sb(name, shape, dt=F32):
            return ctx.enter_context(nc.sbuf_tensor(name, shape, dt))

        primed = []

        def sem(name, per=1, start=0):
            s = Sem(ctx.enter_context(nc.semaphore(name)), per, start)
            if start:
                primed.append(s)
            return s

        xres = sb("xres", [P, T, P])
        xh = sb("xh", [P, T, P])
        normed_t = sb("normed_t", [P, N])
        qk_t = sb("qk_t", [P, N])
        heads_t = sb("heads_t", [P, 4, N])
        gate_t = sb("gate_t", [P, EC, N])
        val = sb("val", [P, T, HID])
        sim = sb("sim", [P, T, P])
        attn_t = sb("attn_t", [P, T, P])
        link = sb("link", [P, T, P])
        kv = sb("kv", [P, HID])
        gated_t = sb("gated_t", [P, EC, N])
        z = sb("z", [P, T, P])
        x1 = sb("x1", [P, T, P])
        x1t = sb("x1t", [P, N])
        lmax, lsum = sb("lmax", [P, T]), sb("lsum", [P, T])
        gate = sb("gate", [P, T, E])
        top, topi, topf = sb("top", [P, T, 8]), sb("topi", [P, T, 8], U32), sb("topf", [P, T, 8])
        hit0, hit1 = sb("hit0", [P, T, E]), sb("hit1", [P, T, E])
        wexp = sb("wexp", [P, T, E])
        z2 = sb("z2", [P, T, P])
        x2 = sb("x2", [P, T, P])
        x2t = sb("x2t", [P, N])
        pm = sb("pm", [P, T, 2 * HEADS, HD])
        pmax, pmin = sb("pmax", [P, T * 2 * HEADS]), sb("pmin", [P, T * 2 * HEADS])
        pe_in = sb("pe_in", [P, T * 2 * HEADS, 2, HD])
        psum_, prec = sb("psum_", [P, T * 2 * HEADS, 2]), sb("prec", [P, T * 2 * HEADS, 2])
        feat = sb("feat", [P, T, 2, HEADS, 32])
        vaug = sb("vaug", [P, T, HEADS, VW])
        qf_t, kf_t = sb("qf_t", [P, T, QUADS, P]), sb("kf_t", [P, T, QUADS, P])
        amask = sb("amask", [P, 2, HEADS, P])
        state = sb("state", [P, T - 1, QUADS, 4, VW])
        den = sb("den", [P, T, HEADS])
        y, yt = xh, sb("yt", [P, N])
        z3, x3b = z, sb("x3b", [P, T, P])
        stats, mv, rstd = sb("stats", [P, T, 6]), sb("mv", [P, T, 2]), sb("rstd", [P, T, 1])

        pads = sem("pads")
        xh_ok, xht_mm, normed_ok = sem("xh_ok", T), sem("xht_mm", 1), sem("normed_ok", 1)
        qk_mm, gate_mm, val_mm = sem("qk_mm", 1), sem("gate_mm", EC), sem("val_mm", 2)
        qk_ok, gate_ok, valb_ok, val_ok = sem("qk_ok", 1), sem("gate_ok", EC), sem("valb_ok", 2), sem("val_ok", 2)
        quad_ok, lin_ok = sem("quad_ok", 2, 1), sem("lin_ok", 2, 1)
        sim_mm, attn_ok = sem("sim_mm", 1), sem("attn_ok", 1)
        link_mm, link_ok, kv_mm, kv_ok = sem("link_mm", 1), sem("link_ok", 1), sem("kv_mm", 1), sem("kv_ok", 1)
        outt_mm, gated_ok, out_mm = sem("outt_mm", EC), sem("gated_ok", EC, 1), sem("out_mm", 1, 1)
        xres_ok, x1_ok = sem("xres_ok", 2), sem("x1_ok", T, 1)
        x1t_mm, x1t_ok, logit_mm = sem("x1t_mm", 1), sem("x1t_ok", 1), sem("logit_mm", 1)
        shift_ok, exp_ok = sem("shift_ok", 1), sem("exp_ok", 1)
        y_mm, y_used, x2_ok = sem("y_mm", T), sem("y_used", T), sem("x2_ok", T)
        x2t_mm, x2t_ok = sem("x2t_mm", 1), sem("x2t_ok", 1)
        qkv_mm, pm_ok, v_ok, min_ok, neg_ok = (sem("qkv_mm", T), sem("pm_ok", 2), sem("v_ok", 2), sem("min_ok", 2),
                                               sem("neg_ok", 2))
        pos_ok, fexp_ok, feat_ok = sem("pos_ok", 2), sem("fexp_ok", 2), sem("feat_ok", 2)
        ft_mm, ft_ok = sem("ft_mm", T), sem("ft_ok", T)
        a_mm, amask_dve, acopy_ok, amask_pool = sem("a_mm", T), sem("amask_dve", T), sem("acopy_ok", T), sem("amask_pool", T)
        st_mm, st_ok, num_mm, y_ok = sem("st_mm", 1), sem("st_ok", 1), sem("num_mm", T), sem("y_ok", 1)
        yt_mm, yt_ok, z3_mm, z3_ok = sem("yt_mm", 1), sem("yt_ok", 1), sem("z3_mm", 1), sem("z3_ok", 1, 1)
        x3_ok, x3t_mm, x3t_ok = sem("x3_ok", T), sem("x3t_mm", 1), sem("x3t_ok", 1)
        bn_ok, x3_kept = sem("bn_ok", 1, 1), sem("x3_kept", 1, 1)
        var_ok, rstd_ok = sem("var_ok", 4), sem("rstd_ok", 4)
        spare = sem("spare").h
        own = sem("dve_own", 0)
        own.per = OWN_LAYERS
        pool_own = sem("pool_own", 2)

        with nc.Block() as block:
            @block.gpsimd
            def _(pool):
                for s in primed:
                    pool.sem_inc(s.h, 1)
                nc.gpsimd.memset(feat[:], 0.0)
                nc.gpsimd.memset(vaug[:], 1.0).then_inc(pads.h, 1)
                arrived(pool, "l0")

                def inverse_root(b, k):
                    wait(pool, var_ok, b, k)
                    nc.gpsimd.tensor_tensor(rstd[:], rstd[:], bc(v.minus_half[:].unsqueeze(1), [P, T, 1]), ALU.pow)\
                        .then_inc(rstd_ok.h, 1)

                with pool.Fori(0, B) as b:
                    inverse_root(b, 1)
                    wait_last(pool, x1_ok, b)
                    wait_apart(pool, spare, v.x_in, v.x_in.at(b, 16))
                    xs = v.xall[:, bass.ds(b * T, T), :]
                    nc.gpsimd.tensor_tensor(xres[:], xs, xs, ALU.add).then_inc(xres_ok.h, 1)
                    wait(pool, xres_ok, b, 1)
                    nc.gpsimd.tensor_tensor(xres[:], xres[:], bc(v.bout[:].unsqueeze(1), [P, T, P]), ALU.add)\
                        .then_inc(xres_ok.h, 1)
                    wait_last(pool, out_mm, b)
                    wait_apart(pool, spare, qk_ok, qk_ok.at(b, 1))
                    for h in (1, 3):
                        nc.gpsimd.tensor_scalar(heads_t[:, h, :], qk_t[:], v.gam[:, h:h + 1], v.bet[:, h:h + 1],
                                                ALU.mult, ALU.add).then_inc(lin_ok.h, 1)
                    for k in (2, 3):
                        inverse_root(b, k)
                    for i in range(2):
                        rows = slice(2 * HEADS * 2 * i, 2 * HEADS * 2 * (i + 1))
                        wait(pool, min_ok, b, i + 1)
                        nc.gpsimd.tensor_tensor(pe_in[:, rows, 1, :], bc(pmin[:, rows].unsqueeze(2), [P, 4 * HEADS, HD]),
                                                pm[:, 2 * i:2 * i + 2].rearrange("p t h d -> p (t h) d"),
                                                ALU.subtract).then_inc(neg_ok.h, 1)
                    for u in range(T):
                        wait_apart(pool, spare, acopy_ok, acopy_ok.at(b, u + 1))
                        half = amask[:, u % 2].rearrange("p (c g) t -> p c g t", g=4)[:, :, 2:4, :]
                        nc.gpsimd.affine_select(half, half, pattern=[[0, QUADS], [0, 2], [1, P]], compare_op=ALU.is_ge,
                                                fill=0.0, base=0, channel_multiplier=-1).then_inc(amask_pool.h, 1)
                    inverse_root(b, 4)
                    wait_apart(pool, spare, x3_ok, x3_ok.at(b, T))
                    nc.gpsimd.tensor_copy(v.x3[:, bass.ds(b * T, T), :], x3b[:]).then_inc(x3_kept.h, 1)

            @block.scalar
            def _(act):
                act.wait_ge(pads.h, 1)
                arrived(act, "l0")
                with act.Fori(0, B) as b:
                    wait(act, xht_mm, b)
                    nc.scalar.activation(normed_t[:], bank[0][:], ACT.Identity, bias=v.b_col[:], scale=v.g_col[:])\
                        .then_inc(normed_ok.h, 1)
                    wait(act, qk_mm, b)
                    wait_last(act, lin_ok, b)
                    wait_last(act, quad_ok, b)
                    nc.scalar.activation(qk_t[:], bank[1][:], ACT.Silu, bias=v.bqk_col[:]).then_inc(qk_ok.h, 1)
                    wait_last(act, gated_ok, b)
                    for c in range(EC):
                        wait(act, gate_mm, b, c + 1)
                        nc.scalar.activation(gate_t[:, c, :], bank[2 + c][:], ACT.Silu, bias=v.bh_gate[:, c:c + 1])\
                            .then_inc(gate_ok.h, 1)
                    for i in range(2):
                        wait(act, valb_ok, b, i + 1)
                        nc.scalar.activation(val[:, 2 * i:2 * i + 2, :], val[:, 2 * i:2 * i + 2, :], ACT.Silu)\
                            .then_inc(val_ok.h, 1)
                    wait(act, link_mm, b)
                    nc.scalar.copy(link[:].rearrange("p t d -> p (t d)"), bank[7][:]).then_inc(link_ok.h, 1)
                    wait(act, kv_mm, b)
                    nc.scalar.mul(kv[:], bank[0][:, 0:HID], 1.0 / N).then_inc(kv_ok.h, 1)
                    wait(act, x1t_mm, b)
                    nc.scalar.copy(x1t[:], bank[4][:]).then_inc(x1t_ok.h, 1)
                    wait(act, shift_ok, b)
                    nc.scalar.activation(gate[:], gate[:], ACT.Exp).then_inc(exp_ok.h, 1)
                    wait(act, x2t_mm, b)
                    nc.scalar.copy(x2t[:], bank[4][:]).then_inc(x2t_ok.h, 1)
                    for i in range(2):
                        wait(act, pm_ok, b, i + 1)
                        nc.scalar.copy(vaug[:, 2 * i:2 * i + 2, :, 0:HD],
                                       psum[:, 2 * i:2 * i + 2, 2 * P:3 * P].rearrange("p t (h d) -> p t h d", d=HD))\
                            .then_inc(v_ok.h, 1)
                    for i in range(2):
                        rows = slice(4 * HEADS * i, 4 * HEADS * (i + 1))
                        wait(act, pos_ok, b, i + 1)
                        wait(act, neg_ok, b, i + 1)
                        nc.scalar.activation(pe_in[:, rows], pe_in[:, rows], ACT.Exp).then_inc(fexp_ok.h, 1)
                    for u in range(T):
                        wait(act, ft_mm, b, u + 1)
                        q = 4 + 2 * (u % 2)
                        nc.scalar.copy(qf_t[:, u].rearrange("p c t -> p (c t)"), bank[q])
                        nc.scalar.copy(kf_t[:, u].rearrange("p c t -> p (c t)"), bank[q + 1]).then_inc(ft_ok.h, 1)
                    for u in range(T):
                        wait(act, a_mm, b, u + 1)
                        if u >= 2:
                            wait(act, num_mm, b, u - 1)
                        nc.scalar.copy(amask[:, u % 2].rearrange("p (c g) t -> p g c t", g=4)[:, 2:4],
                                       psum[:, 6:8, :].rearrange("p g (c t) -> p g c t", c=QUADS))\
                            .then_inc(acopy_ok.h, 1)
                    wait(act, yt_mm, b)
                    nc.scalar.copy(yt[:], bank[2]).then_inc(yt_ok.h, 1)
                    wait(act, x3t_mm, b)
                    nc.scalar.copy(v.x3t[:, bass.ds(b * N, N)], bank[4][:]).then_inc(x3t_ok.h, 1)

            @block.vector
            def _(dve):
                def step(ins, plain=False):
                    ins.then_inc(own.h, 1)
                    own.seen += 1
                    if plain:
                        wait_apart(dve, spare, own, own.at(bb, own.seen))
                    else:
                        dve.wait_ge(own.h, own.at(bb, own.seen))

                def norm(src, dst, done):
                    layer_norm(nc, dve, spare, bb, own, stats, mv, rstd, src, dst, T, var_ok, rstd_ok, done)

                arrived(dve, "l0")
                arrived(dve, "l1")
                dve.wait_ge(v.dset.h, 6)
                with dve.Fori(0, B) as b:
                    bb = b
                    own.seen = var_ok.seen = 0
                    wait_apart(dve, spare, v.x_in, v.x_in.at(b, 16))
                    norm(lambda u: v.xall[:, bass.ds(b * T + u, 1), :].rearrange("p a d -> p (a d)"),
                         lambda u: xh[:, u, :], xh_ok)
                    for i in range(2):
                        wait(dve, val_mm, b, i + 1)
                        nc.vector.tensor_tensor(val[:, 2 * i:2 * i + 2, :],
                                                bank[4 + i][:].rearrange("p (t e) -> p t e", t=2),
                                                bc(v.bh_v[:].unsqueeze(1), [P, 2, HID]), ALU.add)\
                            .then_inc(valb_ok.h, 1)
                    wait(dve, qk_ok, b)
                    for h in (0, 2):
                        nc.vector.tensor_scalar(heads_t[:, h, :], qk_t[:], v.gam[:, h:h + 1], v.bet[:, h:h + 1],
                                                ALU.mult, ALU.add).then_inc(quad_ok.h, 1)
                    wait(dve, sim_mm, b)
                    step(nc.vector.scalar_tensor_tensor(sim[:], bank[6][:].rearrange("p (t i) -> p t i", t=T),
                                                        1.0 / GROUP, bc(v.bias_t[:].unsqueeze(1), [P, T, P]),
                                                        ALU.mult, ALU.add))
                    nc.vector.scalar_tensor_tensor(attn_t[:], sim[:], 0.0, sim[:], ALU.max, ALU.mult)\
                        .then_inc(attn_ok.h, 1)
                    for c in range(EC):
                        wait(dve, outt_mm, b, c + 1)
                        wait(dve, gate_ok, b, c + 1)
                        nc.vector.tensor_tensor(gated_t[:, c, :], gate_t[:, c, :], bank[(1, 7)[c]][:], ALU.mult)\
                            .then_inc(gated_ok.h, 1)
                    wait(dve, out_mm, b)
                    wait(dve, xres_ok, b)
                    step(nc.vector.tensor_tensor(z[:], bank[0][:].rearrange("p (t d) -> p t d", t=T), xres[:],
                                                 ALU.add))
                    norm(lambda u: z[:, u, :], lambda u: x1[:, u, :], x1_ok)

                    wait(dve, logit_mm, b)
                    logits = bank[5][:, 0:T * E].rearrange("p (t e) -> p t e", t=T)
                    step(nc.vector.tensor_reduce(lmax[:], logits, X, ALU.max))
                    nc.vector.tensor_tensor(gate[:], logits, bc(lmax[:].unsqueeze(2), [P, T, E]), ALU.subtract)\
                        .then_inc(shift_ok.h, 1)
                    wait(dve, exp_ok, b)
                    step(nc.vector.tensor_reduce(lsum[:], gate[:], X, ALU.add))
                    step(nc.vector.reciprocal(lsum[:], lsum[:]))
                    step(nc.vector.tensor_tensor(gate[:], gate[:], bc(lsum[:].unsqueeze(2), [P, T, E]), ALU.mult), True)
                    for u in range(T):
                        ins = nc.vector.max(top[:, u, :], gate[:, u, :])
                    step(ins, True)
                    for u in range(T):
                        ins = nc.vector.max_index(topi[:, u, :], top[:, u, :], gate[:, u, :])
                    step(ins)
                    nc.vector.tensor_copy(topf[:], topi[:])
                    step(nc.vector.tensor_tensor(lsum[:], top[:, :, 0], top[:, :, 1], ALU.add))
                    step(nc.vector.tensor_scalar(lsum[:], lsum[:], 1e-9, None, ALU.add))
                    nc.vector.reciprocal(lsum[:], lsum[:])
                    iota = bc(v.iota_e[:].unsqueeze(1), [P, T, E])
                    for j, hit in ((0, hit0), (1, hit1)):
                        ins = nc.vector.tensor_tensor(hit[:], iota, bc(topf[:, :, j:j + 1], [P, T, E]), ALU.is_equal)
                    step(ins)
                    for j, hit in ((0, hit0), (1, hit1)):
                        ins = nc.vector.tensor_tensor(hit[:], hit[:], bc(top[:, :, j:j + 1], [P, T, E]), ALU.mult)
                    step(ins)
                    step(nc.vector.tensor_tensor(hit0[:], hit0[:], hit1[:], ALU.add))
                    step(nc.vector.tensor_tensor(wexp[:], hit0[:], bc(lsum[:].unsqueeze(2), [P, T, E]), ALU.mult), True)
                    for p in range(T // 2):
                        for e in range(E):
                            for t in range(2):
                                u = 2 * p + t
                                if e == 0:
                                    wait(dve, y_mm, b, u + 1)
                                else:
                                    after = 0 if e == E - 1 and t == 1 else 1
                                    dve.wait_ge(own.h, own.at(b, own.seen - after))
                                src = bank[(2, 6)[t] + e // 4][:, P * (e % 4):P * (e % 4) + P]
                                ins = nc.vector.scalar_tensor_tensor(z2[:, u, :], src, wexp[:, u, e:e + 1],
                                                                     (z2 if e else x1)[:, u, :], ALU.mult, ALU.add)
                                if e < E - 1:
                                    ins.then_inc(own.h, 1)
                                    own.seen += 1
                                else:
                                    ins.then_inc(y_used.h, 1)
                    wait(dve, y_used, b)
                    norm(lambda u: z2[:, u, :], lambda u: x2[:, u, :], x2_ok)

                    for i in range(2):
                        wait(dve, qkv_mm, b, 2 * i + 2)
                        nc.vector.tensor_tensor(
                            pm[:, 2 * i:2 * i + 2].rearrange("p t h d -> p t (h d)"), psum[:, 2 * i:2 * i + 2, 0:2 * P],
                            bc(v.map_bias_all[:].rearrange("p i h d -> p (i h d)").unsqueeze(1), [P, 2, 2 * P]),
                            ALU.add).then_inc(pm_ok.h, 1)
                    for i in range(2):
                        rows = slice(4 * HEADS * i, 4 * HEADS * (i + 1))
                        half = pm[:, 2 * i:2 * i + 2].rearrange("p t h d -> p (t h) d")
                        wait(dve, pm_ok, b, i + 1)
                        nc.vector.tensor_reduce(pmin[:, rows], half, X, ALU.min).then_inc(min_ok.h, 1)
                        step(nc.vector.tensor_reduce(pmax[:, rows], half, X, ALU.max))
                        nc.vector.tensor_tensor(pe_in[:, rows, 0, :], half,
                                                bc(pmax[:, rows].unsqueeze(2), [P, 4 * HEADS, HD]),
                                                ALU.subtract).then_inc(pos_ok.h, 1)
                    for i in range(2):
                        rows = slice(4 * HEADS * i, 4 * HEADS * (i + 1))
                        wait(dve, fexp_ok, b, i + 1)
                        step(nc.vector.tensor_reduce(psum_[:, rows], pe_in[:, rows], X, ALU.add))
                        step(nc.vector.reciprocal(prec[:, rows], psum_[:, rows]))
                        nc.vector.tensor_tensor(
                            feat[:].rearrange("p t i h (s f) -> p (t i h) s f", s=4)[:, rows, 0:2, :],
                            pe_in[:, rows], bc(prec[:, rows].unsqueeze(3), [P, 4 * HEADS, 2, HD]), ALU.mult)\
                            .then_inc(feat_ok.h, 1)
                    wait(dve, st_mm, b)
                    step(nc.vector.tensor_tensor(
                        state[:].rearrange("p t c g f -> p (t c) g f"),
                        bank[2][:, 0:(T - 1) * HEADS * VW].rearrange("p (a g f) -> p a g f", g=4, f=VW),
                        bc(v.same_quad[:].unsqueeze(1).unsqueeze(3), [P, (T - 1) * QUADS, 4, VW]), ALU.mult))
                    for u in range(1, T - 1):
                        ins = nc.vector.tensor_tensor(state[:, u], state[:, u], state[:, u - 1], ALU.add)
                        if u < T - 2:
                            step(ins)
                    ins.then_inc(st_ok.h, 1)
                    for u in range(T):
                        wait(dve, a_mm, b, u + 1)
                        if u >= 2:
                            wait(dve, num_mm, b, u - 1)
                        for g in range(2):
                            ins = nc.vector.tensor_tensor(
                                amask[:, u % 2].rearrange("p (c g) t -> p g c t", g=4)[:, g],
                                bank[4 + g].rearrange("p (c t) -> p c t", c=QUADS),
                                bc(v.causal[:].unsqueeze(1), [P, QUADS, P]), ALU.mult)
                        ins.then_inc(amask_dve.h, 1)
                    wait(dve, num_mm, b)
                    nd = psum[:, 0:2, :].rearrange("p a (t f) -> p (a t) f", t=2)[:, :, 0:HEADS * VW]\
                        .rearrange("p t (h f) -> p t h f", f=VW)
                    step(nc.vector.tensor_scalar(den[:], nd[:, :, :, HD], 1e-6, None, ALU.max))
                    step(nc.vector.reciprocal(den[:], den[:]))
                    nc.vector.tensor_tensor(y[:].rearrange("p t (h d) -> p t h d", d=HD), nd[:, :, :, 0:HD],
                                            bc(den[:].unsqueeze(3), [P, T, HEADS, HD]), ALU.mult)\
                        .then_inc(y_ok.h, 1)
                    wait(dve, z3_mm, b)
                    nc.vector.tensor_tensor(z3[:], x2[:], bank[3].rearrange("p (t d) -> p t d", t=T), ALU.add)\
                        .then_inc(z3_ok.h, 1)
                    wait(dve, z3_ok, b)
                    wait_last(dve, x3_kept, b)
                    norm(lambda u: z3[:, u, :], lambda u: x3b[:, u, :], x3_ok)
                    wait_apart(dve, spare, x3t_ok, x3t_ok.at(b, 1))
                    nc.vector.bn_stats(v.bn_raw[:, bass.ds(b, 1), :].rearrange("p a s -> p (a s)"), bank[4][:])\
                        .then_inc(bn_ok.h, 1)
                assert own.seen == own.per, own.seen

            @block.tensor
            def _(pe):
                arrived(pe, "l0")
                arrived(pe, "moe")
                pe.wait_ge(v.dset.h, 6)
                with pe.Fori(0, B) as b:
                    wait_last(pe, z3_ok, b)
                    wait_last(pe, bn_ok, b)
                    for u in range(T):
                        wait(pe, xh_ok, b, u + 1)
                        ins = nc.tensor.transpose(bank[0][:, P * u:P * u + P], xh[:, u, :], ident[:])
                    ins.then_inc(xht_mm.h, 1)
                    wait(pe, normed_ok, b)
                    nc.tensor.matmul(bank[1][:], v.wqk[:], normed_t[:], start=True, stop=True).then_inc(qk_mm.h, 1)
                    for i in range(2):
                        for u in (2 * i, 2 * i + 1):
                            ins = nc.tensor.matmul(bank[4 + i][:, HID * (u % 2):HID * (u % 2) + HID],
                                                   normed_t[:, P * u:P * u + P], v.wh[:, 0:HID], start=True, stop=True)
                        ins.then_inc(val_mm.h, 1)
                    for c in range(EC):
                        nc.tensor.matmul(bank[2 + c][:], v.wh[:, HID + P * c:HID + P * c + P], normed_t[:],
                                         start=True, stop=True).then_inc(gate_mm.h, 1)
                    wait(pe, quad_ok, b)
                    for u in range(T):
                        q = slice(P * u, P * u + P)
                        ins = nc.tensor.matmul(bank[6][:, q], heads_t[:, 2, q], heads_t[:, 0, q], start=True, stop=True)
                    ins.then_inc(sim_mm.h, 1)
                    wait(pe, lin_ok, b)
                    for u in range(T):
                        q = slice(P * u, P * u + P)
                        ins = nc.tensor.transpose(bank[7][:, q], heads_t[:, 3, q], ident[:])
                    ins.then_inc(link_mm.h, 1)
                    wait(pe, link_ok, b)
                    wait(pe, val_ok, b)
                    for u in range(T):
                        ins = nc.tensor.matmul(bank[0][:, 0:HID], link[:, u, :], val[:, u, :],
                                               start=(u == 0), stop=(u == T - 1))
                    ins.then_inc(kv_mm.h, 1)
                    wait(pe, kv_ok, b)
                    wait(pe, attn_ok, b)
                    for c in range(EC):
                        o = bank[(1, 7)[c]]
                        for u in range(T):
                            nc.tensor.matmul(o[:, P * u:P * u + P], val[:, u, P * c:P * c + P], attn_t[:, u, :],
                                             start=(u == 0), stop=False, skip_group_check=True)
                        ins = nc.tensor.matmul(o[:], kv[:, P * c:P * c + P], heads_t[:, 1, :], start=False, stop=True,
                                               skip_group_check=True)
                        ins.then_inc(outt_mm.h, 1)
                    wait(pe, gated_ok, b)
                    for u in range(T):
                        for c in range(EC):
                            ins = nc.tensor.matmul(bank[0][:, P * u:P * u + P], gated_t[:, c, P * u:P * u + P],
                                                   v.wout0[:, c, :], start=(c == 0), stop=(c == EC - 1))
                    ins.then_inc(out_mm.h, 1)

                    for u in range(T):
                        wait(pe, x1_ok, b, u + 1)
                        ins = nc.tensor.transpose(bank[4][:, P * u:P * u + P], x1[:, u, :], ident[:])
                    ins.then_inc(x1t_mm.h, 1)
                    wait(pe, x1t_ok, b)
                    for u in range(T):
                        ins = nc.tensor.matmul(bank[5][:, E * u:E * u + E], x1t[:, P * u:P * u + P], v.wg[:],
                                               start=True, stop=True)
                    ins.then_inc(logit_mm.h, 1)
                    for u in range(T):
                        if u >= 2:
                            wait(pe, y_used, b, u - 1)
                        for k in range(2):
                            ins = nc.tensor.matmul(bank[(2, 6)[u % 2] + k][:], x1t[:, P * u:P * u + P],
                                                   v.we[:, 4 * k:4 * k + 4, :].rearrange("p e m -> p (e m)"),
                                                   start=True, stop=True)
                        ins.then_inc(y_mm.h, 1)

                    for u in range(T):
                        wait(pe, x2_ok, b, u + 1)
                        ins = nc.tensor.transpose(bank[4][:, P * u:P * u + P], x2[:, u, :], ident[:])
                    ins.then_inc(x2t_mm.h, 1)
                    wait(pe, x2t_ok, b)
                    for u in range(T):
                        nc.tensor.matmul(bank[u][:, 0:3 * P], x2t[:, P * u:P * u + P], v.wcomb[:],
                                         start=True, stop=True).then_inc(qkv_mm.h, 1)
                    for u in range(T):
                        if u % 2 == 0:
                            wait(pe, feat_ok, b, u // 2 + 1)
                        if u >= 2:
                            wait(pe, ft_ok, b, u - 1)
                        for i in range(2):
                            for c in range(QUADS):
                                ins = nc.tensor.transpose(
                                    bank[4 + 2 * (u % 2) + i][:, P * c:P * c + P],
                                    feat[:, u, i, 4 * c:4 * c + 4, :].rearrange("p h f -> p (h f)"), ident[:])
                        ins.then_inc(ft_mm.h, 1)
                    wait(pe, v_ok, b)
                    for u in range(T - 1):
                        for c in range(QUADS):
                            at = HEADS * VW * u + 4 * VW * c
                            ins = nc.tensor.matmul(bank[2][:, at:at + 4 * VW],
                                                   feat[:, u, 1, 4 * c:4 * c + 4, :].rearrange("p h f -> p (h f)"),
                                                   vaug[:, u, 4 * c:4 * c + 4, :].rearrange("p h f -> p (h f)"),
                                                   start=True, stop=True)
                    ins.then_inc(st_mm.h, 1)

                    def scores(u):
                        if u:
                            wait(pe, amask_dve, b, u)
                            wait(pe, acopy_ok, b, u)
                        else:
                            wait(pe, ft_ok, b)
                        for c in range(QUADS):
                            for g in range(4):
                                r = slice(32 * g, 32 * g + 32)
                                ins = nc.tensor.matmul(bank[4 + g][:, P * c:P * c + P], kf_t[r, u, c, :],
                                                       qf_t[r, u, c, :], start=True, stop=True)
                        ins.then_inc(a_mm.h, 1)

                    def numerators(u):
                        wait(pe, amask_dve, b, u + 1)
                        wait(pe, amask_pool, b, u + 1)
                        at, first = 256 * (u % 2), True
                        if u:
                            if u == 1:
                                wait(pe, st_ok, b)
                            for c in range(QUADS):
                                nc.tensor.matmul(bank[u // 2][:, at + 36 * c:at + 36 * c + 36], qf_t[:, u, c, :],
                                                 state[:, u - 1, c].rearrange("p g f -> p (g f)"),
                                                 start=first, stop=False, skip_group_check=True)
                                first = False
                        for h in range(HEADS):
                            ins = nc.tensor.matmul(bank[u // 2][:, at + VW * h:at + VW * h + VW],
                                                   amask[:, u % 2, h, :], vaug[:, u, h, :],
                                                   start=first, stop=True, skip_group_check=True)
                            first = False
                        ins.then_inc(num_mm.h, 1)

                    scores(0)
                    for u in range(T):
                        if u < T - 1:
                            scores(u + 1)
                        numerators(u)
                    wait(pe, y_ok, b)
                    for u in range(T):
                        ins = nc.tensor.transpose(bank[2][:, P * u:P * u + P], y[:, u, :], ident[:])
                    ins.then_inc(yt_mm.h, 1)
                    wait(pe, yt_ok, b)
                    for u in range(T):
                        ins = nc.tensor.matmul(bank[3][:, P * u:P * u + P], yt[:, P * u:P * u + P], v.wout1_t[:],
                                               start=True, stop=True)
                    ins.then_inc(z3_mm.h, 1)
                    for u in range(T):
                        wait(pe, x3_ok, b, u + 1)
                        ins = nc.tensor.transpose(
                            bank[4][:, P * u:P * u + P], x3b[:, u, :], ident[:])
                    ins.then_inc(x3t_mm.h, 1)


OWN_LAYERS = 72
OWN_PEER = 29


def peer_loop(nc, v):
    B, N, T, NH, NK, K, SETS, EH, PAIRS = v.B, v.N, v.T, v.NH, v.NK, v.K, v.SETS, v.EH, v.PAIRS
    bank, ident, bc, arrived = v.bank, v.ident, v.bc, v.arrived
    HK = NH * K
    LB = 512 // (2 * EH)
    QB = P // LB
    ctx = ExitStack()
    with ctx:
        def sb(name, shape, dt=F32):
            return ctx.enter_context(nc.sbuf_tensor(name, shape, dt))

        primed = []

        def sem(name, per=1, start=0):
            s = Sem(ctx.enter_context(nc.semaphore(name)), per, start)
            if start:
                primed.append(s)
            return s

        xn = sb("xn", [P, N])
        keysims = sb("keysims", [P, T, SETS, NK])
        side, side_i = sb("side", [P, T, SETS, K]), sb("side_i", [P, T, SETS, K], U32)
        side_f = sb("side_f", [P, T, SETS, K])
        cand = sb("cand", [P, 2, NH, K, K])
        best, best_i = sb("best", [P, T, NH, K]), sb("best_i", [P, 2, NH, K], U32)
        rc = sb("rc", [P, 2, 2, HK], U32)
        eq = sb("eq", [P, 2, SETS, K, K])
        dec = sb("dec", [P, SETS, K])
        e_num, lohi = sb("e_num", [P, HK], U32), sb("lohi", [P, T, 2, HK], U32)
        comp = sb("comp", [P, PAIRS, 3, 2, HK])
        lh_t = sb("lh_t", [P, 2, P], F16)
        w_t = sb("w_t", [P, P])
        w_hi, w_lo = sb("w_hi", [P, P], F16), sb("w_lo", [P, P], F16)
        hot_lo = sb("hot_lo", [P, P, P], F16)
        hot_hi = sb("hot_hi", [P, EH, P], F16)
        hot_w = sb("hot_w", [P, 2, 2, EH, P], F16)
        hid = sb("hid", [P, T, EH, P])
        mix = sb("mix", [P, 2 * EH, P])
        z4, o4 = sb("z4", [P, T, P]), sb("o4", [P, T, P])
        stats, mv, rstd = sb("stats4", [P, T, 6]), sb("mv4", [P, T, 2]), sb("rstd4", [P, T, 1])
        bn_inv = sb("bn_inv", [P, 1])

        bn_var, bn_pow, bn_done = sem("bn_var"), sem("bn_pow"), sem("bn_done")
        zeroed = sem("zeroed")
        xn_ok, xn_sub = sem("xn_ok", 1), sem("xn_sub", 1)
        ksim_mm, ksim_ok = sem("ksim_mm", T, 1), sem("ksim_ok", T)
        h_mm, h_ok = sem("h_mm", EH, 1), sem("h_ok", EH)
        side_ok, cand_ok, best_ok = sem("side_ok", T, 1), sem("cand_ok", T), sem("best_ok", T)
        lohi_ok, sig_ok, comp_ok = sem("lohi_ok", T), sem("sig_ok", T), sem("comp_ok", T)
        comp_mm, comp_t_ok = sem("comp_mm", PAIRS, 1), sem("comp_t_ok", PAIRS)
        side_f_ok, eq_is, eq_ok = sem("side_f_ok", T), sem("eq_is", T), sem("eq_ok", T)
        hot_ok, g_mm, mix_ok = sem("hot_ok", PAIRS * QB), sem("g_mm", PAIRS * QB, 1), sem("mix_ok", PAIRS * QB, 1)
        out_mm, z4_ok, o4_ok, stored = sem("out4_mm", T, 1), sem("z4_ok", T, 1), sem("o4_ok", T), sem("stored", 16, 1)
        var_ok, rstd_ok = sem("var4_ok", 1), sem("rstd4_ok", 1)
        spare = sem("spare4").h
        own = sem("dve_own4", OWN_PEER)

        with nc.Block() as block:
            @block.sync
            def _(sp):
                with sp.Fori(0, B) as b:
                    wait(sp, o4_ok, b)
                    sp.dma_start(v.out[bass.ds(b, 1), :, :].rearrange("a (t p) d -> p (a t) d", p=P), o4[:])\
                        .then_inc(stored.h, 16)
                sp.wait_ge(stored.h, stored.start + 16 * B)

            @block.gpsimd
            def _(pool):
                for s in primed:
                    pool.sem_inc(s.h, 1)
                nc.gpsimd.memset(hot_w[:], 0.0).then_inc(zeroed.h, 1)
                pool.wait_ge(bn_var.h, 1)
                nc.gpsimd.tensor_tensor(bn_inv[:], bn_inv[:], v.minus_half[:], ALU.pow).then_inc(bn_pow.h, 1)
                with pool.Fori(0, B) as b:
                    for p in range(PAIRS):
                        for u in (2 * p, 2 * p + 1):
                            wait(pool, side_ok, b, u + 1)
                            if p:
                                wait(pool, best_ok, b, u - 1)
                            nc.gpsimd.tensor_tensor(
                                cand[:, u % 2], bc(side[:, u, 0:NH, :].unsqueeze(3), [P, NH, K, K]),
                                bc(side[:, u, NH:SETS, :].unsqueeze(2), [P, NH, K, K]), ALU.add)\
                                .then_inc(cand_ok.h, 1)
                        for u in (2 * p, 2 * p + 1):
                            wait(pool, side_f_ok, b, u + 1)
                            wait(pool, eq_is, b, u + 1)
                            nc.gpsimd.tensor_tensor(
                                eq[:, u % 2], eq[:, u % 2], bc(side_f[:, u].unsqueeze(2), [P, SETS, K, K]), ALU.mult)\
                                .then_inc(eq_ok.h, 1)
                    wait(pool, var_ok, b)
                    nc.gpsimd.tensor_tensor(rstd[:], rstd[:], bc(v.minus_half[:].unsqueeze(1), [P, T, 1]), ALU.pow)\
                        .then_inc(rstd_ok.h, 1)

            @block.scalar
            def _(act):
                with act.Fori(0, B) as b:
                    for u in range(T):
                        wait(act, ksim_mm, b, u + 1)
                        wait_last(act, side_ok, b)
                        nc.scalar.copy(keysims[:, u].rearrange("p s k -> p (s k)"), bank[u % 2][:])\
                            .then_inc(ksim_ok.h, 1)
                    wait_last(act, mix_ok, b)
                    for c in range(EH):
                        wait(act, h_mm, b, c + 1)
                        nc.scalar.activation(hid[:, :, c, :], bank[6 + c % 2][:].rearrange("p (t l) -> p t l", t=T),
                                             ACT.Gelu).then_inc(h_ok.h, 1)
                    wait_last(act, comp_mm, b)
                    for u in range(T):
                        wait(act, side_ok, b, u + 1)
                        nc.scalar.copy(side_f[:, u], side_i[:, u]).then_inc(side_f_ok.h, 1)
                        wait(act, best_ok, b, u + 1)
                        nc.scalar.activation(comp[:, u // 2, 2, u % 2, :],
                                             best[:, u].rearrange("p h k -> p (h k)"), ACT.Sigmoid)\
                            .then_inc(sig_ok.h, 1)
                        wait(act, lohi_ok, b, u + 1)
                        nc.scalar.copy(comp[:, u // 2, 0:2, u % 2, :], lohi[:, u]).then_inc(comp_ok.h, 1)
                        if u % 2:
                            p = u // 2
                            wait(act, comp_mm, b, p + 1)
                            if p:
                                wait(act, hot_ok, b, QB * p)
                            nc.scalar.copy(w_t[:], bank[1][:, 2 * P:3 * P])
                            nc.scalar.copy(lh_t[:].rearrange("p i l -> p (i l)"), bank[1][:, 0:2 * P])\
                                .then_inc(comp_t_ok.h, 1)

            @block.vector
            def _(dve):
                def step(ins, plain=False):
                    ins.then_inc(own.h, 1)
                    own.seen += 1
                    if plain:
                        wait_apart(dve, spare, own, own.at(bb, own.seen))
                    else:
                        dve.wait_ge(own.h, own.at(bb, own.seen))

                arrived(dve, "bn")
                nc.vector.bn_aggr(v.bn_mv[:], v.bn_raw[:].rearrange("p b s -> p (b s)")).then_inc(bn_done.h, 1)
                dve.wait_ge(bn_done.h, 1)
                nc.vector.tensor_scalar(bn_inv[:], v.bn_mv[:, 1:2], EPS, None, ALU.add).then_inc(bn_var.h, 1)
                dve.wait_ge(bn_pow.h, 1)
                nc.vector.tensor_tensor(v.bn_scale[:], bn_inv[:], v.bn_g[:], ALU.mult).then_inc(bn_done.h, 1)
                dve.wait_ge(bn_done.h, 2)
                dve.wait_ge(zeroed.h, 1)
                with dve.Fori(0, B) as b:
                    bb = b
                    own.seen = var_ok.seen = 0

                    def first_choice(u):
                        wait_apart(dve, spare, ksim_ok, ksim_ok.at(b, u + 1))
                        for s in range(SETS):
                            ins = nc.vector.max(side[:, u, s, :], keysims[:, u, s, :])
                        step(ins, True)
                        for s in range(SETS):
                            ins = nc.vector.max_index(side_i[:, u, s, :], side[:, u, s, :], keysims[:, u, s, :])
                        ins.then_inc(side_ok.h, 1)

                    def second_choice(u):
                        wait_apart(dve, spare, cand_ok, cand_ok.at(b, u + 1))
                        for h in range(NH):
                            ins = nc.vector.max(best[:, u, h, :], cand[:, u % 2, h].rearrange("p r c -> p (r c)"))
                        step(ins, True)
                        for h in range(NH):
                            ins = nc.vector.max_index(best_i[:, u % 2, h, :], best[:, u, h, :],
                                                      cand[:, u % 2, h].rearrange("p r c -> p (r c)"))
                        ins.then_inc(best_ok.h, 1)
                        wait(dve, best_ok, b, u + 1)
                        flat = best_i[:, u % 2].rearrange("p h k -> p (h k)")
                        nc.vector.tensor_scalar(rc[:, u % 2, 0, :], flat, 3, None, ALU.logical_shift_right)
                        step(nc.vector.tensor_scalar(rc[:, u % 2, 1, :], flat, K - 1, None, ALU.bitwise_and))
                        nc.vector.tensor_tensor(
                            eq[:, u % 2],
                            bc(rc[:, u % 2].rearrange("p s (h k) -> p (s h) k", k=K).unsqueeze(3), [P, SETS, K, K]),
                            bc(v.iota_k[:].unsqueeze(1).unsqueeze(1), [P, SETS, K, K]), ALU.is_equal)\
                            .then_inc(eq_is.h, 1)

                    def numbers(u):
                        wait(dve, eq_ok, b, u + 1)
                        step(nc.vector.tensor_reduce(dec[:], eq[:, u % 2], X, ALU.add))
                        step(nc.vector.scalar_tensor_tensor(
                            e_num[:], dec[:, 0:NH, :].rearrange("p h k -> p (h k)"), float(NK),
                            dec[:, NH:SETS, :].rearrange("p h k -> p (h k)"), ALU.mult, ALU.add))
                        nc.vector.tensor_scalar(lohi[:, u, 0, :], e_num[:], P - 1, None, ALU.bitwise_and)
                        nc.vector.tensor_scalar(lohi[:, u, 1, :], e_num[:], 7, None, ALU.logical_shift_right)\
                            .then_inc(lohi_ok.h, 1)

                    def one_hots(p):
                        wait(dve, comp_t_ok, b, p + 1)
                        if p:
                            wait(dve, g_mm, b, QB * p)
                        else:
                            wait_last(dve, g_mm, b)
                        nc.vector.tensor_scalar(w_hi[:], w_t[:], WEIGHT_SCALE, None, ALU.mult)
                        step(nc.vector.tensor_tensor(hot_hi[:], bc(lh_t[:, 1:2, :], [P, EH, P]), v.iota_hi[:],
                                                     ALU.is_equal))
                        step(nc.vector.scalar_tensor_tensor(w_lo[:], w_t[:], WEIGHT_SCALE, w_hi[:], ALU.mult,
                                                            ALU.subtract))
                        for t in range(2):
                            q = slice(HK * t, HK * t + HK)
                            for i, w in enumerate((w_hi, w_lo)):
                                ins = nc.vector.tensor_tensor(hot_w[q, i, t], hot_hi[q],
                                                              bc(w[q].unsqueeze(1), [HK, EH, P]), ALU.mult)
                        for q in range(QB):
                            lanes = slice(LB * q, LB * q + LB)
                            nc.vector.tensor_tensor(hot_lo[:, :, lanes], bc(lh_t[:, 0:1, lanes], [P, P, LB]),
                                                    v.iota_lo[:, :, lanes], ALU.is_equal).then_inc(hot_ok.h, 1)

                    def weigh(p, banks):
                        for q in banks:
                            wait(dve, g_mm, b, QB * p + q + 1)
                            if p == 0 and q == 0:
                                wait(dve, h_ok, b)
                                wait_last(dve, out_mm, b)
                            elif q == 0:
                                wait(dve, out_mm, b, 2 * p)
                            lanes = slice(LB * q, LB * q + LB)
                            nc.vector.scalar_tensor_tensor(
                                mix[:, :, lanes].rearrange("p e l -> p l e"),
                                bank[2 + q][:].rearrange("p (l e) -> p l e", e=2 * EH), 1.0 / WEIGHT_SCALE,
                                hid[:, 2 * p:2 * p + 2, :, lanes].rearrange("p t e l -> p l (t e)"),
                                ALU.mult, ALU.mult).then_inc(mix_ok.h, 1)

                    def residual(p):
                        wait(dve, out_mm, b, 2 * p + 2)
                        for u in (2 * p, 2 * p + 1):
                            nc.vector.tensor_tensor(z4[:, u, :], bank[p][:, P * (u % 2):P * (u % 2) + P],
                                                    v.x3[:, bass.ds(b * T + u, 1), :].rearrange("p a d -> p (a d)"),
                                                    ALU.add).then_inc(z4_ok.h, 1)

                    wait_last(dve, h_mm, b)
                    wait_last(dve, ksim_mm, b)
                    nc.vector.tensor_scalar(xn[:], v.x3t[:, bass.ds(b * N, N)], v.bn_mv[:, 0:1], v.bn_scale[:],
                                            ALU.subtract, ALU.mult).then_inc(xn_sub.h, 1)
                    wait(dve, xn_sub, b)
                    nc.vector.tensor_scalar(xn[:], xn[:], v.bn_b[:], None, ALU.add).then_inc(xn_ok.h, 1)
                    for u in (0, 1):
                        first_choice(u)
                    for u in (0, 1):
                        second_choice(u)
                    first_choice(2)
                    for u in (0, 1):
                        numbers(u)
                    first_choice(3)
                    one_hots(0)
                    for u in (2, 3):
                        second_choice(u)
                    weigh(0, range(0, QB // 2))
                    for u in (2, 3):
                        numbers(u)
                    weigh(0, range(QB // 2, QB))
                    one_hots(1)
                    residual(0)
                    weigh(1, range(QB))
                    residual(1)
                    wait(dve, z4_ok, b)
                    dve.wait_ge(stored.h, b * 16 + stored.start)
                    layer_norm(nc, dve, spare, b, own, stats, mv, rstd, lambda u: z4[:, u, :], lambda u: o4[:, u, :],
                               T, var_ok, rstd_ok, o4_ok)
                assert own.seen == own.per, own.seen

            @block.tensor
            def _(pe):
                arrived(pe, "peer")
                with pe.Fori(0, B) as b:
                    wait(pe, xn_ok, b)
                    wait_last(pe, z4_ok, b)
                    for u in range(T):
                        if u >= 2:
                            wait(pe, ksim_ok, b, u - 1)
                        nc.tensor.matmul(bank[u % 2][:], xn[:, P * u:P * u + P],
                                         v.keysim[:].rearrange("p s k -> p (s k)"), start=True, stop=True)\
                            .then_inc(ksim_mm.h, 1)
                    for c in range(EH):
                        if c >= 2:
                            wait(pe, h_ok, b, c - 1)
                        nc.tensor.matmul(bank[6 + c % 2][:], v.down_t[:, c, :], v.x3t[:, bass.ds(b * N, N)],
                                         start=True, stop=True).then_inc(h_mm.h, 1)

                    def transposes(p):
                        wait(pe, comp_ok, b, 2 * p + 2)
                        for i in range(3):
                            ins = nc.tensor.transpose(bank[1][:, P * i:P * i + P],
                                                      comp[:, p, i].rearrange("p t k -> p (t k)"), ident[:])
                        ins.then_inc(comp_mm.h, 1)

                    def gathered(p):
                        for q in range(QB):
                            wait(pe, hot_ok, b, QB * p + q + 1)
                            if p:
                                wait(pe, mix_ok, b, q + 1)
                            for lane in range(LB * q, LB * q + LB):
                                for i in range(2):
                                    c = 2 * EH * (lane % LB)
                                    ins = nc.tensor.matmul(
                                        bank[2 + q][:, c:c + 2 * EH], hot_lo[:, :, lane],
                                        hot_w[:, i, :, :, lane].rearrange("p t e -> p (t e)"),
                                        start=(i == 0), stop=(i == 1))
                            ins.then_inc(g_mm.h, 1)

                    def outputs(p):
                        wait(pe, mix_ok, b, QB * p + QB)
                        for t in range(2):
                            for e in range(EH):
                                ins = nc.tensor.matmul(bank[p][:, P * t:P * t + P], mix[:, EH * t + e, :],
                                                       v.upw[:, e, :], start=(e == 0), stop=(e == EH - 1))
                            ins.then_inc(out_mm.h, 1)

                    wait(pe, ksim_ok, b)
                    transposes(0)
                    gathered(0)
                    transposes(1)
                    outputs(0)
                    gathered(1)
                    outputs(1)


_INS = ["L0_attn_x", "L0_attn_ln_g", "L0_attn_ln_b", "L0_attn_W_h", "L0_attn_b_h", "L0_attn_W_qk", "L0_attn_b_qk",
        "L0_attn_os_gamma", "L0_attn_os_beta", "L0_attn_rel_emb", "L0_attn_W_out", "L0_attn_b_out", "L0_ffn_Wg",
        "L0_ffn_We", "L1_attn_w_qkv", "L1_attn_wq_map", "L1_attn_bq_map", "L1_attn_wk_map", "L1_attn_bk_map",
        "L1_attn_w_out", "L1_ffn_bn_gamma", "L1_ffn_bn_beta", "L1_ffn_w_q", "L1_ffn_keys_p", "L1_ffn_down",
        "L1_ffn_up"]


def kernel(**inputs):
    import numpy as _np
    import concourse.bacc as _bacc
    from concourse.bass_utils import run_bass_kernel_spmd as _run

    nc = _bacc.Bacc("TRN2", target_bir_lowering=False, num_devices=1)
    arrays, args = {}, []
    for name in _INS:
        a = _np.ascontiguousarray(inputs[name])
        arrays[f"in_{name}"] = a
        args.append(nc.dram_tensor(f"in_{name}", a.shape, mybir.dt.from_np(a.dtype), kind="ExternalInput").ap())
    shape = inputs["L0_attn_x"].shape
    args.append(nc.dram_tensor("out_0", shape, F32, kind="ExternalOutput").ap())
    build(nc, *args)
    r = _run(nc, [arrays], core_ids=[0])
    return r.results[0]["out_0"]
```

```python
from contextlib import ExitStack

import numpy as np
import concourse.bass as bass
from concourse import mybir

ALU = mybir.AluOpType
ACT = mybir.ActivationFunctionType
X = mybir.AxisListType.X
F32 = mybir.dt.float32
BF16 = mybir.dt.bfloat16
F16 = mybir.dt.float16
U32 = mybir.dt.uint32

P = 128
EPS = 1e-5
MASKED = -1e30
FEAT_SCALE, SCORE_SCALE = 2.0 ** 12, 2.0 ** 14
WEIGHT_SCALE = 4096.0


class Sem:

    def __init__(self, handle, per=1, start=0):
        self.h, self.per, self.start, self.seen = handle, per, start, 0

    def at(self, b, k):
        return b * self.per + (k + self.start)


def wait(eng, s, b, k=None):
    eng.wait_ge(s.h, s.at(b, s.per if k is None else k))


def wait_last(eng, s, b):
    assert s.start
    eng.wait_ge(s.h, s.at(b, 0))


class Shared:
    pass


def bucket_of(rel, buckets=32, max_dist=128):
    nb = buckets // 2
    n, exact = abs(rel), nb // 2
    if n < exact:
        return n + (nb if rel < 0 else 0)
    large = np.log(np.float32(n) / np.float32(exact)) / np.float32(np.log(max_dist / exact)) * np.float32(nb - exact)
    return min(exact + int(large), nb - 1) + (nb if rel < 0 else 0)


def bucket_runs(group):
    row = [bucket_of(m - (group - 1)) for m in range(2 * group - 1)]
    runs, i = [], 0
    while i < len(row):
        j = i + 1
        step = row[j] - row[i] if j < len(row) and row[j] - row[i] in (0, 1) else 0
        while j < len(row) and row[j] - row[j - 1] == step:
            j += 1
        runs.append((i, j - i, row[i], step))
        i = j
    return runs


def build(nc, x, ln_g, ln_b, W_h, b_h, W_qk, b_qk, os_gamma, os_beta, rel_emb, W_out, b_out, Wg, We,
          w_qkv, wq_map, bq_map, wk_map, bk_map, w_out, bn_gamma, bn_beta, w_q, keys_p, down, up, out):
    B, N, D = x.shape
    HID = W_h.shape[1] // 2
    EC = HID // P
    GROUP = 32
    T = N // P
    E = Wg.shape[1]
    HEADS, HD = D // wq_map.shape[0], wq_map.shape[0]
    QUADS = HEADS // 4
    NH, NK, _, KD = keys_p.shape
    K = 8
    SETS = 2 * NH
    EH = NK * NK // P
    PAIRS = T // 2

    ctx = ExitStack()
    with ctx:
        def sb(name, shape, dt=F32):
            return ctx.enter_context(nc.sbuf_tensor(name, shape, dt))

        def sem(name, per=1):
            s = Sem(ctx.enter_context(nc.semaphore(name)), per)
            return s

        psum = ctx.enter_context(nc.psum_tensor("psum", [P, 8, 512], F32))
        bank = [psum[:, i, :] for i in range(8)]

        ident = sb("ident", [P, P])
        flip = sb("flip", [GROUP, P])
        spread = sb("spread", [HD, P])
        causal = sb("causal", [P, P])
        same8 = sb("same8", [P, HEADS, HD])
        minus_half = sb("minus_half", [P, 1])
        same_quad = sb("same_quad", [P, 4])
        iota_e = sb("iota_e", [P, E])
        iota_k = sb("iota_k", [P, K])
        iota_lo = sb("iota_lo", [P, P, P], F16)
        iota_hi = sb("iota_hi", [P, EH, P], F16)
        g_col, b_col = sb("g_col", [P, 1]), sb("b_col", [P, 1])
        wh, bh_gate, bh_v = sb("wh", [P, 2 * HID]), sb("bh_gate", [P, EC]), sb("bh_v", [P, HID])
        wqk, bqk_col = sb("wqk", [P, P]), sb("bqk_col", [P, 1])
        gam, bet = sb("gam", [P, 4]), sb("bet", [P, 4])
        hankel, bias_t, bias_raw = sb("hankel", [GROUP, GROUP]), sb("bias_t", [P, P]), sb("bias_raw", [P, GROUP])
        wout0, bout = sb("wout0", [P, EC, P]), sb("bout", [P, P])
        wg, we = sb("wg", [P, E]), sb("we", [P, E, P])
        wqkv = sb("wqkv", [P, 3, P])
        maps_t, maps_bd = sb("maps_t", [HD, 2, HD]), sb("maps_bd", [P, 2, HEADS, HD])
        map_bias = sb("map_bias", [P, 2, HD])
        map_bias_all = sb("map_bias_all", [P, 2, HEADS, HD])
        wcomb = sb("wcomb", [P, 3 * P])
        wout1, wout1_t = sb("wout1", [P, P]), sb("wout1_t", [P, P])
        bn_g, bn_b = sb("bn_g", [P, 1]), sb("bn_b", [P, 1])
        upw, down_t = sb("upw", [P, EH, P]), sb("down_t", [P, EH, P])
        keysim = sb("keysim", [P, SETS, NK])
        x3t = sb("x3t", [P, B * N])
        x3 = sb("x3", [P, B * T, P])
        bn_raw = sb("bn_raw", [P, B, 6])
        bn_mv, bn_scale = sb("bn_mv", [P, 2]), sb("bn_scale", [P, 1])
        xall = sb("xall", [P, B * T, P])
        rel_row = nc.dram_tensor("rel_row", [2 * GROUP], F32, kind="Internal").ap()

        loaded = {n: sem("ld_" + n) for n in ("l0", "moe", "l1", "bn", "rel", "hankel", "peer", "keys")}
        x_in = sem("x_in", 16)
        consts, consts_lo = sem("consts"), sem("consts_lo")
        dset = sem("dve_setup")
        setup_mm, setup_cp = sem("setup_mm"), sem("setup_cp")

        load_count = {}

        def load(eng, group, dst, src):
            load_count[group] = load_count.get(group, 0) + 1
            eng.dma_start(dst, src, allow_slow_non_contiguous=True).then_inc(loaded[group].h, 16)

        def arrived(eng, group):
            eng.wait_ge(loaded[group].h, 16 * load_count[group])

        def col(v):
            return v.rearrange("(p a) -> p a", a=1)

        def rows(v, n=P):
            return bass.AP(v.tensor, v.offset, [[0, n]] + [list(s) for s in v.ap])

        def bc(ap, shape):
            return ap.broadcast_to(shape)

        setup_sb = ExitStack()
        wqn = setup_sb.enter_context(nc.sbuf_tensor("wqn", [P, SETS, P], F32))
        keysn = setup_sb.enter_context(nc.sbuf_tensor("keysn", [P, 2, 2, KD], F32))
        keys_t = setup_sb.enter_context(nc.sbuf_tensor("keys_t", [P, 2, 2, P], F32))
        downn = setup_sb.enter_context(nc.sbuf_tensor("downn", [P, EH, P], F32))
        iota_u = setup_sb.enter_context(nc.sbuf_tensor("iota_u", [P, P], F32))

        with nc.Block() as block:
            @block.sync
            def _(sp):
                for pos, n, first, step in bucket_runs(GROUP):
                    dst = rel_row[pos:pos + n]
                    src = bass.AP(rel_emb.tensor, rel_emb.offset + first, [[step, n], [1, 1]])
                    load(sp, "rel", dst.rearrange("(n a) -> n a", a=1), src)
                for b in range(B):
                    sp.dma_start(xall[:, T * b:T * b + T, :], x[b].rearrange("(t p) d -> p t d", p=P))\
                        .then_inc(x_in.h, 16)
                arrived(sp, "rel")
                load(sp, "hankel", hankel[:], bass.AP(rel_row.tensor, rel_row.offset, [[1, GROUP], [1, GROUP]]))
                load(sp, "l0", g_col[:], col(ln_g))
                load(sp, "l0", b_col[:], col(ln_b))
                load(sp, "l0", wqk[:], W_qk)
                load(sp, "l0", wh[:], W_h)
                load(sp, "l0", bqk_col[:], col(b_qk))
                load(sp, "l0", bh_gate[:], b_h[HID:2 * HID].rearrange("(c p) -> p c", p=P))
                load(sp, "l0", bh_v[:], rows(b_h[0:HID]))
                load(sp, "l0", gam[:], os_gamma.rearrange("h p -> p h"))
                load(sp, "l0", bet[:], os_beta.rearrange("h p -> p h"))
                load(sp, "l0", wout0[:], W_out.rearrange("(c p) n -> p c n", p=P))
                load(sp, "l0", bout[:], rows(b_out))
                load(sp, "moe", wg[:], Wg)
                load(sp, "moe", we[:], We.rearrange("e d m -> d e m"))

            @block.scalar
            def _(act):
                load(act, "l1", wqkv[:], w_qkv.rearrange("(i p) d -> p i d", p=P))
                for i, (w, bias) in enumerate(((wq_map, bq_map), (wk_map, bk_map))):
                    load(act, "l1", maps_t[:, i, :], w.rearrange("e d -> d e"))
                    load(act, "l1", map_bias[:, i, :], rows(bias))
                load(act, "l1", wout1[:], w_out)
                load(act, "keys", wqn[:], w_q.rearrange("(s p) d -> p s d", p=P))
                load(act, "keys", keysn[:].rearrange("p a s k -> p a (s k)"),
                     keys_p.rearrange("(a h) k s d -> (h k) a (s d)", a=2))
                load(act, "keys", downn[:], down[0:NK * NK, :].rearrange("(c p) d -> p c d", p=P))
                load(act, "peer", upw[:], up[0:NK * NK, :].rearrange("(c p) d -> p c d", p=P))
                load(act, "bn", bn_g[:], col(bn_gamma))
                load(act, "bn", bn_b[:], col(bn_beta))

            @block.gpsimd
            def _(pool):
                nc.gpsimd.memset(ident[:], 0.0)
                nc.gpsimd.memset(minus_half[:], -0.5)
                nc.gpsimd.memset(flip[:], 0.0)
                nc.gpsimd.memset(spread[:], 0.0)
                nc.gpsimd.memset(causal[:], SCORE_SCALE / FEAT_SCALE ** 2)
                nc.gpsimd.memset(same8[:], 1.0)
                nc.gpsimd.memset(same_quad[:], SCORE_SCALE / FEAT_SCALE ** 2)
                nc.gpsimd.iota(iota_u[:], pattern=[[1, P]], base=0, channel_multiplier=0,
                               allow_small_or_imprecise_dtypes=True).then_inc(consts.h, 1)
                pool.wait_ge(consts.h, 1)
                nc.gpsimd.affine_select(ident[:], ident[:], pattern=[[-1, P]], compare_op=ALU.not_equal, fill=1.0,
                                        base=0, channel_multiplier=1)
                nc.gpsimd.affine_select(flip[:].rearrange("p (g j) -> p g j", j=GROUP),
                                        flip[:].rearrange("p (g j) -> p g j", j=GROUP),
                                        pattern=[[0, P // GROUP], [1, GROUP]], compare_op=ALU.not_equal, fill=1.0,
                                        base=1 - GROUP, channel_multiplier=1)
                nc.gpsimd.affine_select(spread[:].rearrange("p (h d) -> p h d", d=HD),
                                        spread[:].rearrange("p (h d) -> p h d", d=HD),
                                        pattern=[[0, HEADS], [-1, HD]], compare_op=ALU.not_equal, fill=1.0,
                                        base=0, channel_multiplier=1)
                nc.gpsimd.affine_select(causal[:], causal[:], pattern=[[1, P]], compare_op=ALU.is_ge, fill=0.0,
                                        base=0, channel_multiplier=-1)
                nc.gpsimd.affine_select(same8[:], same8[:], pattern=[[-HD, HEADS], [0, HD]], compare_op=ALU.is_ge,
                                        fill=0.0, base=0, channel_multiplier=1)
                nc.gpsimd.affine_select(same_quad[:], same_quad[:], pattern=[[-32, 4]], compare_op=ALU.is_ge,
                                        fill=0.0, base=0, channel_multiplier=1).then_inc(consts.h, 1)
                pool.wait_ge(consts.h, 2)
                nc.gpsimd.affine_select(same8[:], same8[:], pattern=[[HD, HEADS], [0, HD]], compare_op=ALU.is_ge,
                                        fill=0.0, base=HD - 1, channel_multiplier=-1)
                nc.gpsimd.affine_select(same_quad[:], same_quad[:], pattern=[[32, 4]], compare_op=ALU.is_ge,
                                        fill=0.0, base=31, channel_multiplier=-1).then_inc(consts.h, 1)
                nc.gpsimd.iota(iota_lo[:, P // 2:P, :], pattern=[[1, P // 2], [0, P]], base=P // 2, channel_multiplier=0,
                               allow_small_or_imprecise_dtypes=True).then_inc(consts_lo.h, 1)
                pool.wait_ge(consts_lo.h, 1)

            @block.vector
            def _(dve):
                nc.vector.memset(bias_t[:], MASKED).then_inc(dset.h, 1)
                dve.wait_ge(dset.h, 1)
                dve.wait_ge(consts.h, 1)
                nc.vector.tensor_copy(iota_e[:], iota_u[:, 0:E])
                nc.vector.tensor_copy(iota_k[:], iota_u[:, 0:K])
                nc.vector.tensor_copy(iota_hi[:], bc(iota_u[:, 0:EH].unsqueeze(2), [P, EH, P]))
                nc.vector.tensor_copy(iota_lo[:, 0:P // 2, :], bc(iota_u[:, 0:P // 2].unsqueeze(2), [P, P // 2, P]))\
                    .then_inc(dset.h, 1)
                dve.wait_ge(consts.h, 3)
                dve.wait_ge(setup_mm.h, 1)
                arrived(dve, "l1")
                nc.vector.tensor_copy(map_bias_all[:], bc(map_bias[:].unsqueeze(2), [P, 2, HEADS, HD]))
                for i in range(2):
                    nc.vector.tensor_tensor(maps_bd[:, i], same8[:],
                                            bc(bank[0][:, HD * i:HD * i + HD].unsqueeze(1), [P, HEADS, HD]),
                                            ALU.mult).then_inc(dset.h, 1)
                dve.wait_ge(setup_mm.h, 2)
                nc.vector.tensor_copy(wcomb[:], bank[2][:, 0:3 * P])
                nc.vector.tensor_copy(wout1_t[:], bank[2][:, 3 * P:4 * P])
                dve.wait_ge(setup_mm.h, 3)
                nc.vector.tensor_copy(keys_t[:].rearrange("p a s k -> p (a s k)"), bank[3][:]).then_inc(dset.h, 1)
                dve.wait_ge(setup_mm.h, 4)
                for c in range(2):
                    nc.vector.tensor_copy(down_t[:, 4 * c:4 * c + 4, :].rearrange("p c k -> p (c k)"), bank[4 + c][:])
                dve.wait_ge(setup_mm.h, 5)
                nc.vector.tensor_copy(keysim[:].rearrange("p s k -> p (s k)"), bank[6][:])
                dve.wait_ge(setup_mm.h, 6)
                for g in range(P // GROUP):
                    q = slice(GROUP * g, GROUP * g + GROUP)
                    ins = nc.vector.tensor_scalar(bias_t[q, q], bank[1][q, 0:GROUP], float(P ** 0.5), None, ALU.mult)
                ins.then_inc(dset.h, 1)

            @block.tensor
            def _(pe):
                pe.wait_ge(consts.h, 3)
                arrived(pe, "l1")
                for i in range(2):
                    mm = nc.tensor.matmul(bank[0][:, HD * i:HD * i + HD], spread[:], maps_t[:, i, :],
                                          start=True, stop=True)
                mm.then_inc(setup_mm.h, 1)
                pe.wait_ge(dset.h, 4)
                for i in range(2):
                    nc.tensor.matmul(bank[2][:, P * i:P * i + P], wqkv[:, i, :],
                                     maps_bd[:, i].rearrange("p h e -> p (h e)"), start=True, stop=True)
                nc.tensor.transpose(bank[2][:, 2 * P:3 * P], wqkv[:, 2, :], ident[:])
                nc.tensor.transpose(bank[2][:, 3 * P:4 * P], wout1[:], ident[:]).then_inc(setup_mm.h, 1)
                arrived(pe, "keys")
                for a in range(2):
                    for s in range(2):
                        mm = nc.tensor.transpose(bank[3][:, P * (2 * a + s):P * (2 * a + s) + P], keysn[:, a, s, :],
                                                 ident[:])
                mm.then_inc(setup_mm.h, 1)
                for c in range(EH):
                    mm = nc.tensor.transpose(bank[4 + c // 4][:, P * (c % 4):P * (c % 4) + P], downn[:, c, :], ident[:])
                mm.then_inc(setup_mm.h, 1)
                pe.wait_ge(dset.h, 5)
                for s in range(2):
                    for h in range(NH):
                        r = s * NH + h
                        mm = nc.tensor.matmul(bank[6][:, NK * r:NK * r + NK], wqn[:, r, :],
                                              keys_t[:, h // 4, s, NK * (h % 4):NK * (h % 4) + NK],
                                              start=True, stop=True)
                mm.then_inc(setup_mm.h, 1)
                arrived(pe, "hankel")
                nc.tensor.matmul(bank[1][:, 0:GROUP], flip[:], hankel[:], start=True, stop=True).then_inc(setup_mm.h, 1)
        setup_sb.close()

        shared = Shared()
        shared.B, shared.D, shared.E, shared.EC, shared.EH, shared.GROUP = B, D, E, EC, EH, GROUP
        shared.HD, shared.HEADS, shared.HID, shared.K, shared.N, shared.NH = HD, HEADS, HID, K, N, NH
        shared.NK, shared.PAIRS, shared.QUADS, shared.SETS, shared.T, shared.arrived = NK, PAIRS, QUADS, SETS, T, arrived
        shared.b_col, shared.bank, shared.bc, shared.bet, shared.bh_gate, shared.bh_v = b_col, bank, bc, bet, bh_gate, bh_v
        shared.bias_t, shared.bn_b, shared.bn_g, shared.bn_mv, shared.bn_raw, shared.bn_scale = bias_t, bn_b, bn_g, bn_mv, bn_raw, bn_scale
        shared.bout, shared.bqk_col, shared.causal, shared.down_t, shared.dset, shared.g_col = bout, bqk_col, causal, down_t, dset, g_col
        shared.gam, shared.ident, shared.iota_e, shared.iota_hi, shared.iota_k, shared.iota_lo = gam, ident, iota_e, iota_hi, iota_k, iota_lo
        shared.keysim, shared.map_bias, shared.minus_half, shared.out, shared.same_quad, shared.upw = keysim, map_bias, minus_half, out, same_quad, upw
        shared.wcomb, shared.we, shared.wg, shared.wh, shared.wout0, shared.wout1_t = wcomb, we, wg, wh, wout0, wout1_t
        shared.wqk, shared.x3, shared.x3t, shared.x_in, shared.xall = wqk, x3, x3t, x_in, xall
        shared.psum, shared.map_bias_all = psum, map_bias_all
        layers_loop(nc, shared)
        peer_loop(nc, shared)


def wait_apart(eng, spare, s, value):
    eng.wait_ge(s.h, value)
    eng.sem_inc(spare, 1)


def layer_norm(nc, dve, spare, b, own, stats, mv, rstd, src, dst, tiles, var_ok, rstd_ok, done, ready=None):
    half = tiles // 2
    for i in range(2):
        if ready:
            ready(i)
        q = slice(half * i, half * i + half)
        for u in range(half * i, half * i + half):
            nc.vector.bn_stats(stats[:, u, :], src(u)).then_inc(own.h, 1)
            own.seen += 1
        for u in range(half * i, half * i + half):
            wait_apart(dve, spare, own, own.at(b, own.seen - half + u - half * i + 1))
            ins = nc.vector.bn_aggr(mv[:, u, :], stats[:, u, :])
        ins.then_inc(own.h, 1)
        own.seen += 1
        dve.wait_ge(own.h, own.at(b, own.seen))
        nc.vector.tensor_scalar(rstd[:, q], mv[:, q, 1:2], EPS, None, ALU.add).then_inc(var_ok.h, 1)
        var_ok.seen += 1
    for i in range(2):
        dve.wait_ge(rstd_ok.h, rstd_ok.at(b, var_ok.seen - 1 + i))
        for u in range(half * i, half * i + half):
            nc.vector.tensor_scalar(dst(u), src(u), mv[:, u, 0:1], rstd[:, u, :], ALU.subtract, ALU.mult)\
                .then_inc(done.h, 1)


def layers_loop(nc, v):
    B, N, D, T, E, EC, HID = v.B, v.N, v.D, v.T, v.E, v.EC, v.HID
    HEADS, HD, QUADS, GROUP = v.HEADS, v.HD, v.QUADS, v.GROUP
    bank, psum, ident, bc, arrived = v.bank, v.psum, v.ident, v.bc, v.arrived
    Y_BANK = (2, 6, 0, 4)
    VW = HD + 1
    ctx = ExitStack()
    with ctx:
        def sb(name, shape, dt=F32):
            return ctx.enter_context(nc.sbuf_tensor(name, shape, dt))

        primed = []

        def sem(name, per=1, start=0):
            s = Sem(ctx.enter_context(nc.semaphore(name)), per, start)
            if start:
                primed.append(s)
            return s

        xres = sb("xres", [P, T, P])
        xh = sb("xh", [P, T, P])
        normed_t = sb("normed_t", [P, N])
        qk_t = sb("qk_t", [P, N])
        heads_t = sb("heads_t", [P, 4, N])
        gate_t = sb("gate_t", [P, EC, N])
        val = sb("val", [P, T, HID])
        sim = sb("sim", [P, T, P])
        attn_t = sb("attn_t", [P, T, P])
        link = sb("link", [P, T, P])
        kv = sb("kv", [P, HID])
        gated_t = sb("gated_t", [P, EC, N])
        z = sb("z", [P, T, P])
        x1 = sb("x1", [P, T, P])
        x1t = sb("x1t", [P, N])
        lmax, lsum = sb("lmax", [P, T]), sb("lsum", [P, T])
        gate = sb("gate", [P, T, E])
        top, topi, topf = sb("top", [P, T, 8]), sb("topi", [P, T, 8], U32), sb("topf", [P, T, 8])
        hit0, hit1 = sb("hit0", [P, T, E]), sb("hit1", [P, T, E])
        wexp = sb("wexp", [P, T, E])
        z2 = sb("z2", [P, T, P])
        x2 = sb("x2", [P, T, P])
        x2t = x1t
        pm = sb("pm", [P, T, 2 * HEADS, HD])
        pmax, pmin = sb("pmax", [P, T * 2 * HEADS]), sb("pmin", [P, T * 2 * HEADS])
        pe_in = sb("pe_in", [P, T * 2 * HEADS, 2, HD])
        psum_, prec = sb("psum_", [P, T * 2 * HEADS, 2]), sb("prec", [P, T * 2 * HEADS, 2])
        feat = sb("feat", [P, T, 2, HEADS, 32])
        values = sb("values", [P, T, HEADS, HD])
        vparts = sb("vparts", [P, T, HEADS, 3, VW], BF16)
        k16 = sb("k16", [P, T, HEADS, 32], F16)
        k_t = sb("k_t", [P, T, QUADS, P], F16)
        q_hi, q_lo = sb("q_hi", [P, T, QUADS, P], F16), sb("q_lo", [P, T, QUADS, P], F16)
        s_hi, s_lo = sb("s_hi", [P, 2, 4, N], F16), sb("s_lo", [P, 2, 4, N], F16)
        ident16 = sb("ident16", [P, P], F16)
        masked = (heads_t, feat[:, 0:2].rearrange("p t i h f -> p (t i h f)").rearrange("p (g n) -> p g n", g=4))
        vrest = z2
        sums = pe_in[:].rearrange("p r i d -> p (r i d)")[:, 0:T * HEADS * VW]\
            .rearrange("p (t h f) -> p t h f", t=T, f=VW)
        state = sb("state", [P, T - 1, QUADS, 4, VW])
        state_parts = sb("state_parts", [P, T - 1, QUADS, 4, 3, VW], BF16)
        part = [state_parts[:, :, :, :, i, :].rearrange("p t c g f -> p (t c g) f") for i in range(3)]
        state_flat = state[:].rearrange("p t c g f -> p (t c g) f")
        den = sb("den", [P, T, HEADS])
        y, yt, z3, x3b = xh, qk_t, z, x1
        stats, mv, rstd = sb("stats", [P, T, 6]), sb("mv", [P, T, 2]), sb("rstd", [P, T, 1])

        pads, ident16_ok = sem("pads"), sem("ident16_ok")
        xh_ok, xht_mm, normed_ok = sem("xh_ok", T), sem("xht_mm", 1), sem("normed_ok", 1)
        qk_mm, gate_mm, val_mm = sem("qk_mm", 1), sem("gate_mm", EC), sem("val_mm", 2)
        qk_ok, gate_ok, valb_ok, val_ok = sem("qk_ok", 1), sem("gate_ok", EC), sem("valb_ok", 2), sem("val_ok", 2)
        quad_ok, lin_ok = sem("quad_ok", 2, 1), sem("lin_ok", 2, 1)
        sim_mm, attn_ok = sem("sim_mm", 1), sem("attn_ok", 1)
        link_mm, link_ok, kv_mm, kv_ok = sem("link_mm", 1), sem("link_ok", 1), sem("kv_mm", 1), sem("kv_ok", 1)
        outt_mm, gated_ok, out_mm = sem("outt_mm", EC), sem("gated_ok", EC, 1), sem("out_mm", 1, 1)
        xres_ok, x1_ok = sem("xres_ok", 2), sem("x1_ok", T, 1)
        x1t_mm, x1t_ok, logit_mm = sem("x1t_mm", 1), sem("x1t_ok", 1), sem("logit_mm", 1)
        shift_ok, exp_ok = sem("shift_ok", 1), sem("exp_ok", 1)
        y_mm, y_used, x2_ok = sem("y_mm", T), sem("y_used", T), sem("x2_ok", T)
        x2t_mm, x2t_ok = sem("x2t_mm", 1), sem("x2t_ok", 1)
        qkv_mm, pm_ok, v_ok, min_ok, neg_ok = (sem("qkv_mm", T), sem("pm_ok", 2), sem("v_ok", 2), sem("min_ok", 2),
                                               sem("neg_ok", 2))
        pos_ok, fexp_ok, feat_ok = sem("pos_ok", 2), sem("fexp_ok", 2), sem("feat_ok", 2)
        v1_ok, vrest_ok, v2_ok, v3_ok = sem("v1_ok", 1), sem("vrest_ok", 1), sem("v2_ok", 1), sem("v3_ok", 1)
        twice_ok, khi_ok, k16_ok = sem("twice_ok", 2), sem("khi_ok", 2), sem("k16_ok", T)
        ft_mm, qhi_ok, qlo_ok, ft_ok = sem("ft_mm", T), sem("qhi_ok", T), sem("qlo_ok", T), sem("ft_ok", T)
        a_mm, masked_ok, shi_ok, slo_ok = sem("a_mm", 4 * T), sem("masked_ok", 4 * T), sem("shi_ok", 4 * T), sem("slo_ok", 3 * T)
        slo_dve = sem("slo_dve", T)
        sums_ok = sem("sums_ok", T)
        st1_ok, st_rest, st2_ok, st3_ok = sem("st1_ok", 1), sem("st_rest", 1), sem("st2_ok", 1), sem("st3_ok", 1)
        st_mm, st_ok, num_mm, y_ok = sem("st_mm", 1), sem("st_ok", 1), sem("num_mm", T), sem("y_ok", 1)
        yt_mm, yt_ok, z3_mm, z3_ok = sem("yt_mm", 1), sem("yt_ok", 1), sem("z3_mm", 1), sem("z3_ok", 1, 1)
        x3_ok, x3t_mm, x3t_ok = sem("x3_ok", T), sem("x3t_mm", 1), sem("x3t_ok", 1)
        bn_ok, x3_kept = sem("bn_ok", 1, 1), sem("x3_kept", 1, 1)
        var_ok, rstd_ok = sem("var_ok", 8), sem("rstd_ok", 8)
        spare = sem("spare").h
        own = sem("dve_own", 0)
        own.per = OWN_LAYERS
        pool_own = sem("pool_own", 2)

        with nc.Block() as block:
            @block.gpsimd
            def _(pool):
                for s in primed:
                    pool.sem_inc(s.h, 1)
                nc.gpsimd.memset(vparts[:], 0.0).then_inc(pads.h, 1)
                pool.wait_ge(pads.h, 1)
                nc.gpsimd.memset(vparts[:, :, :, 0, HD:VW], 1.0).then_inc(pads.h, 1)
                arrived(pool, "l0")

                def inverse_root(b, k):
                    for i in range(2):
                        q = slice(T // 2 * i, T // 2 * (i + 1))
                        wait(pool, var_ok, b, 2 * k - 1 + i)
                        nc.gpsimd.tensor_tensor(rstd[:, q], rstd[:, q], bc(v.minus_half[:].unsqueeze(1), [P, T // 2, 1]),
                                                ALU.pow).then_inc(rstd_ok.h, 1)

                with pool.Fori(0, B) as b:
                    inverse_root(b, 1)
                    wait_last(pool, x1_ok, b)
                    wait_apart(pool, spare, v.x_in, v.x_in.at(b, 16))
                    xs = v.xall[:, bass.ds(b * T, T), :]
                    nc.gpsimd.tensor_tensor(xres[:], xs, xs, ALU.add).then_inc(xres_ok.h, 1)
                    wait(pool, xres_ok, b, 1)
                    nc.gpsimd.tensor_tensor(xres[:], xres[:], bc(v.bout[:].unsqueeze(1), [P, T, P]), ALU.add)\
                        .then_inc(xres_ok.h, 1)
                    wait_last(pool, out_mm, b)
                    wait_apart(pool, spare, qk_ok, qk_ok.at(b, 1))
                    for h in (1, 3):
                        nc.gpsimd.tensor_scalar(heads_t[:, h, :], qk_t[:], v.gam[:, h:h + 1], v.bet[:, h:h + 1],
                                                ALU.mult, ALU.add).then_inc(lin_ok.h, 1)
                    for k in (2, 3):
                        inverse_root(b, k)
                    for i in range(2):
                        rows = slice(2 * HEADS * 2 * i, 2 * HEADS * 2 * (i + 1))
                        wait(pool, min_ok, b, i + 1)
                        nc.gpsimd.tensor_tensor(pe_in[:, rows, 1, :], bc(pmin[:, rows].unsqueeze(2), [P, 4 * HEADS, HD]),
                                                pm[:, 2 * i:2 * i + 2].rearrange("p t h d -> p (t h) d"),
                                                ALU.subtract).then_inc(neg_ok.h, 1)
                    wait(pool, v1_ok, b)
                    nc.gpsimd.tensor_tensor(vrest[:].rearrange("p t (h d) -> p t h d", d=HD), values[:],
                                            vparts[:, :, :, 0, 0:HD], ALU.subtract).then_inc(vrest_ok.h, 1)
                    wait(pool, v2_ok, b)
                    nc.gpsimd.tensor_tensor(vparts[:, :, :, 2, 0:HD], vrest[:].rearrange("p t (h d) -> p t h d", d=HD),
                                            vparts[:, :, :, 1, 0:HD], ALU.subtract).then_inc(v3_ok.h, 1)
                    for u in range(T):
                        for g in range(1, 4):
                            wait(pool, shi_ok, b, 4 * u + g + 1)
                            nc.gpsimd.tensor_tensor(s_lo[:, u % 2, g, :], masked[u % 2][:, g, :], s_hi[:, u % 2, g, :],
                                                    ALU.subtract).then_inc(slo_ok.h, 1)
                        if u == 0:
                            wait(pool, st1_ok, b)
                            nc.gpsimd.tensor_tensor(state_flat, state_flat, part[0], ALU.subtract)\
                                .then_inc(st_rest.h, 1)
                            wait(pool, st2_ok, b)
                            nc.gpsimd.tensor_tensor(part[2], state_flat, part[1], ALU.subtract).then_inc(st3_ok.h, 1)
                    inverse_root(b, 4)
                    wait_apart(pool, spare, x3_ok, x3_ok.at(b, T))
                    nc.gpsimd.tensor_copy(v.x3[:, bass.ds(b * T, T), :], x3b[:]).then_inc(x3_kept.h, 1)

            @block.scalar
            def _(act):
                nc.scalar.copy(ident16[:], ident[:]).then_inc(ident16_ok.h, 1)
                act.wait_ge(pads.h, 2)
                arrived(act, "l0")
                with act.Fori(0, B) as b:
                    wait(act, xht_mm, b)
                    nc.scalar.activation(normed_t[:], bank[0][:], ACT.Identity, bias=v.b_col[:], scale=v.g_col[:])\
                        .then_inc(normed_ok.h, 1)
                    wait(act, qk_mm, b)
                    wait_last(act, lin_ok, b)
                    wait_last(act, quad_ok, b)
                    nc.scalar.activation(qk_t[:], bank[1][:], ACT.Silu, bias=v.bqk_col[:]).then_inc(qk_ok.h, 1)
                    wait_last(act, gated_ok, b)
                    for c in range(EC):
                        wait(act, gate_mm, b, c + 1)
                        nc.scalar.activation(gate_t[:, c, :], bank[2 + c][:], ACT.Silu, bias=v.bh_gate[:, c:c + 1])\
                            .then_inc(gate_ok.h, 1)
                    for i in range(2):
                        wait(act, valb_ok, b, i + 1)
                        nc.scalar.activation(val[:, 2 * i:2 * i + 2, :], val[:, 2 * i:2 * i + 2, :], ACT.Silu)\
                            .then_inc(val_ok.h, 1)
                    wait(act, link_mm, b)
                    nc.scalar.copy(link[:].rearrange("p t d -> p (t d)"), bank[7][:]).then_inc(link_ok.h, 1)
                    wait(act, kv_mm, b)
                    nc.scalar.mul(kv[:], bank[0][:, 0:HID], 1.0 / N).then_inc(kv_ok.h, 1)
                    wait(act, x1t_mm, b)
                    nc.scalar.copy(x1t[:], bank[4][:]).then_inc(x1t_ok.h, 1)
                    wait(act, shift_ok, b)
                    nc.scalar.activation(gate[:], gate[:], ACT.Exp).then_inc(exp_ok.h, 1)
                    wait(act, x2t_mm, b)
                    nc.scalar.copy(x2t[:], bank[4][:]).then_inc(x2t_ok.h, 1)
                    for i in range(2):
                        wait(act, pm_ok, b, i + 1)
                        nc.scalar.copy(values[:, 2 * i:2 * i + 2],
                                       psum[:, 2 * i:2 * i + 2, 2 * P:3 * P].rearrange("p t (h d) -> p t h d", d=HD))\
                            .then_inc(v_ok.h, 1)
                    wait(act, v_ok, b)
                    nc.scalar.copy(vparts[:, :, :, 0, 0:HD], values[:]).then_inc(v1_ok.h, 1)
                    for i in range(2):
                        rows = slice(4 * HEADS * i, 4 * HEADS * (i + 1))
                        wait(act, pos_ok, b, i + 1)
                        wait(act, neg_ok, b, i + 1)
                        nc.scalar.activation(pe_in[:, rows], pe_in[:, rows], ACT.Exp).then_inc(fexp_ok.h, 1)
                    for i in range(2):
                        tiles = slice(2 * i, 2 * i + 2)
                        wait(act, feat_ok, b, i + 1)
                        nc.scalar.mul(k16[:, tiles, :, 0:2 * HD], feat[:, tiles, 1, :, 0:2 * HD], FEAT_SCALE)\
                            .then_inc(khi_ok.h, 1)
                        nc.scalar.copy(feat[:, tiles, 0, :, 2 * HD:4 * HD], feat[:, tiles, 0, :, 0:2 * HD])\
                            .then_inc(twice_ok.h, 1)
                        if i:
                            wait(act, vrest_ok, b)
                            nc.scalar.copy(vparts[:, :, :, 1, 0:HD], vrest[:].rearrange("p t (h d) -> p t h d", d=HD))\
                                .then_inc(v2_ok.h, 1)
                        for u in (2 * i, 2 * i + 1):
                            wait(act, ft_mm, b, u + 1)
                            q = 4 + 2 * (u % 2)
                            nc.scalar.mul(q_hi[:, u].rearrange("p c t -> p (c t)"), bank[q], FEAT_SCALE)\
                                .then_inc(qhi_ok.h, 1)
                            nc.scalar.copy(k_t[:, u].rearrange("p c t -> p (c t)"), bank[q + 1]).then_inc(ft_ok.h, 1)
                    for u in range(T):
                        for g in range(4):
                            wait(act, masked_ok, b, 4 * u + g + 1)
                            if u >= 2 and g == 0:
                                wait(act, num_mm, b, u - 1)
                            nc.scalar.copy(s_hi[:, u % 2, g, :], masked[u % 2][:, g, :]).then_inc(shi_ok.h, 1)
                        if u == 0:
                            wait(act, st_ok, b)
                            nc.scalar.copy(part[0], state_flat).then_inc(st1_ok.h, 1)
                            wait(act, st_rest, b)
                            nc.scalar.copy(part[1], state_flat).then_inc(st2_ok.h, 1)
                    wait(act, yt_mm, b)
                    nc.scalar.copy(yt[:], bank[2]).then_inc(yt_ok.h, 1)
                    wait(act, x3t_mm, b)
                    nc.scalar.copy(v.x3t[:, bass.ds(b * N, N)], bank[4][:]).then_inc(x3t_ok.h, 1)

            @block.vector
            def _(dve):
                def step(ins, plain=False):
                    ins.then_inc(own.h, 1)
                    own.seen += 1
                    if plain:
                        wait_apart(dve, spare, own, own.at(bb, own.seen))
                    else:
                        dve.wait_ge(own.h, own.at(bb, own.seen))

                def norm(src, dst, done):
                    layer_norm(nc, dve, spare, bb, own, stats, mv, rstd, src, dst, T, var_ok, rstd_ok, done)

                arrived(dve, "l0")
                arrived(dve, "l1")
                dve.wait_ge(v.dset.h, 6)
                with dve.Fori(0, B) as b:
                    bb = b
                    own.seen = var_ok.seen = 0
                    wait_apart(dve, spare, v.x_in, v.x_in.at(b, 16))
                    norm(lambda u: v.xall[:, bass.ds(b * T + u, 1), :].rearrange("p a d -> p (a d)"),
                         lambda u: xh[:, u, :], xh_ok)
                    for i in range(2):
                        wait(dve, val_mm, b, i + 1)
                        nc.vector.tensor_tensor(val[:, 2 * i:2 * i + 2, :],
                                                bank[4 + i][:].rearrange("p (t e) -> p t e", t=2),
                                                bc(v.bh_v[:].unsqueeze(1), [P, 2, HID]), ALU.add)\
                            .then_inc(valb_ok.h, 1)
                    wait(dve, qk_ok, b)
                    for h in (0, 2):
                        nc.vector.tensor_scalar(heads_t[:, h, :], qk_t[:], v.gam[:, h:h + 1], v.bet[:, h:h + 1],
                                                ALU.mult, ALU.add).then_inc(quad_ok.h, 1)
                    wait(dve, sim_mm, b)
                    step(nc.vector.scalar_tensor_tensor(sim[:], bank[6][:].rearrange("p (t i) -> p t i", t=T),
                                                        1.0 / GROUP, bc(v.bias_t[:].unsqueeze(1), [P, T, P]),
                                                        ALU.mult, ALU.add))
                    nc.vector.scalar_tensor_tensor(attn_t[:], sim[:], 0.0, sim[:], ALU.max, ALU.mult)\
                        .then_inc(attn_ok.h, 1)
                    for c in range(EC):
                        wait(dve, outt_mm, b, c + 1)
                        wait(dve, gate_ok, b, c + 1)
                        nc.vector.tensor_tensor(gated_t[:, c, :], gate_t[:, c, :], bank[(1, 7)[c]][:], ALU.mult)\
                            .then_inc(gated_ok.h, 1)
                    wait(dve, out_mm, b)
                    wait(dve, xres_ok, b)
                    step(nc.vector.tensor_tensor(z[:], bank[0][:].rearrange("p (t d) -> p t d", t=T), xres[:],
                                                 ALU.add))
                    norm(lambda u: z[:, u, :], lambda u: x1[:, u, :], x1_ok)

                    wait(dve, logit_mm, b)
                    logits = bank[5][:, 0:T * E].rearrange("p (t e) -> p t e", t=T)
                    step(nc.vector.tensor_reduce(lmax[:], logits, X, ALU.max))
                    nc.vector.tensor_tensor(gate[:], logits, bc(lmax[:].unsqueeze(2), [P, T, E]), ALU.subtract)\
                        .then_inc(shift_ok.h, 1)
                    wait(dve, exp_ok, b)
                    step(nc.vector.tensor_reduce(lsum[:], gate[:], X, ALU.add))
                    step(nc.vector.reciprocal(lsum[:], lsum[:]))
                    step(nc.vector.tensor_tensor(gate[:], gate[:], bc(lsum[:].unsqueeze(2), [P, T, E]), ALU.mult), True)
                    for u in range(T):
                        ins = nc.vector.max(top[:, u, :], gate[:, u, :])
                    step(ins, True)
                    for u in range(T):
                        ins = nc.vector.max_index(topi[:, u, :], top[:, u, :], gate[:, u, :])
                    step(ins)
                    nc.vector.tensor_copy(topf[:], topi[:])
                    step(nc.vector.tensor_tensor(lsum[:], top[:, :, 0], top[:, :, 1], ALU.add))
                    step(nc.vector.tensor_scalar(lsum[:], lsum[:], 1e-9, None, ALU.add))
                    nc.vector.reciprocal(lsum[:], lsum[:])
                    iota = bc(v.iota_e[:].unsqueeze(1), [P, T, E])
                    for j, hit in ((0, hit0), (1, hit1)):
                        ins = nc.vector.tensor_tensor(hit[:], iota, bc(topf[:, :, j:j + 1], [P, T, E]), ALU.is_equal)
                    step(ins)
                    for j, hit in ((0, hit0), (1, hit1)):
                        ins = nc.vector.tensor_tensor(hit[:], hit[:], bc(top[:, :, j:j + 1], [P, T, E]), ALU.mult)
                    step(ins)
                    step(nc.vector.tensor_tensor(hit0[:], hit0[:], hit1[:], ALU.add))
                    step(nc.vector.tensor_tensor(wexp[:], hit0[:], bc(lsum[:].unsqueeze(2), [P, T, E]), ALU.mult), True)
                    for p in range(T // 2):
                        for e in range(E):
                            for t in range(2):
                                u = 2 * p + t
                                if e == 0:
                                    wait(dve, y_mm, b, u + 1)
                                else:
                                    after = 0 if e == E - 1 and t == 1 else 1
                                    dve.wait_ge(own.h, own.at(b, own.seen - after))
                                src = bank[Y_BANK[u] + e // 4][:, P * (e % 4):P * (e % 4) + P]
                                ins = nc.vector.scalar_tensor_tensor(z2[:, u, :], src, wexp[:, u, e:e + 1],
                                                                     (z2 if e else x1)[:, u, :], ALU.mult, ALU.add)
                                if e < E - 1:
                                    ins.then_inc(own.h, 1)
                                    own.seen += 1
                                else:
                                    ins.then_inc(y_used.h, 1)
                    wait(dve, y_used, b)
                    norm(lambda u: z2[:, u, :], lambda u: x2[:, u, :], x2_ok)

                    for i in range(2):
                        wait(dve, qkv_mm, b, 2 * i + 2)
                        nc.vector.tensor_tensor(
                            pm[:, 2 * i:2 * i + 2].rearrange("p t h d -> p t (h d)"), psum[:, 2 * i:2 * i + 2, 0:2 * P],
                            bc(v.map_bias_all[:].rearrange("p i h d -> p (i h d)").unsqueeze(1), [P, 2, 2 * P]),
                            ALU.add).then_inc(pm_ok.h, 1)
                    for i in range(2):
                        rows = slice(4 * HEADS * i, 4 * HEADS * (i + 1))
                        half = pm[:, 2 * i:2 * i + 2].rearrange("p t h d -> p (t h) d")
                        wait(dve, pm_ok, b, i + 1)
                        nc.vector.tensor_reduce(pmin[:, rows], half, X, ALU.min).then_inc(min_ok.h, 1)
                        step(nc.vector.tensor_reduce(pmax[:, rows], half, X, ALU.max))
                        nc.vector.tensor_tensor(pe_in[:, rows, 0, :], half,
                                                bc(pmax[:, rows].unsqueeze(2), [P, 4 * HEADS, HD]),
                                                ALU.subtract).then_inc(pos_ok.h, 1)
                    def low_q(u):
                        wait(dve, qhi_ok, b, u + 1)
                        nc.vector.scalar_tensor_tensor(
                            q_lo[:, u].rearrange("p c t -> p (c t)"), bank[4 + 2 * (u % 2)], FEAT_SCALE,
                            q_hi[:, u].rearrange("p c t -> p (c t)"), ALU.mult, ALU.subtract).then_inc(qlo_ok.h, 1)

                    for i in range(2):
                        rows = slice(4 * HEADS * i, 4 * HEADS * (i + 1))
                        wait(dve, fexp_ok, b, i + 1)
                        step(nc.vector.tensor_reduce(psum_[:, rows], pe_in[:, rows], X, ALU.add))
                        step(nc.vector.reciprocal(prec[:, rows], psum_[:, rows]))
                        nc.vector.tensor_tensor(
                            feat[:].rearrange("p t i h (s f) -> p (t i h) s f", s=4)[:, rows, 0:2, :],
                            pe_in[:, rows], bc(prec[:, rows].unsqueeze(3), [P, 4 * HEADS, 2, HD]), ALU.mult)\
                            .then_inc(feat_ok.h, 1)
                        for u in (range(2) if i else ()):
                            low_q(u)
                        wait(dve, khi_ok, b, i + 1)
                        for u in (2 * i, 2 * i + 1):
                            nc.vector.scalar_tensor_tensor(
                                k16[:, u, :, 2 * HD:4 * HD], feat[:, u, 1, :, 0:2 * HD], FEAT_SCALE,
                                k16[:, u, :, 0:2 * HD], ALU.mult, ALU.subtract).then_inc(k16_ok.h, 1)
                    for u in range(2, T):
                        low_q(u)

                    def states():
                        wait(dve, st_mm, b)
                        for u in range(T - 1):
                            ins = nc.vector.tensor_reduce(
                                state[:, u].rearrange("p c g f -> p (c g) f"),
                                bank[u + 1][:, 0:HEADS * 3 * VW].rearrange("p (h a f) -> p h f a", a=3, f=VW),
                                X, ALU.add)
                        step(ins)
                        step(nc.vector.tensor_tensor(
                            state[:].rearrange("p t c g f -> p (t c) g f"),
                            state[:].rearrange("p t c g f -> p (t c) g f"),
                            bc(v.same_quad[:].unsqueeze(1).unsqueeze(3), [P, (T - 1) * QUADS, 4, VW]), ALU.mult))
                        for u in range(1, T - 1):
                            ins = nc.vector.tensor_tensor(state[:, u], state[:, u], state[:, u - 1], ALU.add)
                            if u < T - 2:
                                step(ins)
                        ins.then_inc(st_ok.h, 1)

                    def summed(u):
                        wait(dve, num_mm, b, u + 1)
                        nc.vector.tensor_reduce(
                            sums[:, u], bank[u][:, 0:HEADS * 3 * VW].rearrange("p (h a f) -> p h f a", a=3, f=VW),
                            X, ALU.add).then_inc(sums_ok.h, 1)

                    for u in range(T):
                        for g in range(4):
                            wait(dve, a_mm, b, 4 * u + g + 1)
                            if u >= 2 and g == 0:
                                wait(dve, slo_dve, b, u - 1)
                            elif u >= 2:
                                wait(dve, slo_ok, b, 3 * (u - 2) + g)
                            nc.vector.tensor_tensor(
                                masked[u % 2][:, g, :].rearrange("p (c t) -> p c t", c=QUADS),
                                bank[4 + g].rearrange("p (c t) -> p c t", c=QUADS),
                                bc(v.causal[:].unsqueeze(1), [P, QUADS, P]), ALU.mult).then_inc(masked_ok.h, 1)
                        wait(dve, shi_ok, b, 4 * u + 1)
                        nc.vector.tensor_tensor(s_lo[:, u % 2, 0, :], masked[u % 2][:, 0, :], s_hi[:, u % 2, 0, :],
                                                ALU.subtract).then_inc(slo_dve.h, 1)
                        if u == 0:
                            states()
                        if u:
                            summed(u - 1)
                    summed(T - 1)
                    wait(dve, sums_ok, b)
                    step(nc.vector.tensor_scalar(den[:], sums[:, :, :, HD], 1e-6 * SCORE_SCALE, None, ALU.max))
                    step(nc.vector.reciprocal(den[:], den[:]))
                    nc.vector.tensor_tensor(y[:].rearrange("p t (h d) -> p t h d", d=HD), sums[:, :, :, 0:HD],
                                            bc(den[:].unsqueeze(3), [P, T, HEADS, HD]), ALU.mult)\
                        .then_inc(y_ok.h, 1)
                    wait(dve, z3_mm, b)
                    nc.vector.tensor_tensor(z3[:], x2[:], bank[3].rearrange("p (t d) -> p t d", t=T), ALU.add)\
                        .then_inc(z3_ok.h, 1)
                    wait(dve, z3_ok, b)
                    wait_last(dve, x3_kept, b)
                    norm(lambda u: z3[:, u, :], lambda u: x3b[:, u, :], x3_ok)
                    wait_apart(dve, spare, x3t_ok, x3t_ok.at(b, 1))
                    nc.vector.bn_stats(v.bn_raw[:, bass.ds(b, 1), :].rearrange("p a s -> p (a s)"), bank[4][:])\
                        .then_inc(bn_ok.h, 1)
                assert own.seen == own.per, own.seen

            @block.tensor
            def _(pe):
                arrived(pe, "l0")
                arrived(pe, "moe")
                pe.wait_ge(ident16_ok.h, 1)
                pe.wait_ge(v.dset.h, 6)
                with pe.Fori(0, B) as b:
                    wait_last(pe, z3_ok, b)
                    wait_last(pe, bn_ok, b)
                    for u in range(T):
                        wait(pe, xh_ok, b, u + 1)
                        ins = nc.tensor.transpose(bank[0][:, P * u:P * u + P], xh[:, u, :], ident[:])
                    ins.then_inc(xht_mm.h, 1)
                    wait(pe, normed_ok, b)
                    nc.tensor.matmul(bank[1][:], v.wqk[:], normed_t[:], start=True, stop=True).then_inc(qk_mm.h, 1)
                    for i in range(2):
                        for u in (2 * i, 2 * i + 1):
                            ins = nc.tensor.matmul(bank[4 + i][:, HID * (u % 2):HID * (u % 2) + HID],
                                                   normed_t[:, P * u:P * u + P], v.wh[:, 0:HID], start=True, stop=True)
                        ins.then_inc(val_mm.h, 1)
                    for c in range(EC):
                        nc.tensor.matmul(bank[2 + c][:], v.wh[:, HID + P * c:HID + P * c + P], normed_t[:],
                                         start=True, stop=True).then_inc(gate_mm.h, 1)
                    wait(pe, quad_ok, b)
                    for u in range(T):
                        q = slice(P * u, P * u + P)
                        ins = nc.tensor.matmul(bank[6][:, q], heads_t[:, 2, q], heads_t[:, 0, q], start=True, stop=True)
                    ins.then_inc(sim_mm.h, 1)
                    wait(pe, lin_ok, b)
                    for u in range(T):
                        q = slice(P * u, P * u + P)
                        ins = nc.tensor.transpose(bank[7][:, q], heads_t[:, 3, q], ident[:])
                    ins.then_inc(link_mm.h, 1)
                    wait(pe, link_ok, b)
                    wait(pe, val_ok, b)
                    for u in range(T):
                        ins = nc.tensor.matmul(bank[0][:, 0:HID], link[:, u, :], val[:, u, :],
                                               start=(u == 0), stop=(u == T - 1))
                    ins.then_inc(kv_mm.h, 1)
                    wait(pe, kv_ok, b)
                    wait(pe, attn_ok, b)
                    for c in range(EC):
                        o = bank[(1, 7)[c]]
                        for u in range(T):
                            nc.tensor.matmul(o[:, P * u:P * u + P], val[:, u, P * c:P * c + P], attn_t[:, u, :],
                                             start=(u == 0), stop=False, skip_group_check=True)
                        ins = nc.tensor.matmul(o[:], kv[:, P * c:P * c + P], heads_t[:, 1, :], start=False, stop=True,
                                               skip_group_check=True)
                        ins.then_inc(outt_mm.h, 1)
                    wait(pe, gated_ok, b)
                    for u in range(T):
                        for c in range(EC):
                            ins = nc.tensor.matmul(bank[0][:, P * u:P * u + P], gated_t[:, c, P * u:P * u + P],
                                                   v.wout0[:, c, :], start=(c == 0), stop=(c == EC - 1))
                    ins.then_inc(out_mm.h, 1)

                    for u in range(T):
                        wait(pe, x1_ok, b, u + 1)
                        ins = nc.tensor.transpose(bank[4][:, P * u:P * u + P], x1[:, u, :], ident[:])
                    ins.then_inc(x1t_mm.h, 1)
                    wait(pe, x1t_ok, b)
                    for u in range(T):
                        ins = nc.tensor.matmul(bank[5][:, E * u:E * u + E], x1t[:, P * u:P * u + P], v.wg[:],
                                               start=True, stop=True)
                    ins.then_inc(logit_mm.h, 1)
                    for u in range(T):
                        if u == T - 1:
                            wait(pe, shift_ok, b)
                        for k in range(2):
                            ins = nc.tensor.matmul(bank[Y_BANK[u] + k][:], x1t[:, P * u:P * u + P],
                                                   v.we[:, 4 * k:4 * k + 4, :].rearrange("p e m -> p (e m)"),
                                                   start=True, stop=True)
                        ins.then_inc(y_mm.h, 1)

                    for u in range(T):
                        wait(pe, x2_ok, b, u + 1)
                        ins = nc.tensor.transpose(bank[4][:, P * u:P * u + P], x2[:, u, :], ident[:])
                    ins.then_inc(x2t_mm.h, 1)
                    wait(pe, x2t_ok, b)
                    for u in range(T):
                        nc.tensor.matmul(bank[u][:, 0:3 * P], x2t[:, P * u:P * u + P], v.wcomb[:],
                                         start=True, stop=True).then_inc(qkv_mm.h, 1)
                    for u in range(T):
                        if u % 2 == 0:
                            wait(pe, twice_ok, b, u // 2 + 1)
                        if u >= 2:
                            wait(pe, ft_ok, b, u - 1)
                            wait(pe, qlo_ok, b, u - 1)
                        q = 4 + 2 * (u % 2)
                        for c in range(QUADS):
                            nc.tensor.transpose(bank[q][:, P * c:P * c + P],
                                                feat[:, u, 0, 4 * c:4 * c + 4, :].rearrange("p h f -> p (h f)"),
                                                ident[:])
                        wait(pe, k16_ok, b, u + 1)
                        for c in range(QUADS):
                            ins = nc.tensor.matmul(bank[q + 1][:, P * c:P * c + P],
                                                   k16[:, u, 4 * c:4 * c + 4, :].rearrange("p h f -> p (h f)"),
                                                   ident16[:], start=True, stop=True)
                        ins.then_inc(ft_mm.h, 1)
                    def products():
                        wait(pe, v3_ok, b)
                        for u in range(T - 1):
                            for c in range(QUADS):
                                at = 4 * 3 * VW * c
                                ins = nc.tensor.matmul(bank[u + 1][:, at:at + 4 * 3 * VW],
                                                       k16[:, u, 4 * c:4 * c + 4, :].rearrange("p h f -> p (h f)"),
                                                       vparts[:, u, 4 * c:4 * c + 4].rearrange("p h a f -> p (h a f)"),
                                                       start=True, stop=True)
                        ins.then_inc(st_mm.h, 1)

                    def scores(u):
                        if u == 0:
                            wait(pe, ft_ok, b)
                            wait(pe, qlo_ok, b)
                        for g in range(4):
                            if u:
                                wait(pe, masked_ok, b, 4 * (u - 1) + g + 1)
                            r = slice(32 * g, 32 * g + 32)
                            for c in range(QUADS):
                                for q in (q_hi, q_lo):
                                    ins = nc.tensor.matmul(bank[4 + g][:, P * c:P * c + P], k_t[r, u, c, :],
                                                           q[r, u, c, :], start=(q is q_hi), stop=(q is q_lo))
                            ins.then_inc(a_mm.h, 1)

                    def numerators(u):
                        first = True
                        if u:
                            if u == 1:
                                wait(pe, st3_ok, b)
                            for c in range(QUADS):
                                at = 4 * 3 * VW * c
                                for q in (q_hi, q_lo):
                                    nc.tensor.matmul(bank[u][:, at:at + 4 * 3 * VW], q[:, u, c, :],
                                                     state_parts[:, u - 1, c].rearrange("p g a f -> p (g a f)"),
                                                     start=first, stop=False, skip_group_check=True)
                                    first = False
                        wait(pe, slo_dve, b, u + 1)
                        wait(pe, slo_ok, b, 3 * u + 3)
                        for g in range(4):
                            for c in range(QUADS):
                                h, q = 4 * c + g, slice(P * c, P * c + P)
                                at = 3 * VW * h
                                nc.tensor.matmul(bank[u][:, at:at + 2 * VW], s_lo[:, u % 2, g, q],
                                                 vparts[:, u, h, 0:2, :].rearrange("p a f -> p (a f)"),
                                                 start=first, stop=False, skip_group_check=True)
                                first = False
                                ins = nc.tensor.matmul(bank[u][:, at:at + 3 * VW], s_hi[:, u % 2, g, q],
                                                       vparts[:, u, h].rearrange("p a f -> p (a f)"),
                                                       start=False, stop=True, skip_group_check=True)
                        ins.then_inc(num_mm.h, 1)

                    scores(0)
                    products()
                    for u in range(T):
                        if u < T - 1:
                            scores(u + 1)
                        numerators(u)
                    wait(pe, y_ok, b)
                    for u in range(T):
                        ins = nc.tensor.transpose(bank[2][:, P * u:P * u + P], y[:, u, :], ident[:])
                    ins.then_inc(yt_mm.h, 1)
                    wait(pe, yt_ok, b)
                    for u in range(T):
                        ins = nc.tensor.matmul(bank[3][:, P * u:P * u + P], yt[:, P * u:P * u + P], v.wout1_t[:],
                                               start=True, stop=True)
                    ins.then_inc(z3_mm.h, 1)
                    for u in range(T):
                        wait(pe, x3_ok, b, u + 1)
                        ins = nc.tensor.transpose(
                            bank[4][:, P * u:P * u + P], x3b[:, u, :], ident[:])
                    ins.then_inc(x3t_mm.h, 1)


OWN_LAYERS = 77
OWN_PEER = 30


def peer_loop(nc, v):
    B, N, T, NH, NK, K, SETS, EH, PAIRS = v.B, v.N, v.T, v.NH, v.NK, v.K, v.SETS, v.EH, v.PAIRS
    bank, ident, bc, arrived = v.bank, v.ident, v.bc, v.arrived
    HK = NH * K
    LB = 512 // (2 * EH)
    QB = P // LB
    ctx = ExitStack()
    with ctx:
        def sb(name, shape, dt=F32):
            return ctx.enter_context(nc.sbuf_tensor(name, shape, dt))

        primed = []

        def sem(name, per=1, start=0):
            s = Sem(ctx.enter_context(nc.semaphore(name)), per, start)
            if start:
                primed.append(s)
            return s

        normed, xn = sb("normed", [P, B * N]), sb("xn", [P, N])
        keysims = sb("keysims", [P, T, SETS, NK])
        side, side_i = sb("side", [P, T, SETS, K]), sb("side_i", [P, T, SETS, K], U32)
        side_f = sb("side_f", [P, T, SETS, K])
        cand = sb("cand", [P, 2, NH, K, K])
        best, best_i = sb("best", [P, T, NH, K]), sb("best_i", [P, 2, NH, K], U32)
        rc = sb("rc", [P, 2, 2, HK], U32)
        eq = sb("eq", [P, 2, SETS, K, K])
        dec = sb("dec", [P, SETS, K])
        e_num, lohi = sb("e_num", [P, HK], U32), sb("lohi", [P, T, 2, HK], U32)
        comp = sb("comp", [P, PAIRS, 3, 2, HK])
        lh_t = sb("lh_t", [P, 2, P], F16)
        w_t = sb("w_t", [P, P])
        w_hi, w_lo = sb("w_hi", [P, P], F16), sb("w_lo", [P, P], F16)
        hot_lo = sb("hot_lo", [P, P, P], F16)
        hot_hi = sb("hot_hi", [P, EH, P], F16)
        hot_w = sb("hot_w", [P, 2, 2, EH, P], F16)
        hid = sb("hid", [P, T, EH, P])
        mix = sb("mix", [P, 2 * EH, P])
        z4, o4 = sb("z4", [P, T, P]), sb("o4", [P, T, P])
        stats, mv, rstd = sb("stats4", [P, T, 6]), sb("mv4", [P, T, 2]), sb("rstd4", [P, T, 1])
        bn_inv = sb("bn_inv", [P, 1])

        bn_var, bn_pow, bn_done = sem("bn_var"), sem("bn_pow"), sem("bn_done")
        zeroed = sem("zeroed")
        xn_ok, xn_sub, normed_ok = sem("xn_ok", 1), sem("xn_sub"), sem("normed4_ok")
        ksim_mm, ksim_ok = sem("ksim_mm", T, 1), sem("ksim_ok", T)
        h_mm, h_ok = sem("h_mm", EH, 1), sem("h_ok", EH)
        side_ok, cand_ok, best_ok = sem("side_ok", T, 1), sem("cand_ok", T), sem("best_ok", T)
        lohi_ok, sig_ok, comp_ok = sem("lohi_ok", T), sem("sig_ok", T), sem("comp_ok", T)
        comp_mm, comp_t_ok = sem("comp_mm", PAIRS, 1), sem("comp_t_ok", PAIRS)
        side_f_ok, eq_is, eq_ok = sem("side_f_ok", T), sem("eq_is", T), sem("eq_ok", T)
        hot_ok, g_mm, mix_ok = sem("hot_ok", PAIRS * QB), sem("g_mm", PAIRS * QB, 1), sem("mix_ok", PAIRS * QB, 1)
        out_mm, z4_ok, o4_ok, stored = sem("out4_mm", T, 1), sem("z4_ok", T, 1), sem("o4_ok", T), sem("stored", 16, 1)
        var_ok, rstd_ok = sem("var4_ok", 2), sem("rstd4_ok", 2)
        spare = sem("spare4").h
        own = sem("dve_own4", OWN_PEER)

        with nc.Block() as block:
            @block.sync
            def _(sp):
                with sp.Fori(0, B) as b:
                    wait(sp, o4_ok, b)
                    sp.dma_start(v.out[bass.ds(b, 1), :, :].rearrange("a (t p) d -> p (a t) d", p=P), o4[:])\
                        .then_inc(stored.h, 16)
                sp.wait_ge(stored.h, stored.start + 16 * B)

            @block.gpsimd
            def _(pool):
                for s in primed:
                    pool.sem_inc(s.h, 1)
                nc.gpsimd.memset(hot_w[:], 0.0).then_inc(zeroed.h, 1)
                pool.wait_ge(bn_var.h, 1)
                nc.gpsimd.tensor_tensor(bn_inv[:], bn_inv[:], v.minus_half[:], ALU.pow).then_inc(bn_pow.h, 1)
                with pool.Fori(0, B) as b:
                    for p in range(PAIRS):
                        for u in (2 * p, 2 * p + 1):
                            wait(pool, side_ok, b, u + 1)
                            if p:
                                wait(pool, best_ok, b, u - 1)
                            nc.gpsimd.tensor_tensor(
                                cand[:, u % 2], bc(side[:, u, 0:NH, :].unsqueeze(3), [P, NH, K, K]),
                                bc(side[:, u, NH:SETS, :].unsqueeze(2), [P, NH, K, K]), ALU.add)\
                                .then_inc(cand_ok.h, 1)
                        for u in (2 * p, 2 * p + 1):
                            wait(pool, side_f_ok, b, u + 1)
                            wait(pool, eq_is, b, u + 1)
                            nc.gpsimd.tensor_tensor(
                                eq[:, u % 2], eq[:, u % 2], bc(side_f[:, u].unsqueeze(2), [P, SETS, K, K]), ALU.mult)\
                                .then_inc(eq_ok.h, 1)
                    for i in range(2):
                        q = slice(T // 2 * i, T // 2 * (i + 1))
                        wait(pool, var_ok, b, i + 1)
                        nc.gpsimd.tensor_tensor(rstd[:, q], rstd[:, q], bc(v.minus_half[:].unsqueeze(1), [P, T // 2, 1]),
                                                ALU.pow).then_inc(rstd_ok.h, 1)

            @block.scalar
            def _(act):
                act.wait_ge(normed_ok.h, B)
                with act.Fori(0, B) as b:
                    wait_last(act, ksim_mm, b)
                    nc.scalar.copy(xn[:], normed[:, bass.ds(b * N, N)]).then_inc(xn_ok.h, 1)
                    for u in range(T):
                        wait(act, ksim_mm, b, u + 1)
                        wait_last(act, side_ok, b)
                        nc.scalar.copy(keysims[:, u].rearrange("p s k -> p (s k)"), bank[6 + u % 2][:])\
                            .then_inc(ksim_ok.h, 1)
                    wait_last(act, mix_ok, b)
                    for c in range(EH):
                        wait(act, h_mm, b, c + 1)
                        nc.scalar.activation(hid[:, :, c, :], bank[6 + c % 2][:].rearrange("p (t l) -> p t l", t=T),
                                             ACT.Gelu).then_inc(h_ok.h, 1)
                    wait_last(act, comp_mm, b)
                    for p in range(PAIRS):
                        for u in (2 * p, 2 * p + 1):
                            wait(act, side_ok, b, u + 1)
                            nc.scalar.copy(side_f[:, u], side_i[:, u]).then_inc(side_f_ok.h, 1)
                        for u in (2 * p, 2 * p + 1):
                            wait(act, best_ok, b, u + 1)
                            nc.scalar.activation(comp[:, p, 2, u % 2, :],
                                                 best[:, u].rearrange("p h k -> p (h k)"), ACT.Sigmoid)\
                                .then_inc(sig_ok.h, 1)
                        for u in (2 * p, 2 * p + 1):
                            wait(act, lohi_ok, b, u + 1)
                            nc.scalar.copy(comp[:, p, 0:2, u % 2, :], lohi[:, u]).then_inc(comp_ok.h, 1)
                        wait(act, comp_mm, b, p + 1)
                        if p:
                            wait(act, hot_ok, b, QB * p)
                        nc.scalar.copy(w_t[:], bank[1][:, 2 * P:3 * P])
                        nc.scalar.copy(lh_t[:].rearrange("p i l -> p (i l)"), bank[1][:, 0:2 * P])\
                            .then_inc(comp_t_ok.h, 1)

            @block.vector
            def _(dve):
                def step(ins, plain=False):
                    ins.then_inc(own.h, 1)
                    own.seen += 1
                    if plain:
                        wait_apart(dve, spare, own, own.at(bb, own.seen))
                    else:
                        dve.wait_ge(own.h, own.at(bb, own.seen))

                arrived(dve, "bn")
                nc.vector.bn_aggr(v.bn_mv[:], v.bn_raw[:].rearrange("p b s -> p (b s)")).then_inc(bn_done.h, 1)
                dve.wait_ge(bn_done.h, 1)
                nc.vector.tensor_scalar(bn_inv[:], v.bn_mv[:, 1:2], EPS, None, ALU.add).then_inc(bn_var.h, 1)
                dve.wait_ge(bn_pow.h, 1)
                nc.vector.tensor_tensor(v.bn_scale[:], bn_inv[:], v.bn_g[:], ALU.mult).then_inc(bn_done.h, 1)
                dve.wait_ge(bn_done.h, 2)
                dve.wait_ge(zeroed.h, 1)
                for b in range(B):
                    q = slice(N * b, N * b + N)
                    nc.vector.tensor_scalar(normed[:, q], v.x3t[:, q], v.bn_mv[:, 0:1], v.bn_scale[:], ALU.subtract,
                                            ALU.mult).then_inc(xn_sub.h, 1)
                for b in range(B):
                    q = slice(N * b, N * b + N)
                    dve.wait_ge(xn_sub.h, b + 1)
                    nc.vector.tensor_scalar(normed[:, q], normed[:, q], v.bn_b[:], None, ALU.add).then_inc(normed_ok.h, 1)
                with dve.Fori(0, B) as b:
                    bb = b
                    own.seen = var_ok.seen = 0

                    def first_choice(u):
                        wait_apart(dve, spare, ksim_ok, ksim_ok.at(b, u + 1))
                        for s in range(SETS):
                            ins = nc.vector.max(side[:, u, s, :], keysims[:, u, s, :])
                        step(ins, True)
                        for s in range(SETS):
                            ins = nc.vector.max_index(side_i[:, u, s, :], side[:, u, s, :], keysims[:, u, s, :])
                        ins.then_inc(side_ok.h, 1)

                    def second_choice(u):
                        wait_apart(dve, spare, cand_ok, cand_ok.at(b, u + 1))
                        for h in range(NH):
                            ins = nc.vector.max(best[:, u, h, :], cand[:, u % 2, h].rearrange("p r c -> p (r c)"))
                        step(ins, True)
                        for h in range(NH):
                            ins = nc.vector.max_index(best_i[:, u % 2, h, :], best[:, u, h, :],
                                                      cand[:, u % 2, h].rearrange("p r c -> p (r c)"))
                        ins.then_inc(best_ok.h, 1)
                        wait(dve, best_ok, b, u + 1)
                        flat = best_i[:, u % 2].rearrange("p h k -> p (h k)")
                        nc.vector.tensor_scalar(rc[:, u % 2, 0, :], flat, 3, None, ALU.logical_shift_right)
                        step(nc.vector.tensor_scalar(rc[:, u % 2, 1, :], flat, K - 1, None, ALU.bitwise_and))
                        nc.vector.tensor_tensor(
                            eq[:, u % 2],
                            bc(rc[:, u % 2].rearrange("p s (h k) -> p (s h) k", k=K).unsqueeze(3), [P, SETS, K, K]),
                            bc(v.iota_k[:].unsqueeze(1).unsqueeze(1), [P, SETS, K, K]), ALU.is_equal)\
                            .then_inc(eq_is.h, 1)

                    def numbers(u):
                        wait(dve, eq_ok, b, u + 1)
                        step(nc.vector.tensor_reduce(dec[:], eq[:, u % 2], X, ALU.add))
                        step(nc.vector.scalar_tensor_tensor(
                            e_num[:], dec[:, 0:NH, :].rearrange("p h k -> p (h k)"), float(NK),
                            dec[:, NH:SETS, :].rearrange("p h k -> p (h k)"), ALU.mult, ALU.add))
                        nc.vector.tensor_scalar(lohi[:, u, 0, :], e_num[:], P - 1, None, ALU.bitwise_and)
                        nc.vector.tensor_scalar(lohi[:, u, 1, :], e_num[:], 7, None, ALU.logical_shift_right)\
                            .then_inc(lohi_ok.h, 1)

                    def one_hots(p):
                        wait(dve, comp_t_ok, b, p + 1)
                        if p:
                            wait(dve, g_mm, b, QB * p)
                        else:
                            wait_last(dve, g_mm, b)
                        nc.vector.tensor_scalar(w_hi[:], w_t[:], WEIGHT_SCALE, None, ALU.mult)
                        step(nc.vector.tensor_tensor(hot_hi[:], bc(lh_t[:, 1:2, :], [P, EH, P]), v.iota_hi[:],
                                                     ALU.is_equal))
                        step(nc.vector.scalar_tensor_tensor(w_lo[:], w_t[:], WEIGHT_SCALE, w_hi[:], ALU.mult,
                                                            ALU.subtract))
                        for t in range(2):
                            q = slice(HK * t, HK * t + HK)
                            for i, w in enumerate((w_hi, w_lo)):
                                ins = nc.vector.tensor_tensor(hot_w[q, i, t], hot_hi[q],
                                                              bc(w[q].unsqueeze(1), [HK, EH, P]), ALU.mult)
                        for q in range(QB):
                            lanes = slice(LB * q, LB * q + LB)
                            nc.vector.tensor_tensor(hot_lo[:, :, lanes], bc(lh_t[:, 0:1, lanes], [P, P, LB]),
                                                    v.iota_lo[:, :, lanes], ALU.is_equal).then_inc(hot_ok.h, 1)

                    def weigh(p, banks):
                        for q in banks:
                            wait(dve, g_mm, b, QB * p + q + 1)
                            if p == 0 and q == 0:
                                wait(dve, h_ok, b)
                                wait_last(dve, out_mm, b)
                            elif q == 0:
                                wait(dve, out_mm, b, 2 * p)
                            lanes = slice(LB * q, LB * q + LB)
                            nc.vector.scalar_tensor_tensor(
                                mix[:, :, lanes].rearrange("p e l -> p l e"),
                                bank[2 + q][:].rearrange("p (l e) -> p l e", e=2 * EH), 1.0 / WEIGHT_SCALE,
                                hid[:, 2 * p:2 * p + 2, :, lanes].rearrange("p t e l -> p l (t e)"),
                                ALU.mult, ALU.mult).then_inc(mix_ok.h, 1)

                    def residual(p):
                        wait(dve, out_mm, b, 2 * p + 2)
                        for u in (2 * p, 2 * p + 1):
                            nc.vector.tensor_tensor(z4[:, u, :], bank[p][:, P * (u % 2):P * (u % 2) + P],
                                                    v.x3[:, bass.ds(b * T + u, 1), :].rearrange("p a d -> p (a d)"),
                                                    ALU.add).then_inc(z4_ok.h, 1)
                        wait(dve, z4_ok, b, 2 * p + 2)

                    for u in (0, 1):
                        first_choice(u)
                    for u in (0, 1):
                        second_choice(u)
                    first_choice(2)
                    for u in (0, 1):
                        numbers(u)
                    first_choice(3)
                    one_hots(0)
                    for u in (2, 3):
                        second_choice(u)
                    weigh(0, range(0, QB // 2))
                    for u in (2, 3):
                        numbers(u)
                    weigh(0, range(QB // 2, QB))
                    one_hots(1)
                    weigh(1, range(QB))
                    dve.wait_ge(stored.h, b * 16 + stored.start)
                    layer_norm(nc, dve, spare, b, own, stats, mv, rstd, lambda u: z4[:, u, :], lambda u: o4[:, u, :],
                               T, var_ok, rstd_ok, o4_ok, residual)
                assert own.seen == own.per, own.seen

            @block.tensor
            def _(pe):
                arrived(pe, "peer")
                with pe.Fori(0, B) as b:
                    wait(pe, xn_ok, b)
                    for u in range(T):
                        if u >= 2:
                            wait(pe, ksim_ok, b, u - 1)
                        nc.tensor.matmul(bank[6 + u % 2][:], xn[:, P * u:P * u + P],
                                         v.keysim[:].rearrange("p s k -> p (s k)"), start=True, stop=True)\
                            .then_inc(ksim_mm.h, 1)
                    for c in range(EH):
                        if c < 2:
                            wait(pe, ksim_ok, b, T - 1 + c)
                        else:
                            wait(pe, h_ok, b, c - 1)
                        nc.tensor.matmul(bank[6 + c % 2][:], v.down_t[:, c, :], v.x3t[:, bass.ds(b * N, N)],
                                         start=True, stop=True).then_inc(h_mm.h, 1)

                    def transposes(p):
                        wait(pe, comp_ok, b, 2 * p + 2)
                        for i in range(3):
                            ins = nc.tensor.transpose(bank[1][:, P * i:P * i + P],
                                                      comp[:, p, i].rearrange("p t k -> p (t k)"), ident[:])
                        ins.then_inc(comp_mm.h, 1)

                    def gathered(p):
                        for q in range(QB):
                            wait(pe, hot_ok, b, QB * p + q + 1)
                            if p:
                                wait(pe, mix_ok, b, q + 1)
                            for lane in range(LB * q, LB * q + LB):
                                for i in range(2):
                                    c = 2 * EH * (lane % LB)
                                    ins = nc.tensor.matmul(
                                        bank[2 + q][:, c:c + 2 * EH], hot_lo[:, :, lane],
                                        hot_w[:, i, :, :, lane].rearrange("p t e -> p (t e)"),
                                        start=(i == 0), stop=(i == 1))
                            ins.then_inc(g_mm.h, 1)

                    def outputs(p):
                        wait(pe, mix_ok, b, QB * p + QB)
                        for t in range(2):
                            for e in range(EH):
                                ins = nc.tensor.matmul(bank[p][:, P * t:P * t + P], mix[:, EH * t + e, :],
                                                       v.upw[:, e, :], start=(e == 0), stop=(e == EH - 1))
                            ins.then_inc(out_mm.h, 1)

                    wait_last(pe, z4_ok, b)
                    transposes(0)
                    gathered(0)
                    transposes(1)
                    outputs(0)
                    gathered(1)
                    outputs(1)


_INS = ["L0_attn_x", "L0_attn_ln_g", "L0_attn_ln_b", "L0_attn_W_h", "L0_attn_b_h", "L0_attn_W_qk", "L0_attn_b_qk",
        "L0_attn_os_gamma", "L0_attn_os_beta", "L0_attn_rel_emb", "L0_attn_W_out", "L0_attn_b_out", "L0_ffn_Wg",
        "L0_ffn_We", "L1_attn_w_qkv", "L1_attn_wq_map", "L1_attn_bq_map", "L1_attn_wk_map", "L1_attn_bk_map",
        "L1_attn_w_out", "L1_ffn_bn_gamma", "L1_ffn_bn_beta", "L1_ffn_w_q", "L1_ffn_keys_p", "L1_ffn_down",
        "L1_ffn_up"]


def kernel(**inputs):
    import numpy as _np
    import concourse.bacc as _bacc
    from concourse.bass_utils import run_bass_kernel_spmd as _run

    nc = _bacc.Bacc("TRN2", target_bir_lowering=False, num_devices=1)
    arrays, args = {}, []
    for name in _INS:
        a = _np.ascontiguousarray(inputs[name])
        arrays[f"in_{name}"] = a
        args.append(nc.dram_tensor(f"in_{name}", a.shape, mybir.dt.from_np(a.dtype), kind="ExternalInput").ap())
    shape = inputs["L0_attn_x"].shape
    args.append(nc.dram_tensor("out_0", shape, F32, kind="ExternalOutput").ap())
    build(nc, *args)
    r = _run(nc, [arrays], core_ids=[0])
    return r.results[0]["out_0"]
```
